# Optimizing a Trainium2 kernel written in Bass

```python
import numpy as np
import jax
import jax.numpy as jnp

def _softmax(x, axis=-1):
    return jax.nn.softmax(x, axis=axis)

def _gelu(x):
    return jax.nn.gelu(x, approximate=True)

def _silu(x):
    return jax.nn.silu(x)

def _sigmoid(x):
    return jax.nn.sigmoid(x)

def _layernorm(x, axis=-1, eps=1e-05):
    m = jnp.mean(x, axis=axis, keepdims=True)
    v = jnp.var(x, axis=axis, keepdims=True)
    return (x - m) / jnp.sqrt(v + eps)

def _scatter_add(tgt, idx, src, axis=0):
    return tgt.at[idx].add(src)

def _segment_sum(src, seg, n):
    return jax.ops.segment_sum(src, seg, n)
kernel_name = 'mk_gps_d1_gnn_r8_9db351'

def setup_inputs(seed: int=0):
    np.random.seed(seed)
    _w = jnp.asarray

    def _rec_inputs():
        import jax
        import jax.numpy as jnp
        _gk = jax.random.key(seed)
        x = -0.0003929 + 0.9999 * jax.random.normal(jax.random.fold_in(_gk, 1), (6250, 256), jnp.float32)
        src = jax.random.randint(jax.random.fold_in(_gk, 2), (200000,), 0, 6250, jnp.int32)
        dst = jnp.minimum((6250 * jax.random.uniform(jax.random.fold_in(_gk, 3), (200000,)) ** 2.0).astype(jnp.int32), 49999)
        _o = jnp.argsort(dst, stable=True)
        src = src[_o]
        dst = dst[_o]
        edge_weight = 0.00540447 + 1.00226 * jax.random.normal(jax.random.fold_in(_gk, 12), (200000,), jnp.float32)
        return (x, src, dst, edge_weight)
    x, src, dst, edge_weight = _rec_inputs()

    def _L0_gnn_setup():
        import jax, jax.numpy as jnp
        import numpy as np
        from itertools import combinations
        NDIM = 256
        BATCH = 8192

        def _build_mat(rots, idx_i, idx_j, ndim):

            def step(mat, t):
                i, j, theta = t
                c = jnp.cos(theta)
                s = jnp.sin(theta)
                ri = mat[i]
                rj = mat[j]
                mat = mat.at[i].set(c * ri - s * rj)
                mat = mat.at[j].set(s * ri + c * rj)
                return (mat, None)
            mat0 = jnp.eye(ndim, dtype=rots.dtype)
            mat, _ = jax.lax.scan(step, mat0, (idx_i, idx_j, rots))
            return mat.T
        key = jax.random.key(seed)
        k1, k2 = jax.random.split(key)
        pairs = np.array(list(combinations(range(NDIM), 2)), dtype=np.int32)
        return {'x': jax.random.normal(k1, (BATCH, NDIM), dtype=jnp.float32), 'rots': jax.random.normal(k2, (pairs.shape[0],), dtype=jnp.float32), 'idx_i': jnp.asarray(pairs[:, 0]), 'idx_j': jnp.asarray(pairs[:, 1])}
    _L0_gnn_all = _L0_gnn_setup()
    _L0_gnn_in = {k: v for k, v in _L0_gnn_all.items() if k in ()}
    del _L0_gnn_all

    def _L0_mix_setup():
        import jax, jax.numpy as jnp
        import numpy as np
        A, Bc, Cc = (0.5, 1.0, 1.0)
        H = 8
        EPS = 1e-12

        def _normalize(t):
            n = jnp.linalg.norm(t, axis=-1, keepdims=True)
            return t / jnp.maximum(n, EPS)
        key = jax.random.key(seed)
        ks = jax.random.split(key, 5)
        B, N, C = (8, 256, 256)
        D = C // H
        x = jax.random.normal(ks[0], (B, N, C), dtype=jnp.float32)
        Wqkv = jax.random.normal(ks[1], (3 * H * D, C), dtype=jnp.float32) * 0.02
        bqkv = jnp.zeros((3 * H * D,), dtype=jnp.float32)
        Wproj = jax.random.normal(ks[2], (C, H * D), dtype=jnp.float32) * 0.02
        bproj = jnp.zeros((C,), dtype=jnp.float32)
        temperature = jnp.ones((1, H, 1, 1), dtype=jnp.float32)
        return {'x': x, 'Wqkv': Wqkv, 'bqkv': bqkv, 'Wproj': Wproj, 'bproj': bproj, 'temperature': temperature}
    _L0_mix_all = _L0_mix_setup()
    _L0_mix_in = {k: v for k, v in _L0_mix_all.items() if k in ('Wqkv', 'bqkv', 'Wproj', 'bproj', 'temperature')}
    del _L0_mix_all

    def _L0_ffn_setup():
        import math
        import jax, jax.numpy as jnp
        import numpy as np
        CAPACITY_FACTOR = 1.25
        key = jax.random.key(seed)
        ks = jax.random.split(key, 5)
        B, L, D, F, E = (8, 1024, 256, 1024, 8)
        h = jax.random.normal(ks[0], (B, L, D), dtype=jnp.float32)
        gate_w = jax.random.normal(ks[1], (D, E), dtype=jnp.float32) * 0.02
        gate_b = jnp.zeros((E,), dtype=jnp.float32)
        w1 = jax.random.normal(ks[2], (E, D, F), dtype=jnp.float32) * (1.0 / math.sqrt(D))
        b1 = jnp.zeros((E, F), dtype=jnp.float32)
        w2 = jax.random.normal(ks[3], (E, F, D), dtype=jnp.float32) * (1.0 / math.sqrt(F))
        b2 = jnp.zeros((E, D), dtype=jnp.float32)
        return {'h': h, 'gate_w': gate_w, 'gate_b': gate_b, 'w1': w1, 'b1': b1, 'w2': w2, 'b2': b2}
    _L0_ffn_all = _L0_ffn_setup()
    _L0_ffn_in = {k: v for k, v in _L0_ffn_all.items() if k in ('gate_w', 'gate_b', 'w1', 'b1', 'w2', 'b2')}
    del _L0_ffn_all
    return {'x': x, 'src': src, 'dst': dst, 'edge_weight': edge_weight, 'L0_mix_Wqkv': _L0_mix_in['Wqkv'], 'L0_mix_bqkv': _L0_mix_in['bqkv'], 'L0_mix_Wproj': _L0_mix_in['Wproj'], 'L0_mix_bproj': _L0_mix_in['bproj'], 'L0_mix_temperature': _L0_mix_in['temperature'], 'L0_ffn_gate_w': _L0_ffn_in['gate_w'], 'L0_ffn_gate_b': _L0_ffn_in['gate_b'], 'L0_ffn_w1': _L0_ffn_in['w1'], 'L0_ffn_b1': _L0_ffn_in['b1'], 'L0_ffn_w2': _L0_ffn_in['w2'], 'L0_ffn_b2': _L0_ffn_in['b2']}

def reference(x, src, dst, edge_weight, L0_mix_Wqkv, L0_mix_bqkv, L0_mix_Wproj, L0_mix_bproj, L0_mix_temperature, L0_ffn_gate_w, L0_ffn_gate_b, L0_ffn_w1, L0_ffn_b1, L0_ffn_w2, L0_ffn_b2):
    import jax
    import jax.numpy as jnp

    def _L0_gnn_ref(x, rots, idx_i, idx_j):
        import jax, jax.numpy as jnp
        import numpy as np
        from itertools import combinations
        NDIM = 256
        BATCH = 8192

        def _build_mat(rots, idx_i, idx_j, ndim):

            def step(mat, t):
                i, j, theta = t
                c = jnp.cos(theta)
                s = jnp.sin(theta)
                ri = mat[i]
                rj = mat[j]
                mat = mat.at[i].set(c * ri - s * rj)
                mat = mat.at[j].set(s * ri + c * rj)
                return (mat, None)
            mat0 = jnp.eye(ndim, dtype=rots.dtype)
            mat, _ = jax.lax.scan(step, mat0, (idx_i, idx_j, rots))
            return mat.T
        m = _build_mat(rots, idx_i, idx_j, x.shape[-1])
        return x @ m

    def _L0_mix_ref(x, Wqkv, bqkv, Wproj, bproj, temperature):
        import jax, jax.numpy as jnp
        import numpy as np
        A, Bc, Cc = (0.5, 1.0, 1.0)
        H = 8
        EPS = 1e-12

        def _normalize(t):
            n = jnp.linalg.norm(t, axis=-1, keepdims=True)
            return t / jnp.maximum(n, EPS)
        B, N, C = x.shape
        D = C // H
        scale = float(D) ** 0.25
        qkv = (x @ Wqkv.T + bqkv).reshape(B, N, 3, H, D)
        qkv = jnp.transpose(qkv, (2, 0, 3, 1, 4))
        q, k, v = (qkv[0], qkv[1], qkv[2])
        q = q * scale
        v1 = jnp.concatenate([jnp.ones((B, H, N, 1), dtype=v.dtype), v], axis=-1)
        qn = _normalize(q) * (scale * temperature)
        kn = _normalize(k) * scale
        vN = v1 / N
        kv_mod = jnp.einsum('bhni,bhnj,bhne->bhije', kn, kn, vN)
        kv = jnp.einsum('bhnd,bhne->bhde', kn, vN)
        vsum = jnp.sum(vN, axis=-2)[:, :, None, :]
        y = A * jnp.einsum('bhni,bhnj,bhije->bhne', qn, qn, kv_mod) + scale ** 2 * Bc * jnp.einsum('bhnd,bhde->bhne', qn, kv) + scale ** 4 * Cc * vsum
        y_norm, y = (y[..., :1], y[..., 1:])
        y = y / y_norm
        out = jnp.transpose(y, (0, 2, 1, 3)).reshape(B, N, H * D)
        return out @ Wproj.T + bproj

    def _L0_ffn_ref(h, gate_w, gate_b, w1, b1, w2, b2):
        import math
        import jax, jax.numpy as jnp
        import numpy as np
        CAPACITY_FACTOR = 1.25
        B, L, D = h.shape
        E = gate_w.shape[1]
        T = B * L
        C = max(1, math.ceil(CAPACITY_FACTOR * T / E))
        x = h.reshape(T, D)
        logits = x @ gate_w + gate_b
        probs = jax.nn.softmax(logits, axis=-1)
        idx = jnp.argmax(probs, axis=-1)
        prb = jnp.take_along_axis(probs, idx[:, None], axis=1)[:, 0]
        one_hot = jax.nn.one_hot(idx, E, dtype=jnp.float32)
        pos = (jnp.cumsum(one_hot, axis=0) * one_hot).sum(-1).astype(jnp.int32) - 1
        kept = pos < C
        pos_safe = jnp.where(kept, pos, C)
        buf = jnp.zeros((E, C, D), dtype=h.dtype).at[idx, pos_safe].set(x, mode='drop')
        hmid = jax.nn.relu(jnp.einsum('ecd,edf->ecf', buf, w1) + b1[:, None, :])
        ybuf = jnp.einsum('ecf,efd->ecd', hmid, w2) + b2[:, None, :]
        pos_g = jnp.minimum(pos, C - 1)
        y_tok = ybuf[idx, pos_g] * (prb * kept)[:, None]
        y = y_tok.reshape(B, L, D)
        y = jnp.nan_to_num(y, nan=0.0, posinf=10000.0, neginf=-10000.0)
        return y
    xn = _layernorm(x, axis=-1)
    x = x + _L0_gnn_ref(xn, edge_weight, src, dst) + _L0_mix_ref(xn[None], L0_mix_Wqkv, L0_mix_bqkv, L0_mix_Wproj, L0_mix_bproj, L0_mix_temperature)[0]
    x = x + _L0_ffn_ref(_layernorm(x, axis=-1)[None], L0_ffn_gate_w, L0_ffn_gate_b, L0_ffn_w1, L0_ffn_b1, L0_ffn_w2, L0_ffn_b2)[0]
    return x

_drawn_inputs = setup_inputs


def setup_inputs(seed=0):
    import zlib

    import numpy as np

    out = dict(_drawn_inputs(seed))
    spreads = {'L0_mix_bqkv': (0.0, 0.1),
     'L0_mix_bproj': (0.0, 0.1),
     'L0_mix_temperature': (1.0, 0.6),
     'L0_ffn_gate_b': (0.0, 0.1),
     'L0_ffn_b1': (0.0, 0.605),
     'L0_ffn_b2': (0.0, 0.427)}
    factors = {'edge_weight': 8.0, 'L0_mix_Wqkv': 8.0}
    for name, (base, spread) in spreads.items():
        noise = np.random.default_rng([zlib.crc32(name.encode()), seed]).standard_normal(out[name].shape)
        drawn = base * np.exp(spread * noise) if base else spread * noise
        out[name] = jnp.asarray(drawn.astype(out[name].dtype))
    for name, factor in factors.items():
        out[name] = (out[name] * factor).astype(out[name].dtype)
    return out
```

```python
import math
from contextlib import ExitStack, contextmanager
import concourse.bass as bass
from concourse import mybir

F32 = mybir.dt.float32
I32 = mybir.dt.int32
ALU = mybir.AluOpType
ACT = mybir.ActivationFunctionType
AX = mybir.AxisListType

P = 128
D = 256
SEG = 125
NPAR = 8
Z, QO, QL, FS, FO, CO, SO, D1 = range(NPAR)
LEVELS = 7

TWO_PI_A = 6.28125
TWO_PI_B = float(2 * math.pi - 6.28125) and 0.0019350051879882812
TWO_PI_C = 2 * math.pi - TWO_PI_A - TWO_PI_B
ROUND = 12582912.0
PI_IN = 3.1415925


@contextmanager
def a_semaphore(nc, name):
    held = nc.alloc_semaphore(name)
    yield held
    nc.clear_and_free_semaphores([held])


def build_gnn(nc, ctx, src, dst, ew, mT_out):
    S = src.shape[0]
    L = S // SEG
    W = 2 * L
    BITS = max(1, (W - 1).bit_length())
    B = P - 1
    NCH = -(-SEG * W // (P * B))
    NB = NCH * P
    NPK = -(-(NB * B + P) // P) * P
    assert BITS <= 12 and SEG * L == S

    def sem(n):
        return ctx.enter_context(a_semaphore(nc, n))

    sc = nc.dram_tensor("segments", (2, SEG, W), I32, kind="Internal").ap()
    pk = nc.dram_tensor("packed", (2, NPK), I32, kind="Internal").ap()

    keep_ctx = ExitStack()
    nrun = keep_ctx.enter_context(nc.sbuf_tensor("nrun", [1, 1], I32))
    ident = keep_ctx.enter_context(nc.sbuf_tensor("ident", [P, P], F32))
    tot = keep_ctx.enter_context(nc.sbuf_tensor("tot", [P, 1], F32))
    ones = keep_ctx.enter_context(nc.sbuf_tensor("ones", [P, P], F32))

    with ExitStack() as c:
        def sb(n, s, t=F32):
            return c.enter_context(nc.sbuf_tensor(n, s, t))
        src_i = sb("src_i", [SEG, L], I32)
        dst_i = sb("dst_i", [SEG, L], I32)
        th = sb("th", [SEG, L])
        fi = sb("fi", [SEG, L]); fj = sb("fj", [SEG, L])
        va = sb("va", [SEG, L]); vb = sb("vb", [SEG, L]); pr = sb("pr", [SEG, L]); tmp = sb("tmp", [SEG, L])
        vw = sb("vw", [SEG, W]); kf = sb("kf", [SEG, W]); inc = sb("inc", [SEG, W]); slot = sb("slot", [SEG, W])
        ki = sb("ki", [SEG, W], I32); thw = sb("thw", [SEG, W], I32); bit = sb("bit", [SEG, W], I32)
        cleared = sb("cleared", [SEG, W], I32); zi = sb("zi", [P, max(W, NPK // P)], I32)
        tri = sb("tri", [SEG, SEG + 1])
        base_i = sb("base_i", [1, SEG + 1], I32)
        base_ps = c.enter_context(nc.psum_tensor("base_ps", [P, 512], F32))
        ld = sem("step_loads"); dv = sem("prep_dve"); tr = sem("tri_ready"); bs = sem("base_ps_ready")
        bi = sem("base_ready"); cz = sem("zeros_ready"); comp = sem("compressed"); so = sem("seg_stored"); pkd = sem("packed_done")
        po = sem("pool_consts"); ths = sem("theta_copied"); counted = sem("counted"); seg_in_order = sem("seg_in_order")
        with nc.Block() as block:
            @block.sync
            def _(sp):
                sp.dma_start(src_i[:, :], src.rearrange("(p l) -> p l", l=L)).then_inc(ld, 16)
                sp.dma_start(dst_i[:, :], dst.rearrange("(p l) -> p l", l=L)).then_inc(ld, 16)
                sp.dma_start(th[:, :], ew.rearrange("(p l) -> p l", l=L)).then_inc(ld, 16)
                sp.wait_ge(cz, 1)
                for a in range(2):
                    sp.dma_start(pk[a].rearrange("(p l) -> p l", p=P), zi[:, 0:NPK // P]).then_inc(pkd, 16)
                sp.wait_ge(pkd, 32)
                sp.wait_ge(comp, 1)
                sp.dma_start(sc[0], ki[:, :]).then_inc(so, 16)
                sp.dma_start(sc[1], thw[:, :]).then_inc(so, 16)
                sp.wait_ge(so, 32)
                sp.wait_ge(bi, 1)
                with sp.Fori(0, SEG) as p:
                    at = sp.value_load(base_i[0:1, bass.ds(p, 1)], min_val=0, max_val=(SEG - 1) * W)
                    sp.dma_start(pk[:, bass.ds(at + 1, W)], sc[:, bass.ds(p, 1), :].rearrange("a o w -> a (o w)")).then_inc(pkd, 16)
                    sp.wait_ge(pkd, p * 16 + 48)
                    sp.sem_inc(seg_in_order, 1)

            @block.gpsimd
            def _(g):
                g.memset(zi[:, :], 0).then_inc(cz, 1)
                g.memset(ones[:, :], 1.0).then_inc(po, 1)
                g.memset(ident[:, :], 0.0).then_inc(po, 1)
                g.memset(tri[:, :], 1.0).then_inc(po, 1)
                g.iota(slot[:, :], pattern=[[1, W]], base=1, channel_multiplier=0, allow_small_or_imprecise_dtypes=True).then_inc(po, 1)
                g.wait_ge(po, 4)
                g.affine_select(out=ident[:, :], in_=ident[:, :], compare_op=ALU.not_equal, fill=1.0,
                                base=0, pattern=[[-1, P]], channel_multiplier=1).then_inc(po, 1)
                g.affine_select(out=tri[:, :], in_=tri[:, :], compare_op=ALU.is_gt, fill=0.0,
                                base=0, pattern=[[1, SEG + 1]], channel_multiplier=-1).then_inc(tr, 1)

            @block.scalar
            def _(a):
                a.wait_ge(ld, 48)
                v = thw[:, :].bitcast(F32).rearrange("p (l o) -> p l o", o=2)
                a.activation(v[:, :, 0], th[:, :], ACT.Copy).then_inc(ths, 1)
                a.activation(v[:, :, 1], th[:, :], ACT.Copy).then_inc(ths, 1)

            @block.vector
            def _(v):
                n = [0]

                def link(ins):
                    n[0] += 1
                    ins.then_inc(dv, 1)
                    v.wait_ge(dv, n[0])
                v.wait_ge(ld, 48)
                vw2 = vw[:, :].rearrange("p (l o) -> p l o", o=2)
                kf2 = kf[:, :].rearrange("p (l o) -> p l o", o=2)
                v.tensor_copy(fi[:, :], src_i[:, :])
                link(v.tensor_copy(fj[:, :], dst_i[:, :]))
                v.tensor_scalar(va[:, :], fi[:, :], float(D), None, ALU.is_lt)
                link(v.tensor_scalar(vb[:, :], fj[:, :], float(D), None, ALU.is_lt))
                v.tensor_scalar(fi[:, :], fi[:, :], float(D - 1), None, ALU.min)
                link(v.tensor_scalar(fj[:, :], fj[:, :], float(D - 1), None, ALU.min))
                link(v.tensor_tensor(tmp[:, :], fi[:, :], fj[:, :], ALU.is_equal))
                link(v.tensor_tensor(tmp[:, :], tmp[:, :], vb[:, :], ALU.mult))
                link(v.tensor_scalar(tmp[:, :], tmp[:, :], -1.0, 1.0, ALU.mult, ALU.add))
                link(v.tensor_tensor(va[:, :], va[:, :], tmp[:, :], ALU.mult))
                v.tensor_copy(vw2[:, :, 0], va[:, :])
                v.tensor_copy(vw2[:, :, 1], vb[:, :])
                link(v.tensor_tensor(pr[:, :], va[:, :], vb[:, :], ALU.mult))
                v.scalar_tensor_tensor(kf2[:, :, 0], fj[:, :], float(D), fi[:, :], ALU.mult, ALU.add)
                v.tensor_scalar(pr[:, :], pr[:, :], 65536.0, 131072.0, ALU.mult, ALU.add)
                link(v.scalar_tensor_tensor(tmp[:, :], fi[:, :], float(D), fj[:, :], ALU.mult, ALU.add))
                link(v.tensor_tensor(kf2[:, :, 1], tmp[:, :], pr[:, :], ALU.add))
                v.wait_ge(cz, 1)
                link(v.tensor_tensor_scan(inc[:, :], vw[:, :], zi[0:SEG, 0:W].bitcast(F32), 0.0, ALU.add, ALU.add))
                v.engine_nop().then_inc(counted, 1)
                v.wait_ge(po, 4)
                link(v.tensor_tensor(slot[:, :], slot[:, :], inc[:, :], ALU.subtract))
                link(v.tensor_tensor(slot[:, :], slot[:, :], vw[:, :], ALU.mult))
                v.tensor_copy(ki[:, :], kf[:, :])
                link(v.tensor_copy(bit[:, :], slot[:, :]))
                link(v.tensor_scalar(bit[:, :], bit[:, :], 18, None, ALU.logical_shift_left))
                link(v.tensor_tensor(ki[:, :], ki[:, :], bit[:, :], ALU.bitwise_or))
                v.wait_ge(ths, 2)
                for b in range(BITS):
                    s = 1 << b
                    v.tensor_scalar(bit[:, :], ki[:, :], 1 << (18 + b), None, ALU.bitwise_and)
                    link(v.tensor_scalar(cleared[:, :], ki[:, :], ~(1 << (18 + b)), None, ALU.bitwise_and))
                    link(v.copy_predicated(ki[:, :], bit[:, :], zi[0:SEG, 0:W]))
                    v.copy_predicated(ki[:, 0:W - s], bit[:, s:W], cleared[:, s:W])
                    link(v.copy_predicated(thw[:, 0:W - s], bit[:, s:W], thw[:, s:W]))
                v.engine_nop().then_inc(comp, 1)
                v.wait_ge(bs, 1)
                v.tensor_copy(base_i[:, :], base_ps[0:1, 0:SEG + 1])
                link(v.tensor_copy(tot[:, :], base_ps[:, 256:257]))
                v.engine_nop().then_inc(bi, 1)
                link(v.tensor_scalar(nrun[:, :], base_ps[0:1, SEG:SEG + 1], 1.0 / (2 * B), 1.0, ALU.mult, ALU.add))

            @block.tensor
            def _(pe):
                pe.wait_ge(counted, 1)
                pe.wait_ge(tr, 1)
                pe.wait_ge(po, 1)
                pe.matmul(base_ps[0:1, 0:SEG + 1], inc[:, W - 1:W], tri[:, :], start=True, stop=True)
                pe.matmul(base_ps[:, 256:257], ones[0:SEG, :], inc[:, W - 1:W], start=True, stop=True).then_inc(bs, 1)

    par = keep_ctx.enter_context(nc.sbuf_tensor("par", [P, NB + 2, NPAR], F32))
    with ExitStack() as c0:
      kt = c0.enter_context(nc.sbuf_tensor("kt", [P, NB], I32))
      tt = c0.enter_context(nc.sbuf_tensor("tt", [P, NB], F32))
      with ExitStack() as c:
          def sb(n, s, t=F32):
              return c.enter_context(nc.sbuf_tensor(n, s, t))
          E = P + 1
          kb = sb("kb", [P, NCH, E], I32)
          tb = sb("tb", [P, NCH, E])
          kbf = sb("kbf", [P, NCH, E]); posn = sb("posn", [P, NCH, E]); inr = sb("inr", [P, NCH, E]); pfl = sb("pfl", [P, NCH, 2])
          psk = [c.enter_context(nc.psum_tensor(f"psk{i}", [P, 512], F32)) for i in range(2)]
          pst = [c.enter_context(nc.psum_tensor(f"pst{i}", [P, 512], F32)) for i in range(2)]
          ld = sem("packed_loads"); kr = sem("keys_float"); tp = sem("transposed"); ev = sem("columns_kept")
          dv = sem("cols_dve"); io = sem("cols_iota")

          def overlapped(a):
              return bass.AP(tensor=pk.tensor, offset=a * NPK, ap=[[B, P], [P * B, NCH], [1, E]])

          with nc.Block() as block:
              @block.sync
              def _(sp):
                  sp.dma_start(kb[:, :, :], overlapped(0)).then_inc(ld, 16)
                  sp.dma_start(tb[:, :, :].bitcast(I32), overlapped(1)).then_inc(ld, 16)

              @block.gpsimd
              def _(g):
                  g.iota(posn[:, :, :], pattern=[[P * B, NCH], [1, E]], base=-1, channel_multiplier=B, allow_small_or_imprecise_dtypes=True).then_inc(io, 1)

              @block.tensor
              def _(pe):
                  pe.wait_ge(kr, 1)
                  pe.wait_ge(ld, 32)
                  for q in range(0, NCH, 4):
                      m = min(4, NCH - q)
                      b = (q // 4) % 2
                      if q >= 8:
                          pe.wait_ge(ev, 2 * (q // 4) - 2)
                      for j in range(m):
                          pe.matmul(psk[b][:, j * P:(j + 1) * P], kbf[:, q + j, 0:P], ident[:, :], start=True, stop=True)
                          last = pe.matmul(pst[b][:, j * P:(j + 1) * P], tb[:, q + j, 0:P], ident[:, :], start=True, stop=True)
                      last.then_inc(tp, 1)

              @block.vector
              def _(v):
                  n = [0]

                  def link(ins):
                      n[0] += 1
                      ins.then_inc(dv, 1)
                      v.wait_ge(dv, n[0])
                  v.wait_ge(ld, 32)
                  link(v.tensor_scalar(kb[:, :, :], kb[:, :, :], (1 << 18) - 1, None, ALU.bitwise_and))
                  link(v.tensor_copy(kbf[:, :, :], kb[:, :, :]))
                  v.wait_ge(io, 1)
                  link(v.tensor_scalar(inr[:, :, :], posn[:, :, :], tot[:, 0:1], None, ALU.is_lt))
                  link(v.tensor_tensor(kbf[:, :, :], kbf[:, :, :], inr[:, :, :], ALU.mult))
                  link(v.tensor_copy(kb[:, :, :], kbf[:, :, :]))
                  link(v.tensor_scalar(kb[:, :, :], kb[:, :, :], 1 << 16, None, ALU.bitwise_and))
                  link(v.tensor_copy(pfl[:, :, 0], kb[:, :, 1]))
                  link(v.tensor_copy(pfl[:, :, 1], kb[:, :, P]))
                  link(v.tensor_scalar(inr[:, :, :], inr[:, :, :], -262144.0, 262144.0, ALU.mult, ALU.add))
                  link(v.tensor_scalar(inr[:, :, 0], pfl[:, :, 0], -4.0, 262144.0, ALU.mult, ALU.add))
                  link(v.scalar_tensor_tensor(inr[:, :, B], pfl[:, :, 1], 4.0, inr[:, :, B], ALU.mult, ALU.add))
                  v.tensor_tensor(kbf[:, :, :], kbf[:, :, :], inr[:, :, :], ALU.add).then_inc(kr, 1)
                  for q in range(0, NCH, 4):
                      m = min(4, NCH - q)
                      b = (q // 4) % 2
                      v.wait_ge(tp, q // 4 + 1)
                      v.tensor_copy(kt[:, q * P:(q + m) * P], psk[b][:, 0:m * P]).then_inc(ev, 1)
                      v.tensor_copy(tt[:, q * P:(q + m) * P], pst[b][:, 0:m * P]).then_inc(ev, 1)
                  v.wait_ge(ev, 2 * -(-NCH // 4))
      with ExitStack() as c:
          def sb(n, s, t=F32):
              return c.enter_context(nc.sbuf_tensor(n, s, t))
          w1 = sb("w1", [P, NB]); w2 = sb("w2", [P, NB]); vl = sb("vl", [P, NB]); sgn = sb("sgn", [P, NB])
          wi = sb("wi", [P, NB], I32)
          n1 = sb("n1", [P, 1]); halfpi = sb("halfpi", [P, 1])
          dv = sem("par_dve"); io = sem("par_consts"); ang = sem("angles"); tri_s = sem("sincos")
          with nc.Block() as block:
              @block.gpsimd
              def _(g):
                  g.iota(n1[:, :], pattern=[[0, 1]], base=1, channel_multiplier=1, allow_small_or_imprecise_dtypes=True).then_inc(io, 1)
                  g.memset(halfpi[:, :], math.pi / 2).then_inc(io, 1)
                  g.memset(par[:, NB:NB + 2, :], 0.0).then_inc(io, 1)
                  g.wait_ge(io, 3)
                  g.memset(par[:, NB:NB + 2, Z:Z + 1], -1.0).then_inc(io, 1)
                  g.wait_ge(io, 4)

              @block.scalar
              def _(a):
                  a.wait_ge(io, 2)
                  a.wait_ge(ang, 1)
                  a.activation(w2[:, :], tt[:, :], ACT.Sin).then_inc(tri_s, 1)
                  a.wait_ge(ang, 2)
                  a.wait_ge(tri_s, 1)
                  a.activation(tt[:, :], sgn[:, :], ACT.Sin, bias=halfpi[:, :], scale=-1.0).then_inc(tri_s, 1)

              @block.vector
              def _(v):
                  n = [0]

                  def link(ins):
                      n[0] += 1
                      ins.then_inc(dv, 1)
                      v.wait_ge(dv, n[0])
                  v.wait_ge(io, 2)
                  PA = par[:, 0:NB, :]
                  link(v.tensor_scalar(wi[:, :], kt[:, :], 18, None, ALU.logical_shift_right))
                  link(v.tensor_copy(vl[:, :], wi[:, :]))
                  link(v.tensor_scalar(vl[:, :], vl[:, :], -1.0, 1.0, ALU.mult, ALU.add))
                  link(v.tensor_scalar(w1[:, :], tt[:, :], 1.0 / (2 * math.pi), ROUND, ALU.mult, ALU.add))
                  link(v.tensor_scalar(w1[:, :], w1[:, :], ROUND, None, ALU.subtract))
                  for part in (TWO_PI_A, TWO_PI_B, TWO_PI_C):
                      link(v.scalar_tensor_tensor(tt[:, :], w1[:, :], -part, tt[:, :], ALU.mult, ALU.add))
                  link(v.tensor_scalar(tt[:, :], tt[:, :], PI_IN, -PI_IN, ALU.min, ALU.max))
                  v.engine_nop().then_inc(ang, 1)
                  v.wait_ge(ang, 1)
                  link(v.tensor_scalar(sgn[:, :], tt[:, :], -1.0, None, ALU.mult))
                  link(v.tensor_tensor(sgn[:, :], sgn[:, :], tt[:, :], ALU.max))
                  v.engine_nop().then_inc(ang, 1)
                  v.wait_ge(tri_s, 2)
                  v.tensor_tensor(PA[:, :, CO], tt[:, :], vl[:, :], ALU.mult)
                  link(v.tensor_tensor(w2[:, :], w2[:, :], vl[:, :], ALU.mult))
                  link(v.tensor_scalar(wi[:, :], kt[:, :], 17, 1, ALU.logical_shift_right, ALU.bitwise_and))
                  link(v.tensor_copy(sgn[:, :], wi[:, :]))
                  link(v.tensor_scalar(sgn[:, :], sgn[:, :], 2.0, -1.0, ALU.mult, ALU.add))
                  v.tensor_tensor(PA[:, :, SO], w2[:, :], sgn[:, :], ALU.mult)
                  link(v.tensor_scalar(wi[:, :], kt[:, :], D - 1, None, ALU.bitwise_and))
                  link(v.tensor_copy(w1[:, :], wi[:, :]))
                  v.tensor_scalar(PA[:, :, FS], w1[:, :], float(D), None, ALU.mult)
                  v.tensor_scalar(PA[:, :, QL], w1[:, :], float(D), float(D - 1), ALU.mult, ALU.add)
                  v.scalar_tensor_tensor(PA[:, :, D1], w1[:, :], 1.0, vl[:, :], ALU.add, ALU.mult)
                  link(v.tensor_scalar(tt[:, :], w1[:, :], float(D), n1[:, 0:1], ALU.mult, ALU.add))
                  link(v.scalar_tensor_tensor(tt[:, :], tt[:, :], 1.0, vl[:, :], ALU.add, ALU.mult))
                  v.tensor_scalar(PA[:, :, Z], tt[:, :], -1.0, None, ALU.add)
                  link(v.tensor_scalar(wi[:, :], kt[:, :], 8, D - 1, ALU.logical_shift_right, ALU.bitwise_and))
                  link(v.tensor_copy(w1[:, :], wi[:, :]))
                  v.tensor_scalar(PA[:, :, FO], w1[:, :], float(D), None, ALU.mult)
                  link(v.tensor_scalar(w2[:, :], w1[:, :], float(D), n1[:, 0:1], ALU.mult, ALU.add))
                  link(v.tensor_scalar(wi[:, :], kt[:, :], 16, 1, ALU.logical_shift_right, ALU.bitwise_and))
                  link(v.tensor_copy(w1[:, :], wi[:, :]))
                  link(v.tensor_tensor(PA[:, :, QO], w2[:, :], w1[:, :], ALU.subtract))


    with ExitStack() as c:
        def sb(n, s, t=F32):
            return c.enter_context(nc.sbuf_tensor(n, s, t))

        def ps(n):
            return c.enter_context(nc.psum_tensor(n, [P, 512], F32))
        X2 = range(2)
        parn = sb("parn", [P, 2, NPAR])
        nxt = sb("nxt", [P, 2, 5]); cur = sb("cur", [P, 2, 5])
        zd = sb("zd", [P, 2, P]); zx = sb("zx", [P, 2, P])
        q3 = sb("q3", [P, 3, P]); pred = sb("pred", [P, 3])
        e1 = sb("e1", [P, P]); e2 = sb("e2", [P, P])
        rowk = sb("rowk", [P, D]); row1 = sb("row1", [P, D])
        NN = [sb(f"N{x}", [P, P]) for x in X2]
        NT = [sb(f"NT{x}", [P, P]) for x in X2]
        PQ = [[sb(f"PQ{x}{h}", [P, 2, P]) for h in range(2)] for x in X2]
        ST = [sb(f"ST{x}", [P, P]) for x in X2]
        RR = [sb(f"R{x}", [P, D]) for x in X2]
        r1 = sb("r1", [P, D]); r2 = sb("r2", [P, D])
        FT = [sb(f"FT{x}", [P, D]) for x in X2]
        WT = sb("WT", [P, 2, 2, P])
        M = sb("M", [P, 2, D]); V = sb("V", [P, D]); kp = sb("kp", [P, 2, 2])
        pq = [ps(f"pq{x}") for x in X2]
        pst = [ps(f"pss{x}") for x in X2]
        pz = ps("pz"); pv = ps("pv"); pd = ps("pd"); pw = ps("pw")
        s_nt = sem("nt_in_psum"); s_sp = sem("st_in_psum"); s_lv = sem("level_in_psum"); s_zr = sem("zrow_in_psum"); s_v = sem("v_in_psum")
        s_dl = sem("delta_in_psum"); s_cnt = sem("writers_in_psum"); s_wt = sem("wt_in_psum")
        s_q = sem("q_kept"); s_st = sem("st_kept"); s_zx = sem("zrow_kept"); s_wts = sem("wt_kept")
        s_p = sem("p_kept"); s_vs = sem("v_kept"); s_m = sem("m_updated"); s_keep = sem("keep_ready")
        s_setup = sem("n_ready"); s_dc = sem("loop_dve"); s_par = sem("par_loaded"); s_cur = sem("cur_ready")
        s_zd = sem("zdiag_ready"); s_R = sem("r_ready"); s_FT = sem("ft_ready"); s_gc = sem("loop_pool")
        s_c = sem("loop_consts"); s_go = sem("pool_goes_on"); s_fin = sem("mt_in_psum"); s_mo = sem("mt_kept"); s_out = sem("mt_stored")
        mt = sb("mt", [P, 2, D])
        with nc.Block() as block:
            @block.gpsimd
            def _(g):
                g.iota(rowk[:, :], pattern=[[D, D]], base=0, channel_multiplier=0, allow_small_or_imprecise_dtypes=True).then_inc(s_c, 1)
                g.iota(row1[:, :], pattern=[[1, D]], base=1, channel_multiplier=0, allow_small_or_imprecise_dtypes=True).then_inc(s_c, 1)
                g.memset(M[:, :, :], 0.0).then_inc(s_c, 1)
                g.wait_ge(s_c, 3)
                for k in range(2):
                    g.tensor_copy(M[:, k, k * P:(k + 1) * P], ident[:, :]).then_inc(s_c, 1)
                g.wait_ge(s_c, 5)
                g.memset(kp[:, :, :], 1.0).then_inc(s_keep, 1)
                g.memset(WT[:, :, :, :], 0.0).then_inc(s_wts, 1)
                for x in X2:
                    g.memset(FT[x][:, :], 0.0).then_inc(s_FT, 1)
                g.engine_nop().then_inc(s_m, 1)
                g.tensor_copy(parn[:, :, :], par[:, 0:2, :]).then_inc(s_par, 1)
                g.wait_ge(s_par, 1)
                for x in X2:
                    g.tensor_scalar(zd[:, x, :], ident[:, :], parn[:, x, Z:Z + 1], None, ALU.mult).then_inc(s_zd, 1)
                cnt = g.value_load(nrun[0:1, 0:1], min_val=1, max_val=NB // 2)
                with g.Fori(0, cnt) as i:
                    g.wait_ge(s_setup, i * 2 + 2); g.sem_inc(s_go, 1)
                    g.tensor_copy(cur[:, :, :], nxt[:, :, :]).then_inc(s_cur, 1)
                    g.tensor_copy(parn[:, :, :], par[:, bass.ds(i * 2 + 2, 2), :]).then_inc(s_par, 1)
                    g.wait_ge(s_cur, i + 1)
                    g.wait_ge(s_par, i + 2)
                    g.wait_ge(s_zr, i + 1); g.sem_inc(s_go, 1)
                    for x in X2:
                        g.tensor_scalar(zd[:, x, :], ident[:, :], parn[:, x, Z:Z + 1], None, ALU.mult).then_inc(s_zd, 1)
                    g.wait_ge(s_wts, i + 1); g.sem_inc(s_go, 1)
                    for x in X2:
                        g.tensor_scalar(r1[:, :], rowk[:, :], cur[:, x, 0:1], cur[:, x, 2:3], ALU.is_equal, ALU.mult).then_inc(s_gc, 1)
                        g.tensor_scalar(r2[:, :], rowk[:, :], cur[:, x, 1:2], cur[:, x, 3:4], ALU.is_equal, ALU.mult).then_inc(s_gc, 1)
                        g.wait_ge(s_gc, i * 4 + 2 * x + 2); g.sem_inc(s_go, 1)
                        g.tensor_tensor(RR[x][:, :], r1[:, :], r2[:, :], ALU.add).then_inc(s_R, 1)
                        g.wait_ge(s_R, i * 2 + x + 1); g.sem_inc(s_go, 1)
                    g.wait_ge(s_dl, i * 2 + 2); g.sem_inc(s_go, 1)
                    for x in X2:
                        g.tensor_scalar(FT[x][:, :], row1[:, :], cur[:, x, 4:5], None, ALU.is_equal).then_inc(s_FT, 1)
                    g.wait_ge(s_FT, i * 2 + 4); g.sem_inc(s_go, 1)

            def chain_v(pe, x, i):
                i2 = i * 2
                pe.wait_ge(s_m, i2 + (x + 1))
                pe.wait_ge(s_keep, i + 1) if x == 0 else None
                pe.wait_ge(s_wts, i + 1)
                pe.matmul(pv[:, 0:D], WT[:, x, 0, :], M[:, 0, :], start=True, stop=False)
                pe.matmul(pv[:, 0:D], WT[:, x, 1, :], M[:, 1, :], start=False, stop=True).then_inc(s_v, 1)

            def chain_d(pe, x, i):
                i2 = i * 2
                pe.wait_ge(s_vs, i2 + (x + 1))
                pe.wait_ge(s_FT, i2 + (x + 1))
                pe.matmul(pd[:, 0:D], FT[x][:, 0:P], V[:, :], start=True, stop=True)
                pe.matmul(pd[:, D:2 * D], FT[x][:, P:D], V[:, :], start=True, stop=True).then_inc(s_dl, 1)

            @block.tensor
            def _(pe):
                def zrow(i):
                    pe.wait_ge(s_zd, i * 2 + 2)
                    pe.matmul(pz[:, 0:D], ones[:, :], zd[:, :, :].rearrange("p a b -> p (a b)"), start=True, stop=True).then_inc(s_zr, 1)
                pe.wait_ge(s_c, 5)
                zrow(0)
                cnt = pe.value_load(nrun[0:1, 0:1], min_val=1, max_val=NB // 2)
                with pe.Fori(0, cnt) as i:
                    for x in X2:
                        pe.wait_ge(s_setup, i * 2 + (x + 1))
                        pe.matmul(pq[x][:, 0:P], NN[x][:, :], ident[:, :], start=True, stop=True).then_inc(s_nt, 1)
                        pe.matmul(pst[x][:, 0:P], ident[:, :], ident[:, :], start=True, stop=False)
                        pe.matmul(pst[x][:, 0:P], NN[x][:, :], ident[:, :], start=False, stop=True).then_inc(s_sp, 1)
                    for k in range(LEVELS):
                        h, g = (k % 2), ((k + 1) % 2)
                        for x in X2:
                            if k == 0:
                                pe.wait_ge(s_q, i * 2 + (x + 1))
                                pw_k, qw_k = NN[x][:, :], NT[x][:, :]
                            else:
                                pe.wait_ge(s_p, i * 12 + (2 * (k - 1) + x + 1))
                                pw_k, qw_k = PQ[x][k % 2][:, 0, :], PQ[x][k % 2][:, 1, :]
                            if k < LEVELS - 1:
                                last = pe.matmul(pq[x][:, 0:P], qw_k, pw_k, start=True, stop=True)
                                if k < LEVELS - 2:
                                    last = pe.matmul(pq[x][:, P:2 * P], pw_k, qw_k, start=True, stop=True)
                                last.then_inc(s_lv, 1)
                            if k:
                                pe.wait_ge(s_st, i * 14 + (2 * (k - 1) + x + 1))
                                pe.matmul(pst[x][:, 0:P], pw_k, ST[x][:, :], start=False, stop=True, skip_group_check=True).then_inc(s_sp, 1)
                        if k == 0:
                            pe.wait_ge(s_zx, i + 1)
                            zrow(i + 1)
                            chain_v(pe, 0, i)
                        if k == 1:
                            chain_d(pe, 0, i)
                        if k == 2:
                            chain_v(pe, 1, i)
                        if k == 3:
                            chain_d(pe, 1, i)
                        if k == 5:
                            pe.wait_ge(s_keep, i + 1)
                            pe.wait_ge(s_FT, i * 2 + 4)
                            for x in X2:
                                for r in range(2):
                                    last = pe.matmul(pv[:, D + 2 * x + r:D + 2 * x + r + 1], FT[x][:, r * P:(r + 1) * P], ones[:, 0:1], start=True, stop=True)
                            last.then_inc(s_cnt, 1)
                    for x in X2:
                        pe.wait_ge(s_st, i * 14 + (12 + x + 1))
                        pe.wait_ge(s_R, i * 2 + (x + 1))
                        for r in range(2):
                            last = pe.matmul(pw[:, x * D + r * P:x * D + (r + 1) * P], RR[x][:, r * P:(r + 1) * P], ST[x][:, :], start=True, stop=True)
                    last.then_inc(s_wt, 1)
                for x in X2:
                    chain_v(pe, x, cnt)
                    chain_d(pe, x, cnt)
                pe.wait_ge(s_m, cnt * 2 + 3)
                for a in range(2):
                    for b in range(2):
                        last = pe.matmul(pd[:, a * D + b * P:a * D + (b + 1) * P], M[:, b, a * P:(a + 1) * P], ident[:, :], start=True, stop=True)
                last.then_inc(s_fin, 1)

            @block.scalar
            def _(a):
                def zrow_kept():
                    a.activation(zx[:, :, :].rearrange("p a b -> p (a b)"), pz[:, 0:D], ACT.Copy).then_inc(s_zx, 1)
                a.wait_ge(s_zr, 1)
                zrow_kept()
                cnt = a.value_load(nrun[0:1, 0:1], min_val=1, max_val=NB // 2)
                with a.Fori(0, cnt) as i:
                    for x in X2:
                        a.wait_ge(s_nt, i * 2 + (x + 1))
                        a.activation(NT[x][:, :], pq[x][:, 0:P], ACT.Copy).then_inc(s_q, 1)
                    for k in range(LEVELS):
                        for x in X2:
                            a.wait_ge(s_sp, i * 14 + (2 * k + x + 1))
                            a.activation(ST[x][:, :], pst[x][:, 0:P], ACT.Copy).then_inc(s_st, 1)
                        if k == 0:
                            a.wait_ge(s_zr, i + 2)
                            a.wait_ge(s_setup, i * 2 + 2)
                            zrow_kept()
                    a.wait_ge(s_wt, i + 1)
                    a.wait_ge(s_v, i * 2 + 2)
                    a.activation(WT[:, :, :, :].rearrange("p x a b -> p (x a b)"), pw[:, :], ACT.Copy).then_inc(s_wts, 1)

            @block.vector
            def _(v):
                dc = [0]

                def setup(x, i2, base):
                    n = [0]

                    def link(ins):
                        n[0] += 1
                        ins.then_inc(s_dc, 1)
                        v.wait_ge(s_dc, base + (4 * x + n[0]))
                    zrow = zx[:, x, :]
                    for k, q in enumerate((Z, QO, QL)):
                        last = v.scalar_tensor_tensor(q3[:, k, :], zrow, parn[:, x, q:q + 1], zrow, ALU.is_lt, ALU.mult)
                    link(last)
                    link(v.tensor_reduce(pred[:, :], q3[:, :, :], AX.X, ALU.max))
                    v.tensor_tensor(nxt[:, x, 0:2], pred[:, 0:2], parn[:, x, FS:FO + 1], ALU.max)
                    v.tensor_copy(nxt[:, x, 2:4], parn[:, x, CO:SO + 1])
                    link(v.tensor_scalar(nxt[:, x, 4:5], pred[:, 2:3], parn[:, x, Z:Z + 1], parn[:, x, D1:D1 + 1], ALU.is_equal, ALU.mult))
                    v.tensor_scalar(e1[:, :], zrow, nxt[:, x, 0:1], nxt[:, x, 2:3], ALU.is_equal, ALU.mult)
                    link(v.tensor_scalar(e2[:, :], zrow, nxt[:, x, 1:2], nxt[:, x, 3:4], ALU.is_equal, ALU.mult))
                    v.tensor_tensor(NN[x][:, :], e1[:, :], e2[:, :], ALU.add).then_inc(s_setup, 1)

                def v_kept(x, i2):
                    v.wait_ge(s_v, i2 + (x + 1))
                    v.tensor_copy(V[:, :], pv[:, 0:D]).then_inc(s_vs, 1)

                def m_update(x, i2):
                    v.wait_ge(s_dl, i2 + (x + 1))
                    for r in range(2):
                        last = v.scalar_tensor_tensor(M[:, r, :], M[:, r, :], kp[:, x, r:r + 1], pd[:, r * D:(r + 1) * D], ALU.mult, ALU.add)
                    last.then_inc(s_m, 1)

                v.wait_ge(s_c, 5)
                v.wait_ge(s_par, 1)
                v.wait_ge(s_keep, 1)
                v.wait_ge(s_zx, 1)
                for x in X2:
                    setup(x, 0, 0)
                cnt = v.value_load(nrun[0:1, 0:1], min_val=1, max_val=NB // 2)
                with v.Fori(0, cnt) as i:
                    for k in range(LEVELS - 1):
                        g = (k + 1) % 2
                        for x in X2:
                            v.wait_ge(s_lv, i * 12 + (2 * k + x + 1))
                            w = 2 if k < LEVELS - 2 else 1
                            v.tensor_copy(PQ[x][g][:, 0:w, :].rearrange("p a b -> p (a b)"), pq[x][:, 0:w * P]).then_inc(s_p, 1)
                        if k == 0:
                            v_kept(0, i * 2)
                        if k == 1:
                            v.wait_ge(s_zx, i + 2)
                            v.wait_ge(s_par, i + 2)
                            v.wait_ge(s_cur, i + 1)
                            setup(0, i * 2, i * 8 + 8)
                            m_update(0, i * 2)
                        if k == 2:
                            v_kept(1, i * 2)
                        if k == 3:
                            setup(1, i * 2, i * 8 + 8)
                            m_update(1, i * 2)
                    v.wait_ge(s_cnt, i + 1)
                    v.tensor_scalar(kp[:, :, :].rearrange("p a b -> p (a b)"), pv[:, D:D + 4], -1.0, 1.0, ALU.mult, ALU.add).then_inc(s_keep, 1)
                    v.wait_ge(s_keep, i + 2)
                for x in X2:
                    v_kept(x, cnt * 2)
                    m_update(x, cnt * 2)
                v.wait_ge(s_fin, 1)
                v.tensor_copy(mt[:, :, :].rearrange("p a b -> p (a b)"), pd[:, :]).then_inc(s_mo, 1)

            @block.sync
            def _(sp):
                sp.wait_ge(s_mo, 1)
                sp.dma_start(mT_out.rearrange("(a p) c -> p a c", p=P), mt[:, :, :]).then_inc(s_out, 16)
                sp.wait_ge(s_out, 16)
    keep_ctx.close()

def dram_rows(ap1d, parts, n, at=0):
    return bass.AP(tensor=ap1d.tensor, offset=at, ap=[[0, parts], [1, n]])


class Chain:

    def __init__(self, eng, sem, base=0):
        self.eng, self.sem, self.base, self.n = eng, sem, base, 0

    def link(self, ins):
        self.n += 1
        ins.then_inc(self.sem, 1)
        self.eng.wait_ge(self.sem, self.base + self.n)


def over_tiles(eng, first, body, last):
    with eng.Fori(0, (last - first) // 2) as h:
        for b in range(2):
            body(h * 2 + (first + b), (first + b) % 2, h)


T = 125
NT = 50
H = 8
DH = 32
C = 256
QKV = 3 * C
RR_ = 17
PR = RR_ * DH
FEAT = PR + 1 + DH
KW = FEAT + DH // 2
VW = DH + 1
G5 = 5
SCALE = DH ** 0.25
EPS_N = 1e-12


def layer_norm(nc, prefix, xs, xn, from_dram, xT_dram):
    with ExitStack() as c:
        c.callback(nc.all_engine_barrier)
        def sb(n, s, t=F32):
            return c.enter_context(nc.sbuf_tensor(prefix + n, s, t))

        def sem(n):
            return c.enter_context(a_semaphore(nc, prefix + n))
        st = sb("stats", [T, G5, 6]); mv = sb("mean_var", [T, G5, 2]); sd = sb("sd", [T, G5]); eps = sb("eps", [T, 1])
        ident = sb("ident", [P, P]); xT = sb("xT", [P, 2, 2 * T])
        ps = [c.enter_context(nc.psum_tensor(f"{prefix}ps{b}", [P, 512], F32)) for b in range(2)]
        s_c = sem("consts"); s_ld = [sem(f"loaded{b}") for b in range(2)]; s_dv = sem("dve"); s_go = sem("dve_goes_on"); s_var = sem("var"); s_sd = sem("sd_ready")
        s_xn = sem("xn_ready"); s_tp = sem("transposed"); s_kept = sem("xT_kept"); s_st = sem("xT_stored")
        if xs is None:
            xs = sb("xs", [T, 2, G5, C])
        with nc.Block() as block:
            @block.gpsimd
            def _(g):
                g.memset(ident[:, :], 0.0).then_inc(s_c, 1)
                g.memset(eps[:, :], 1e-5).then_inc(s_c, 1)
                g.wait_ge(s_c, 2)
                g.affine_select(out=ident[:, :], in_=ident[:, :], compare_op=ALU.not_equal, fill=1.0, base=0,
                                pattern=[[-1, P]], channel_multiplier=1).then_inc(s_c, 1)

            def group(q, b):
                return xs[:, b] if from_dram is not None else xs[:, bass.ds(q * G5, G5), :]

            @block.sync
            def _(sp):
                def body(q, b, h_):
                    if from_dram is not None:
                        sp.wait_ge(s_xn, q + 1)
                        sp.dma_start(xs[:, b], from_dram[bass.ds(q * (G5 * T), G5 * T), :].rearrange("(t p) c -> p t c", p=T)).then_inc(s_ld[b], 16)
                if from_dram is not None:
                    over_tiles(sp, 0, body, NT // G5)

            @block.vector
            def _(v):
                v.engine_nop().then_inc(s_xn, 2)

                def body(q, b, h_):
                    ch = Chain(v, s_dv, q * 2)
                    x_ = group(q, b)
                    if from_dram is not None:
                        v.wait_ge(s_ld[b], h_ * 16 + 16)
                    for j in range(G5):
                        last = v.bn_stats(st[:, j, :], x_[:, j, :])
                    ch.link(last)
                    v.sem_inc(s_go, 1)
                    for j in range(G5):
                        last = v.bn_aggr(mv[:, j, :], st[:, j, :])
                    last.then_inc(s_var, 1)
                    v.wait_ge(s_sd, q + 1)
                    ch.link(v.reciprocal(sd[:, :], sd[:, :]))
                    for j in range(G5):
                        last = v.tensor_scalar(xn[:, bass.ds(q * G5 + j, 1), :].rearrange("p o c -> p (o c)"), x_[:, j, :] if from_dram is not None else xs[:, bass.ds(q * G5 + j, 1), :].rearrange("p o c -> p (o c)"),
                                               mv[:, j, 0:1], sd[:, j:j + 1], ALU.subtract, ALU.mult)
                    last.then_inc(s_xn, 1)
                over_tiles(v, 0, body, NT // G5)

            @block.scalar
            def _(a):
                a.wait_ge(s_c, 3)

                def body(q, b, h_):
                    a.wait_ge(s_var, q + 1)
                    a.wait_ge(s_xn, q + 2)
                    a.activation(sd[:, :], mv[:, :, 1], ACT.Sqrt, bias=eps[:, 0:1]).then_inc(s_sd, 1)
                over_tiles(a, 0, body, NT // G5)
    return


def transposed_tiles(nc, prefix, xn, xT_dram):
    with ExitStack() as c:
        c.callback(nc.all_engine_barrier)
        ident = c.enter_context(nc.sbuf_tensor(prefix + "ident", [P, P], F32))
        xT = c.enter_context(nc.sbuf_tensor(prefix + "xT", [P, 2, 2 * T], F32))
        ps = [c.enter_context(nc.psum_tensor(f"{prefix}ps{b}", [P, 512], F32)) for b in range(2)]
        s_c, s_tp, s_kept, *s_st = (c.enter_context(a_semaphore(nc, prefix + n)) for n in ("consts", "transposed", "kept", "stored0", "stored1"))
        xs = c.enter_context(nc.sbuf_tensor(prefix + "xs", [T, 2, C], F32))
        s_xs = c.enter_context(a_semaphore(nc, prefix + "copied"))
        with nc.Block() as block:
            @block.gpsimd
            def _(g):
                g.memset(ident[:, :], 0.0).then_inc(s_c, 1)
                g.wait_ge(s_c, 1)
                g.affine_select(out=ident[:, :], in_=ident[:, :], compare_op=ALU.not_equal, fill=1.0, base=0,
                                pattern=[[-1, P]], channel_multiplier=1).then_inc(s_c, 1)

            @block.vector
            def _(v):
                v.wait_ge(s_c, 2)
                v.engine_nop().then_inc(s_tp, 2)

                def body(t, b, h_):
                    v.wait_ge(s_tp, t + 1)
                    v.tensor_copy(xs[:, b, :], xn[:, bass.ds(t, 1), :].rearrange("p o c -> p (o c)")).then_inc(s_xs, 1)
                over_tiles(v, 0, body, NT)

            @block.tensor
            def _(pe):
                pe.wait_ge(s_c, 2)

                def body(t, b, h_):
                    pe.wait_ge(s_xs, t + 1)
                    pe.wait_ge(s_kept, t + 1)
                    for k in range(2):
                        last = pe.matmul(ps[b][:, k * T:(k + 1) * T], xs[:, b, k * P:(k + 1) * P], ident[0:T, 0:T], start=True, stop=True)
                    last.then_inc(s_tp, 1)
                over_tiles(pe, 0, body, NT)

            @block.scalar
            def _(a):
                a.wait_ge(s_c, 2)
                a.sem_inc(s_kept, 2)
                for q in s_st:
                    a.sem_inc(q, 16)

                def body(t, b, h_):
                    a.wait_ge(s_tp, t + 3)
                    a.wait_ge(s_st[b], h_ * 16 + 16)
                    a.activation(xT[:, b, :], ps[b][:, 0:2 * T], ACT.Copy).then_inc(s_kept, 1)
                over_tiles(a, 0, body, NT)

            @block.sync
            def _(sp):
                def body(t, b, h_):
                    sp.wait_ge(s_kept, t + 3)
                    sp.dma_start(xT_dram[bass.ds(t, 1), :, :].rearrange("o p c -> (o p) c"), xT[:, b, :]).then_inc(s_st[b], 16)
                over_tiles(sp, 0, body, NT)
                for q in s_st:
                    sp.wait_ge(q, 16 + 8 * NT)


def products(eng, dst, src_feat, heads):
    for h in heads:
        f = src_feat(h)
        out = dst(h).rearrange("p (r i) -> p r i", i=DH)
        once = bass.AP(tensor=f.tensor, offset=f.offset + PR + 1, ap=[list(f.ap[0]), [0, RR_], [1, DH]])
        moved = bass.AP(tensor=f.tensor, offset=f.offset + PR + 1, ap=[list(f.ap[0]), [1, RR_], [1, DH]])
        last = eng.tensor_tensor(out, once, moved, ALU.mult)
    return last


def moments(nc, xT_dram, wqkvT, bqkv, mom_dram):
    with ExitStack() as c:
        c.callback(nc.all_engine_barrier)
        def sb(n, s, t=F32):
            return c.enter_context(nc.sbuf_tensor("mo_" + n, s, t))

        def sem(n):
            return c.enter_context(a_semaphore(nc, "mo_" + n))
        w = sb("w", [P, 2, 2 * C]); bias = sb("bias", [T, 2 * C]); xT = sb("xT", [P, 2, 2 * T])
        ks = sb("ks", [T, C]); sq = sb("sq", [T, C]); ss = sb("ss", [T, H])
        feat = [sb(f"feat{b}", [T, H, KW]) for b in range(2)]
        vh = [sb(f"vh{b}", [T, H, VW]) for b in range(2)]
        out = sb("out", [P, 5, 512])
        main = [c.enter_context(nc.psum_tensor(f"mo_main{q}", [P, 512], F32)) for q in range(4)]
        tail = c.enter_context(nc.psum_tensor("mo_tail", [P, 512], F32))
        kv = [c.enter_context(nc.psum_tensor(f"mo_kv{b}", [P, 512], F32)) for b in range(2)]
        s_w = sem("weights"); s_x = [sem(f"xT_loaded{b}") for b in range(2)]; s_kv = sem("kv_in_psum"); s_ks = sem("kv_kept"); s_sq = sem("norms_wanted")
        s_rt = sem("norms_ready"); s_kn = sem("k_normed"); s_fd = sem("features_dve"); s_fp = sem("features_pool"); s_mm = sem("tile_summed")
        s_dv = sem("dve"); s_c = sem("consts"); s_o = sem("kept"); s_out = sem("stored")
        TAIL = FEAT - 512
        with nc.Block() as block:
            @block.sync
            def _(sp):
                sp.dma_start(w[:, :, :], wqkvT[:, C:QKV].rearrange("(a p) n -> p a n", p=P)).then_inc(s_w, 16)
                sp.dma_start(bias[:, :], dram_rows(bqkv, T, 2 * C, C)).then_inc(s_w, 16)

                def body(t, b, h_):
                    sp.wait_ge(s_kv, t + 1)
                    sp.dma_start(xT[:, b, :], xT_dram[bass.ds(t, 1), :, :].rearrange("o p c -> (o p) c")).then_inc(s_x[b], 16)
                over_tiles(sp, 0, body, NT)
                sp.wait_ge(s_o, 5)
                for h in range(H):
                    q, p0 = h // 2, 64 * (h % 2)
                    sp.dma_start(mom_dram[h, :, 0:512], out[p0:p0 + VW, q, :]).then_inc(s_out, 16)
                    sp.dma_start(mom_dram[h, :, 512:FEAT], out[p0:p0 + VW, 4, q * TAIL:(q + 1) * TAIL]).then_inc(s_out, 16)
                sp.wait_ge(s_out, 16 * 2 * H)

            @block.tensor
            def _(pe):
                pe.wait_ge(s_w, 32)
                pe.wait_ge(s_c, 2)
                pe.sem_inc(s_kv, 2)
                pe.sem_inc(s_mm, 2)

                def kv_of(t, b, turn):
                    pe.wait_ge(s_x[b], turn * 16 + 16)
                    pe.wait_ge(s_ks, t + 1)
                    for k in range(2):
                        last = pe.matmul(kv[b][0:T, :], xT[:, b, k * T:(k + 1) * T], w[:, k, :], start=(k == 0), stop=(k == 1))
                    last.then_inc(s_kv, 1)

                def sums(t, b):
                    pe.wait_ge(s_fd, t + 1)
                    pe.wait_ge(s_fp, t + 1)
                    for h in range(H):
                        q, p0 = h // 2, 64 * (h % 2)
                        pe.matmul(main[q][p0:p0 + VW, :], vh[b][:, h, :], feat[b][:, h, 0:512], start=False, stop=True, skip_group_check=True)
                        last = pe.matmul(tail[p0:p0 + VW, q * TAIL:(q + 1) * TAIL], vh[b][:, h, :], feat[b][:, h, 512:FEAT], start=False, stop=True, skip_group_check=True)
                    last.then_inc(s_mm, 1)
                kv_of(0, 0, 0)
                with pe.Fori(0, (NT - 2) // 2) as h2:
                    for b in range(2):
                        kv_of(h2 * 2 + (b + 1), 1 - b, h2 + b)
                        sums(h2 * 2 + b, b)
                kv_of(NT - 1, 1, NT // 2 - 1)
                sums(NT - 2, 0)
                sums(NT - 1, 1)

            @block.vector
            def _(v):
                for q in range(4):
                    v.memset(main[q][:, :], 0.0)
                v.memset(tail[:, :], 0.0).then_inc(s_c, 1)
                for b in range(2):
                    v.memset(vh[b][:, :, 0:1], 1.0)
                    last = v.memset(feat[b][:, :, PR:PR + 1], 1.0)
                last.then_inc(s_c, 1)
                v.wait_ge(s_c, 2)
                v.wait_ge(s_w, 32)
                v.engine_nop().then_inc(s_ks, 2)

                def body(t, b, h_):
                    ch = Chain(v, s_dv, t * 4)
                    v.wait_ge(s_kv, t + 3)
                    v.wait_ge(s_mm, t + 1)
                    v.tensor_tensor(vh[b][:, :, 1:VW], kv[b][0:T, C:2 * C].rearrange("p (h d) -> p h d", d=DH), bias[:, C:2 * C].rearrange("p (h d) -> p h d", d=DH), ALU.add)
                    v.tensor_tensor(ks[:, :], kv[b][0:T, 0:C], bias[:, 0:C], ALU.add).then_inc(s_ks, 1)
                    v.wait_ge(s_ks, t + 3)
                    ch.link(v.tensor_tensor(sq[:, :], ks[:, :], ks[:, :], ALU.mult))
                    v.tensor_reduce(ss[:, :], sq[:, :].rearrange("p (h d) -> p h d", d=DH), AX.X, ALU.add).then_inc(s_sq, 1)
                    v.wait_ge(s_rt, t + 1)
                    ch.link(v.tensor_scalar(ss[:, :], ss[:, :], EPS_N, None, ALU.max))
                    ch.link(v.reciprocal(ss[:, :], ss[:, :]))
                    ch.link(v.tensor_scalar(ss[:, :], ss[:, :], SCALE, None, ALU.mult))
                    ks3 = ks[:, :].rearrange("p (h d) -> p h d", d=DH)
                    v.tensor_tensor(feat[b][:, :, PR + 1:FEAT], ks3, ss[:, :].unsqueeze(2).to_broadcast([T, H, DH]), ALU.mult)
                    v.tensor_tensor(feat[b][:, :, FEAT:KW], ks3[:, :, 0:DH // 2], ss[:, :].unsqueeze(2).to_broadcast([T, H, DH // 2]), ALU.mult).then_inc(s_kn, 1)
                    v.wait_ge(s_kn, t + 1)
                    products(v, lambda h: feat[b][:, h, 0:PR], lambda h: feat[b][:, h, 0:1], range(0, 5)).then_inc(s_fd, 1)
                over_tiles(v, 0, body, NT)
                v.wait_ge(s_mm, NT + 2)
                for q in range(4):
                    v.tensor_copy(out[:, q, :], main[q][:, :]).then_inc(s_o, 1)
                v.tensor_copy(out[:, 4, :], tail[:, :]).then_inc(s_o, 1)

            @block.scalar
            def _(a):
                def body(t, b, h_):
                    a.wait_ge(s_sq, t + 1)
                    a.activation(ss[:, :], ss[:, :], ACT.Sqrt).then_inc(s_rt, 1)
                over_tiles(a, 0, body, NT)

            @block.gpsimd
            def _(g):
                def body(t, b, h_):
                    g.wait_ge(s_kn, t + 1)
                    g.sem_inc(s_c, 1)
                    products(g, lambda h: feat[b][:, h, 0:PR], lambda h: feat[b][:, h, 0:1], range(5, H)).then_inc(s_fp, 1)
                over_tiles(g, 0, body, NT)


def attend(nc, xT_dram, wqkvT, bqkv, temp, wprojT, bproj, mom_dram, mT_dram, x_dram, x1):
    with ExitStack() as c:
        c.callback(nc.all_engine_barrier)
        def sb(n, s, t=F32):
            return c.enter_context(nc.sbuf_tensor("at_" + n, s, t))

        def sem(n):
            return c.enter_context(a_semaphore(nc, "at_" + n))

        def ps(n):
            return c.enter_context(nc.psum_tensor("at_ps_" + n, [P, 512], F32))
        wq = sb("wq", [P, 2, C]); bq = sb("bq", [T, C]); tmp8 = sb("temp", [T, H]); wp = sb("wp", [P, 2, C]); bp = sb("bp", [T, C]); mT = sb("mT", [P, 2, C])
        ident = sb("ident", [P, P]); mom = sb("mom", [VW, H, FEAT]); momT = sb("momT", [P, 5, H, VW]); wt = sb("wt", [P, 5])
        xT = sb("xT", [P, 2, 2 * T]); xs = sb("xs", [T, 2, C])
        qs = sb("qs", [T, C]); sq = sb("sq", [T, C]); ss = sb("ss", [T, H])
        feat = [sb(f"feat{b}", [T, H, KW]) for b in range(2)]
        fT = [sb(f"fT{b}", [P, 4, T]) for b in range(2)]
        fE = [sb(f"fE{b}", [P, 4, T]) for b in range(2)]
        rec = sb("rec", [T, H]); o = sb("o", [T, C]); oT = sb("oT", [P, 2 * T])
        p_q = ps("q"); p_t = [ps(f"t{b}") for b in range(2)]; p_e = [ps(f"e{b}") for b in range(2)]; p_y = ps("y"); p_o = ps("o"); p_r = ps("r")
        names = ("w", "x_ld0", "x_ld1", "q_ps", "q_kept", "sq", "rt", "qn", "fd", "fp", "t_ps", "t_kept", "e_ps", "e_kept", "y_ps", "o_ready", "oT_ps", "oT_kept",
                 "r_ps", "r_kept", "consts", "momT_ps", "momT_kept", "dve", "momw", "xs_free")
        s = {n: sem(n) for n in names}
        with nc.Block() as block:
            @block.sync
            def _(sp):
                sp.dma_start(wq[:, :, :], wqkvT[:, 0:C].rearrange("(a p) n -> p a n", p=P)).then_inc(s["w"], 16)
                sp.dma_start(wp[:, :, :], wprojT.rearrange("(a p) n -> p a n", p=P)).then_inc(s["w"], 16)
                sp.dma_start(mT[:, :, :], mT_dram.rearrange("(a p) n -> p a n", p=P)).then_inc(s["w"], 16)
                sp.dma_start(bq[:, :], dram_rows(bqkv, T, C)).then_inc(s["w"], 16)
                sp.dma_start(bp[:, :], dram_rows(bproj, T, C)).then_inc(s["w"], 16)
                sp.dma_start(tmp8[:, :], dram_rows(temp, T, H)).then_inc(s["w"], 16)
                sp.dma_start(mom[:, :, :], mom_dram.rearrange("h e f -> e h f")).then_inc(s["w"], 16)

                def body(t, b, h_):
                    sp.wait_ge(s["r_kept"], t + 1)
                    sp.dma_start(xT[:, b, :], xT_dram[bass.ds(t, 1), :, :].rearrange("o p c -> (o p) c")).then_inc(s[f"x_ld{b}"], 16)
                    sp.dma_start(xs[:, b, :], x_dram[bass.ds(t * T, T), :]).then_inc(s[f"x_ld{b}"], 16)
                over_tiles(sp, 0, body, NT)

            @block.gpsimd
            def _(g):
                g.memset(ident[:, :], 0.0).then_inc(s["consts"], 1)
                g.memset(wt[:, :], 1.0).then_inc(s["consts"], 1)
                g.wait_ge(s["consts"], 2)
                g.affine_select(out=ident[:, :], in_=ident[:, :], compare_op=ALU.not_equal, fill=1.0, base=0,
                                pattern=[[-1, P]], channel_multiplier=1).then_inc(s["consts"], 1)
                g.memset(wt[0:DH, 0:1], 0.5).then_inc(s["consts"], 1)
                g.memset(wt[:, 4:5], SCALE ** 2).then_inc(s["consts"], 1)
                g.wait_ge(s["consts"], 5)
                g.memset(wt[0:DH, 4:5], 0.5).then_inc(s["consts"], 1)
                g.wait_ge(s["consts"], 6)
                g.memset(wt[DH:DH + 1, 4:5], SCALE ** 4).then_inc(s["consts"], 1)
                g.wait_ge(s["consts"], 7)
                for b in range(2):
                    g.memset(feat[b][:, :, PR:PR + 1], 1.0).then_inc(s["consts"], 1)
                g.wait_ge(s["consts"], 9)

                def body(t, b, h_):
                    g.wait_ge(s["qn"], t + 1)
                    g.sem_inc(s["xs_free"], 1)
                    products(g, lambda h: feat[b][:, h, 0:PR], lambda h: feat[b][:, h, 0:1], range(5, H)).then_inc(s["fp"], 1)
                over_tiles(g, 0, body, NT)

            @block.tensor
            def _(pe):
                pe.wait_ge(s["w"], 16 * 7)
                pe.wait_ge(s["consts"], 9)
                for h in range(H):
                    if h >= 2:
                        pe.wait_ge(s["momT_kept"], h - 1)
                    for k in range(5):
                        m = min(P, FEAT - k * P)
                        last = pe.matmul(p_t[h % 2][0:m, k * VW:(k + 1) * VW], mom[:, h, k * P:k * P + m], ident[0:VW, 0:VW], start=True, stop=True)
                    last.then_inc(s["momT_ps"], 1)
                pe.wait_ge(s["momT_kept"], H)
                pe.wait_ge(s["momw"], 5)
                pe.sem_inc(s["t_ps"], 1)

                def body(t, b, h_):
                    pe.wait_ge(s[f"x_ld{b}"], h_ * 32 + 32)
                    for k in range(2):
                        last = pe.matmul(p_q[0:T, 0:C], xT[:, b, k * T:(k + 1) * T], wq[:, k, :], start=(k == 0), stop=(k == 1))
                    last.then_inc(s["q_ps"], 1)
                    for k in range(2):
                        last = pe.matmul(p_r[0:T, 0:C], xT[:, b, k * T:(k + 1) * T], mT[:, k, :], start=(k == 0), stop=False)

                def out(t, b):
                    pe.wait_ge(s["fd"], t + 1)
                    pe.wait_ge(s["fp"], t + 1)
                    for g4 in range(2):
                        pe.wait_ge(s["e_kept"], t * 2 + (g4 + 1))
                        for j in range(4):
                            last = pe.matmul(p_e[g4][0:FEAT - 512, j * T:(j + 1) * T], feat[b][:, g4 * 4 + j, 512:FEAT], ident[0:T, 0:T], start=True, stop=True)
                        last.then_inc(s["e_ps"], 1)
                    def transposes(h):
                        pe.wait_ge(s["t_kept"], t * 8 + (h + 1))
                        for k in range(4):
                            last = pe.matmul(p_t[h % 2][:, k * T:(k + 1) * T], feat[b][:, h, k * P:(k + 1) * P], ident[0:T, 0:T], start=True, stop=True)
                        last.then_inc(s["t_ps"], 1)

                    def apply(h):
                        pe.wait_ge(s["t_kept"], t * 8 + (h + 3))
                        if h % 4 == 0:
                            pe.wait_ge(s["e_kept"], t * 2 + (h // 4 + 3))
                        for k in range(4):
                            pe.matmul(p_y[0:T, h * VW:(h + 1) * VW], fT[h % 2][:, k, :], momT[:, k, h, :], start=(k == 0), stop=False)
                        last = pe.matmul(p_y[0:T, h * VW:(h + 1) * VW], fE[h // 4][0:FEAT - 512, h % 4, :], momT[0:FEAT - 512, 4, h, :], start=False, stop=True)
                        last.then_inc(s["y_ps"], 1)
                    transposes(0)
                    for h in range(H):
                        if h + 1 < H:
                            transposes(h + 1)
                        apply(h)
                    pe.wait_ge(s["o_ready"], t + 1)
                    for k in range(2):
                        last = pe.matmul(p_o[:, k * T:(k + 1) * T], o[:, k * P:(k + 1) * P], ident[0:T, 0:T], start=True, stop=True)
                    last.then_inc(s["oT_ps"], 1)
                    pe.wait_ge(s["oT_kept"], t + 1)
                    for k in range(2):
                        last = pe.matmul(p_r[0:T, 0:C], oT[:, k * T:(k + 1) * T], wp[:, k, :], start=False, stop=(k == 1))
                    last.then_inc(s["r_ps"], 1)
                    pe.wait_ge(s["r_kept"], t + 3)

                def both(t, b, h_):
                    body(t, b, h_)
                    out(t, b)
                over_tiles(pe, 0, both, NT)

            @block.scalar
            def _(a):
                a.sem_inc(s["t_kept"], 2)
                a.sem_inc(s["e_kept"], 2)

                def body(t, b, h_):
                    a.wait_ge(s["sq"], t + 1)
                    a.activation(ss[:, :], ss[:, :], ACT.Sqrt).then_inc(s["rt"], 1)
                    for g4 in range(2):
                        a.wait_ge(s["e_ps"], t * 2 + (g4 + 1))
                        a.activation(fE[g4][0:FEAT - 512, :, :].rearrange("p a b -> p (a b)"), p_e[g4][0:FEAT - 512, 0:4 * T], ACT.Copy).then_inc(s["e_kept"], 1)
                    for h in range(H):
                        a.wait_ge(s["t_ps"], t * 8 + (h + 2))
                        a.activation(fT[h % 2][:, :, :].rearrange("p a b -> p (a b)"), p_t[h % 2][:, 0:4 * T], ACT.Copy).then_inc(s["t_kept"], 1)
                    a.wait_ge(s["oT_ps"], t + 1)
                    a.activation(oT[:, :], p_o[:, 0:2 * T], ACT.Copy).then_inc(s["oT_kept"], 1)
                over_tiles(a, 0, body, NT)

            @block.vector
            def _(v):
                for h in range(H):
                    v.wait_ge(s["momT_ps"], h + 1)
                    v.tensor_copy(momT[:, 0:4, h, :], p_t[h % 2][:, 0:4 * VW].rearrange("p (k e) -> p k e", e=VW))
                    v.tensor_copy(momT[0:FEAT - 512, 4, h, :], p_t[h % 2][0:FEAT - 512, 4 * VW:5 * VW]).then_inc(s["momT_kept"], 1)
                v.wait_ge(s["momT_kept"], H)
                v.wait_ge(s["consts"], 9)
                for k in range(5):
                    m = min(P, FEAT - k * P)
                    v.tensor_scalar(momT[0:m, k, :, :], momT[0:m, k, :, :], wt[0:m, k:k + 1], 1.0 / (NT * T), ALU.mult, ALU.mult).then_inc(s["momw"], 1)
                v.wait_ge(s["w"], 16 * 7)
                v.engine_nop().then_inc(s["r_kept"], 2)
                ch0 = Chain(v, s["dve"])
                ch0.link(v.tensor_scalar(tmp8[:, :], tmp8[:, :], SCALE * SCALE, None, ALU.mult))
                ch0.link(v.tensor_tensor(bp[:, :], bp[:, :], bp[:, :], ALU.max))

                def body(t, b, h_):
                    ch = Chain(v, s["dve"], t * 7 + 2)
                    v.wait_ge(s["q_ps"], t + 1)
                    ch.link(v.tensor_tensor(qs[:, :], p_q[0:T, 0:C], bq[:, :], ALU.add))
                    ch.link(v.tensor_tensor(sq[:, :], qs[:, :], qs[:, :], ALU.mult))
                    v.tensor_reduce(ss[:, :], sq[:, :].rearrange("p (h d) -> p h d", d=DH), AX.X, ALU.add).then_inc(s["sq"], 1)
                    v.wait_ge(s["rt"], t + 1)
                    ch.link(v.tensor_scalar(ss[:, :], ss[:, :], SCALE, EPS_N, ALU.mult, ALU.max))
                    ch.link(v.reciprocal(ss[:, :], ss[:, :]))
                    ch.link(v.tensor_tensor(ss[:, :], ss[:, :], tmp8[:, :], ALU.mult))
                    qs3 = qs[:, :].rearrange("p (h d) -> p h d", d=DH)
                    v.tensor_tensor(feat[b][:, :, PR + 1:FEAT], qs3, ss[:, :].unsqueeze(2).to_broadcast([T, H, DH]), ALU.mult)
                    v.tensor_tensor(feat[b][:, :, FEAT:KW], qs3[:, :, 0:DH // 2], ss[:, :].unsqueeze(2).to_broadcast([T, H, DH // 2]), ALU.mult).then_inc(s["qn"], 1)
                    v.wait_ge(s["qn"], t + 1)
                    products(v, lambda h: feat[b][:, h, 0:PR], lambda h: feat[b][:, h, 0:1], range(0, 5)).then_inc(s["fd"], 1)
                    v.wait_ge(s["y_ps"], t * 8 + 8)
                    y3 = p_y[0:T, 0:H * VW].rearrange("p (h e) -> p h e", e=VW)
                    ch.link(v.reciprocal(rec[:, :], y3[:, :, 0]))
                    v.tensor_tensor(o[:, :].rearrange("p (h d) -> p h d", d=DH), y3[:, :, 1:VW], rec[:, :].unsqueeze(2).to_broadcast([T, H, DH]), ALU.mult).then_inc(s["o_ready"], 1)
                    x1t = x1[:, bass.ds(t, 1), :].rearrange("p o c -> p (o c)")
                    v.wait_ge(s["r_ps"], t + 1)
                    ch.link(v.tensor_tensor(x1t, p_r[0:T, 0:C], bp[:, :], ALU.add))
                    v.tensor_tensor(x1t, x1t, xs[:, b, :], ALU.add).then_inc(s["r_kept"], 1)
                over_tiles(v, 0, body, NT)

E_N = 8
HID = 1024
CAP = -(-5 * NT * T // (4 * E_N))
ROOM = CAP
NONE = 100000
ZW = E_N * ROOM * C // (4 * P)
F_MAX = 3.4028234663852886e38


def route(nc, xT_dram, gate_w, gate_b, xn, buf_dram, slot_i, coef):
    with ExitStack() as c:
        c.callback(nc.all_engine_barrier)
        def sb(n, s, t=F32):
            return c.enter_context(nc.sbuf_tensor("ro_" + n, s, t))

        def sem(n):
            return c.enter_context(a_semaphore(nc, "ro_" + n))
        gw = sb("gw", [P, 2, E_N]); gb = sb("gb", [T, E_N]); xT = sb("xT", [P, 2, 2 * T]); zero = sb("zero", [P, ZW])
        lg = sb("lg", [T, NT, E_N]); w8 = sb("w8", [T, NT, E_N]); oh = sb("oh", [T, NT, E_N]); ex = sb("ex", [T, NT, E_N]); z50 = sb("z50", [T, NT])
        m = sb("m", [T, NT]); idx = sb("idx", [T, NT]); pos = sb("pos", [T, NT]); kept = sb("kept", [T, NT]); dst = sb("dst", [T, NT])
        tri = sb("tri", [T, T]); ones = sb("ones", [T, T]); dst_i = sb("dst_i", [T, NT], I32)
        rowi = [sb(f"rowi{b}", [T, 1], I32) for b in range(2)]
        rows = [sb(f"rows{b}", [T, C]) for b in range(2)]
        p_l = [c.enter_context(nc.psum_tensor(f"ro_l{b}", [P, 512], F32)) for b in range(2)]
        p_c = c.enter_context(nc.psum_tensor("ro_c", [P, 512], F32)); p_s = c.enter_context(nc.psum_tensor("ro_s", [P, 512], F32))
        s_w = sem("w"); s_z = sem("zero"); s_zf = sem("buf_zeroed"); s_x = [sem(f"x{b}") for b in range(2)]; s_l = sem("l_ps"); s_lk = sem("l_kept"); s_dv = sem("dve")
        s_e = sem("exp_wanted"); s_ex = sem("exp_ready"); s_oh = sem("oh_ready"); s_cp = sem("counts_ps"); s_di = sem("rows_known")
        s_c = sem("consts"); s_cpd = sem("copied"); s_sc = [sem(f"scattered{b}") for b in range(2)]; s_go = sem("pool_goes_on")
        with nc.Block() as block:
            @block.sync
            def _(sp):
                sp.dma_start(gw[:, :, :], gate_w.rearrange("(a p) n -> p a n", p=P)).then_inc(s_w, 16)
                sp.dma_start(gb[:, :], dram_rows(gate_b, T, E_N)).then_inc(s_w, 16)
                sp.wait_ge(s_z, 1)
                flat = bass.AP(tensor=buf_dram.tensor, offset=0, ap=[[4 * ZW, P], [1, 4 * ZW]])
                for k in range(4):
                    sp.dma_start(flat[:, k * ZW:(k + 1) * ZW], zero[:, :]).then_inc(s_zf, 16)

                def body(t, b, h_):
                    sp.wait_ge(s_l, t + 1)
                    sp.dma_start(xT[:, b, :], xT_dram[bass.ds(t, 1), :, :].rearrange("o p c -> (o p) c")).then_inc(s_x[b], 16)
                over_tiles(sp, 0, body, NT)

            @block.tensor
            def _(pe):
                pe.wait_ge(s_w, 32)
                pe.sem_inc(s_l, 2)

                def body(t, b, h_):
                    pe.wait_ge(s_x[b], h_ * 16 + 16)
                    pe.wait_ge(s_lk, t + 1)
                    for k in range(2):
                        last = pe.matmul(p_l[b][0:T, 0:E_N], xT[:, b, k * T:(k + 1) * T], gw[:, k, :], start=(k == 0), stop=(k == 1))
                    last.then_inc(s_l, 1)
                over_tiles(pe, 0, body, NT)
                pe.wait_ge(s_c, 5)
                pe.wait_ge(s_oh, 1)
                ohf = oh[:, :, :].rearrange("p t e -> p (t e)")
                pe.matmul(p_c[0:T, 0:NT * E_N], tri[:, :], ohf, start=True, stop=True)
                pe.matmul(p_s[0:T, 0:NT * E_N], ones[:, :], ohf, start=True, stop=True).then_inc(s_cp, 1)

            @block.scalar
            def _(a):
                a.wait_ge(s_e, 1)
                a.activation(lg[:, :, :], lg[:, :, :], ACT.Exp).then_inc(s_ex, 1)

            @block.vector
            def _(v):
                v.wait_ge(s_w, 32)
                v.engine_nop().then_inc(s_lk, 2)

                def body(t, b, h_):
                    v.wait_ge(s_l, t + 3)
                    v.tensor_tensor(lg[:, bass.ds(t, 1), :].rearrange("p o e -> p (o e)"), p_l[b][0:T, 0:E_N], gb[:, :], ALU.add).then_inc(s_lk, 1)
                over_tiles(v, 0, body, NT)
                v.wait_ge(s_lk, NT + 2)
                v.wait_ge(s_c, 5)
                ch = Chain(v, s_dv)

                def each(a):
                    return a[:, :].unsqueeze(2).to_broadcast([T, NT, E_N])
                ch.link(v.tensor_reduce(m[:, :], lg[:, :, :], AX.X, ALU.max))
                v.tensor_tensor(lg[:, :, :], lg[:, :, :], each(m), ALU.subtract).then_inc(s_e, 1)
                v.wait_ge(s_ex, 1)
                ch.link(v.tensor_reduce(m[:, :], lg[:, :, :], AX.X, ALU.add))
                ch.link(v.reciprocal(m[:, :], m[:, :]))
                ch.link(v.tensor_tensor(lg[:, :, :], lg[:, :, :], each(m), ALU.mult))
                ch.link(v.tensor_reduce(coef[:, :], lg[:, :, :], AX.X, ALU.max))
                ch.link(v.tensor_tensor(oh[:, :, :], lg[:, :, :], each(coef), ALU.is_equal))
                ch.link(v.tensor_tensor(lg[:, :, :], oh[:, :, :], w8[:, :, :], ALU.mult))
                ch.link(v.tensor_reduce(idx[:, :], lg[:, :, :], AX.X, ALU.max))
                v.tensor_tensor(oh[:, :, :], lg[:, :, :], each(idx), ALU.is_equal).then_inc(s_oh, 1)
                v.wait_ge(s_oh, 1)
                v.wait_ge(s_cp, 1)
                tot = p_s[0:T, 0:NT * E_N].rearrange("p (t e) -> p t e", e=E_N)
                for e in range(E_N):
                    last = v.tensor_tensor_scan(ex[:, :, e], tot[:, :, e], z50[:, :], 0.0, ALU.add, ALU.add)
                ch.link(last)
                ch.link(v.tensor_tensor(ex[:, :, :], ex[:, :, :], tot, ALU.subtract))
                ch.link(v.tensor_tensor(ex[:, :, :], ex[:, :, :], p_c[0:T, 0:NT * E_N].rearrange("p (t e) -> p t e", e=E_N), ALU.add))
                ch.link(v.tensor_tensor(ex[:, :, :], ex[:, :, :], oh[:, :, :], ALU.mult))
                ch.link(v.tensor_reduce(pos[:, :], ex[:, :, :], AX.X, ALU.add))
                v.tensor_scalar(idx[:, :], idx[:, :], -float(ROOM), float(E_N * ROOM), ALU.mult, ALU.add)
                ch.link(v.tensor_scalar(pos[:, :], pos[:, :], -1.0, None, ALU.add))
                ch.link(v.tensor_scalar(kept[:, :], pos[:, :], float(CAP), None, ALU.is_lt))
                ch.link(v.tensor_tensor(coef[:, :], coef[:, :], kept[:, :], ALU.mult))
                ch.link(v.tensor_tensor(dst[:, :], pos[:, :], idx[:, :], ALU.add))
                ch.link(v.tensor_scalar(kept[:, :], kept[:, :], -float(NONE), float(NONE), ALU.mult, ALU.add))
                ch.link(v.tensor_tensor(dst[:, :], dst[:, :], kept[:, :], ALU.add))
                v.tensor_copy(dst_i[:, :], dst[:, :]).then_inc(s_di, 1)
                ch.link(v.tensor_scalar(pos[:, :], pos[:, :], float(CAP - 1), None, ALU.min))
                ch.link(v.tensor_tensor(pos[:, :], pos[:, :], idx[:, :], ALU.add))
                ch.link(v.tensor_copy(slot_i[:, :], pos[:, :]))

            @block.gpsimd
            def _(g):
                g.memset(zero[:, :], 0.0).then_inc(s_z, 1)
                g.iota(w8[:, :, :], pattern=[[0, NT], [-1, E_N]], base=E_N, channel_multiplier=0, allow_small_or_imprecise_dtypes=True).then_inc(s_c, 1)
                g.memset(z50[:, :], 0.0).then_inc(s_c, 1)
                g.memset(ones[:, :], 1.0).then_inc(s_c, 1)
                g.memset(tri[:, :], 1.0).then_inc(s_c, 1)
                g.wait_ge(s_c, 4)
                g.affine_select(out=tri[:, :], in_=tri[:, :], compare_op=ALU.is_ge, fill=0.0, base=0,
                                pattern=[[1, T]], channel_multiplier=-1).then_inc(s_c, 1)
                g.wait_ge(s_di, 1)
                g.wait_ge(s_zf, 64)

                def scatter(t, b):
                    g.tensor_copy(rowi[b][:, :], dst_i[:, bass.ds(t, 1)]).then_inc(s_cpd, 1)
                    g.tensor_copy(rows[b][:, :], xn[:, bass.ds(t, 1), :].rearrange("p o c -> p (o c)")).then_inc(s_cpd, 1)
                    g.wait_ge(s_cpd, t * 2 + 2)
                    g.sem_inc(s_go, 1)
                    g.indirect_dma_start(out=buf_dram, out_offset=bass.IndirectOffsetOnAxis(ap=rowi[b][:, 0:1], axis=0),
                                         in_=rows[b][:, :], in_offset=None, bounds_check=E_N * ROOM - 1, oob_is_err=False).then_inc(s_sc[b], 16)
                for t in range(2):
                    scatter(t, t)

                def body(t, b, h_):
                    g.wait_ge(s_sc[b], h_ * 16 + 16)
                    g.sem_inc(s_go, 1)
                    scatter(t, b)
                over_tiles(g, 2, body, NT)
                for q in s_sc:
                    g.wait_ge(q, 8 * NT)


def experts(nc, buf_dram, w1, b1p, w2, b2, y_dram):
    with ExitStack() as c:
        c.callback(nc.all_engine_barrier)
        def sb(n, s, t=F32):
            return c.enter_context(nc.sbuf_tensor("ex_" + n, s, t))

        def sem(n):
            return c.enter_context(a_semaphore(nc, "ex_" + n))
        KC, FC, TT = C // P, HID // P, -(-ROOM // P)
        LAST = CAP - (TT - 1) * P
        ident = sb("ident", [P, P]); b1s = sb("b1", [P, E_N, FC]); b1c = sb("b1c", [P, FC]); b2s = sb("b2", [P, E_N, C])
        w1s = sb("w1", [P, 2, KC, HID]); w2s = sb("w2", [P, 2, FC, C]); xr = sb("xr", [P, 2, TT, C]); XT = sb("XT", [P, KC, TT * P])
        hT = sb("hT", [P, FC, TT * P]); yo = sb("yo", [P, 2, TT, C])
        p_x = [c.enter_context(nc.psum_tensor(f"ex_x{b}", [P, 512], F32)) for b in range(2)]
        p_h = [c.enter_context(nc.psum_tensor(f"ex_h{b}", [P, 512], F32)) for b in range(2)]
        p_y = [c.enter_context(nc.psum_tensor(f"ex_y{b}", [P, 512], F32)) for b in range(2)]
        s_b = sem("biases"); s_c = sem("ident_ready"); s_wl = [sem(f"weights{b}") for b in range(2)]; s_xl = [sem(f"rows{b}") for b in range(2)]; s_xp = sem("xT_ps"); s_xk = sem("xT_kept")
        s_hp = sem("h_ps"); s_hk = sem("h_kept"); s_yp = sem("y_ps"); s_yk = sem("y_kept"); s_ys = sem("y_stored"); s_bc = sem("b1_ready"); s_ysf = sem("rows_free")
        with nc.Block() as block:
            @block.sync
            def _(sp):
                sp.dma_start(b1s[:, :, :], b1p).then_inc(s_b, 16)
                sp.dma_start(b2s[:, :, :], bass.AP(tensor=b2.tensor, offset=0, ap=[[0, P], [C, E_N], [1, C]])).then_inc(s_b, 16)

                def body(e, b, h_):
                    sp.wait_ge(s_yp, e * TT + TT)
                    sp.dma_start(xr[:, b, 0:TT - 1, :], buf_dram[bass.ds(e * ROOM, (TT - 1) * P), :].rearrange("(t p) c -> p t c", p=P)).then_inc(s_xl[b], 16)
                    sp.dma_start(xr[0:LAST, b, TT - 1, :], buf_dram[bass.ds(e * ROOM + (TT - 1) * P, LAST), :]).then_inc(s_xl[b], 16)
                    sp.dma_start(w1s[:, b], w1[bass.ds(e, 1), :, :].rearrange("o (k p) f -> p (o k) f", p=P)).then_inc(s_wl[b], 16)
                    sp.dma_start(w2s[:, b], w2[bass.ds(e, 1), :, :].rearrange("o (k p) f -> p (o k) f", p=P)).then_inc(s_wl[b], 16)
                over_tiles(sp, 0, body, E_N)

            @block.gpsimd
            def _(g):
                g.memset(ident[:, :], 0.0).then_inc(s_c, 1)
                g.wait_ge(s_c, 1)
                g.affine_select(out=ident[:, :], in_=ident[:, :], compare_op=ALU.not_equal, fill=1.0, base=0,
                                pattern=[[-1, P]], channel_multiplier=1).then_inc(s_c, 1)
                g.sem_inc(s_ysf, 2)

                def body(e, b, h_):
                    g.wait_ge(s_yk, e * TT + (TT + 2))
                    g.sem_inc(s_c, 1)
                    g.dma_start(y_dram[bass.ds(e * ROOM, (TT - 1) * P), :].rearrange("(t p) c -> p t c", p=P), yo[:, b, 0:TT - 1, :]).then_inc(s_ys, 16)
                    g.dma_start(y_dram[bass.ds(e * ROOM + (TT - 1) * P, LAST), :], yo[0:LAST, b, TT - 1, :]).then_inc(s_ys, 16)
                    g.wait_ge(s_ys, e * 32 + 32)
                    g.sem_inc(s_ysf, 1)
                over_tiles(g, 0, body, E_N)
                g.wait_ge(s_ys, 32 * E_N)

            halves = [(0, 512), (512, CAP)]

            @block.tensor
            def _(pe):
                pe.wait_ge(s_c, 2)
                pe.sem_inc(s_yp, 2 * TT)

                def body(e, b, h_):
                    pe.wait_ge(s_xl[b], h_ * 32 + 32)
                    for k in range(KC):
                        for q in range(2):
                            n = 2 * k + q
                            pe.wait_ge(s_xk, e * 4 + (n + 1))
                            for j in range(4):
                                m = P if q * 4 + j < TT - 1 else LAST
                                last = pe.matmul(p_x[n % 2][:, j * P:j * P + m], xr[0:m, b, q * 4 + j, k * P:(k + 1) * P], ident[0:m, 0:m], start=True, stop=True)
                            last.then_inc(s_xp, 1)
                    pe.wait_ge(s_wl[b], h_ * 32 + 32)
                    pe.wait_ge(s_xk, e * 4 + 6)
                    for f in range(FC):
                        for q, (lo, hi) in enumerate(halves):
                            n = 2 * f + q
                            pe.wait_ge(s_hk, e * 16 + (n + 1))
                            for k in range(KC):
                                last = pe.matmul(p_h[n % 2][:, 0:hi - lo], w1s[:, b, k, f * P:(f + 1) * P], XT[:, k, lo:hi], start=(k == 0), stop=(k == KC - 1))
                            last.then_inc(s_hp, 1)
                    pe.wait_ge(s_hk, e * 16 + 18)
                    for j in range(TT):
                        m = P if j < TT - 1 else LAST
                        pe.wait_ge(s_yk, e * TT + (j + 1))
                        for f in range(FC):
                            last = pe.matmul(p_y[j % 2][0:m, 0:C], hT[:, f, j * P:j * P + m], w2s[:, b, f, :], start=(f == 0), stop=(f == FC - 1))
                        last.then_inc(s_yp, 1)
                over_tiles(pe, 0, body, E_N)

            @block.scalar
            def _(a):
                a.wait_ge(s_b, 32)
                a.sem_inc(s_hk, 2)

                def body(e, b, h_):
                    a.wait_ge(s_hk, e * 16 + 2)
                    a.activation(b1c[:, :], b1s[:, bass.ds(e, 1), :].rearrange("p o f -> p (o f)"), ACT.Copy).then_inc(s_bc, 1)
                    a.wait_ge(s_bc, e + 1)
                    a.wait_ge(s_yp, e * TT + 2 * TT)
                    for f in range(FC):
                        for q, (lo, hi) in enumerate(halves):
                            a.wait_ge(s_hp, e * 16 + (2 * f + q + 1))
                            a.activation(hT[:, f, lo:hi], p_h[q][:, 0:hi - lo], ACT.Relu, bias=b1c[:, f:f + 1]).then_inc(s_hk, 1)
                over_tiles(a, 0, body, E_N)

            @block.vector
            def _(v):
                v.wait_ge(s_b, 32)
                v.engine_nop().then_inc(s_xk, 2)
                v.engine_nop().then_inc(s_yk, 2)

                def body(e, b, h_):
                    for k in range(KC):
                        for q in range(2):
                            n = 2 * k + q
                            v.wait_ge(s_xp, e * 4 + (n + 1))
                            v.tensor_copy(XT[:, k, halves[q][0]:halves[q][1]], p_x[n % 2][:, 0:halves[q][1] - halves[q][0]]).then_inc(s_xk, 1)
                    for j in range(TT):
                        m = P if j < TT - 1 else LAST
                        v.wait_ge(s_yp, e * TT + (j + 1 + 2 * TT))
                        if j == 0:
                            v.wait_ge(s_ysf, e + 1)
                        v.tensor_tensor(yo[0:m, b, j, :], p_y[j % 2][0:m, 0:C], b2s[0:m, bass.ds(e, 1), :].rearrange("p o c -> p (o c)"), ALU.add).then_inc(s_yk, 1)
                over_tiles(v, 0, body, E_N)


def combine(nc, y_dram, slot_i, coef, x1, out_dram):
    with ExitStack() as c:
        c.callback(nc.all_engine_barrier)
        def sb(n, s, t=F32):
            return c.enter_context(nc.sbuf_tensor("co_" + n, s, t))

        def sem(n):
            return c.enter_context(a_semaphore(nc, "co_" + n))
        rowi = [sb(f"rowi{b}", [T, 1], I32) for b in range(2)]
        y = [sb(f"y{b}", [T, C]) for b in range(2)]
        fine = sb("fine", [T, C], I32); up = sb("up", [T, C]); under = sb("under", [T, C]); down = sb("down", [T, C])
        o = [sb(f"o{b}", [T, C]) for b in range(2)]
        s_r = sem("rows_known"); s_g = [sem(f"gathered{b}") for b in range(2)]; s_dv = sem("dve"); s_o = sem("out_ready"); s_st = [sem(f"stored{b}") for b in range(2)]; s_go = sem("goes_on"); s_vgo = sem("dve_goes_on")
        with nc.Block() as block:
            @block.gpsimd
            def _(g):
                g.sem_inc(s_o, 2)

                def body(t, b, h_):
                    g.wait_ge(s_o, t + 1)
                    g.sem_inc(s_go, 1)
                    g.tensor_copy(rowi[b][:, :], slot_i[:, bass.ds(t, 1)]).then_inc(s_r, 1)
                    g.wait_ge(s_r, t + 1)
                    g.sem_inc(s_go, 1)
                    g.indirect_dma_start(out=y[b][:, :], out_offset=None, in_=y_dram,
                                         in_offset=bass.IndirectOffsetOnAxis(ap=rowi[b][:, 0:1], axis=0)).then_inc(s_g[b], 16)
                over_tiles(g, 0, body, NT)

            @block.vector
            def _(v):
                def body(t, b, h_):
                    ch = Chain(v, s_dv, t * 5)
                    v.wait_ge(s_g[b], h_ * 16 + 16)
                    ch.link(v.tensor_scalar(y[b][:, :], y[b][:, :], coef[:, bass.ds(t, 1)], None, ALU.mult))
                    v.tensor_scalar(up[:, :], y[b][:, :], F_MAX, 10000.0, ALU.is_gt, ALU.mult)
                    ch.link(v.tensor_scalar(under[:, :], y[b][:, :], F_MAX, None, ALU.is_le))
                    v.scalar_tensor_tensor(fine[:, :], y[b][:, :], -F_MAX, under[:, :], ALU.is_ge, ALU.mult)
                    ch.link(v.tensor_scalar(down[:, :], y[b][:, :], -F_MAX, -10000.0, ALU.is_lt, ALU.mult))
                    ch.link(v.tensor_tensor(up[:, :], up[:, :], down[:, :], ALU.add))
                    v.sem_inc(s_vgo, 1)
                    ch.link(v.copy_predicated(up[:, :], fine[:, :], y[b][:, :]))
                    v.wait_ge(s_st[b], h_ * 16 + 16)
                    v.tensor_tensor(o[b][:, :], up[:, :], x1[:, bass.ds(t, 1), :].rearrange("p o c -> p (o c)"), ALU.add).then_inc(s_o, 1)
                over_tiles(v, 0, body, NT)

            @block.sync
            def _(sp):
                for q in s_st:
                    sp.sem_inc(q, 16)

                def body(t, b, h_):
                    sp.wait_ge(s_o, t + 3)
                    sp.dma_start(out_dram[bass.ds(t * T, T), :], o[b][:, :]).then_inc(s_st[b], 16)
                over_tiles(sp, 0, body, NT)
                for q in s_st:
                    sp.wait_ge(q, 16 + 8 * NT)


def gps_layer(nc, x, src, dst, edge_weight, wqkvT, bqkv, wprojT, bproj, temperature, gate_w, gate_b, w1, b1p, w2, b2, out):
    def scratch(n, s):
        return nc.dram_tensor(n, s, F32, kind="Internal").ap()
    mT = scratch("rotationT", (C, C)); xT = scratch("xT_tiles", (NT, P, 2 * T)); mom = scratch("moments", (H, VW, FEAT))
    buf = scratch("expert_rows", (E_N * ROOM, C)); y = scratch("expert_out", (E_N * ROOM, C))
    with ExitStack() as ctx:
        ctx.callback(nc.all_engine_barrier)
        build_gnn(nc, ctx, src, dst, edge_weight, mT)
    with nc.sbuf_tensor("xn", [T, NT, C], F32) as xn:
        layer_norm(nc, "l1_", None, xn, x, None)
        transposed_tiles(nc, "t1_", xn, xT)
    moments(nc, xT, wqkvT, bqkv, mom)
    with ExitStack() as c:
        def sb(n, s, t=F32):
            return c.enter_context(nc.sbuf_tensor(n, s, t))
        x1 = sb("x1", [T, NT, C]); slot_i = sb("slot_i", [T, NT], I32); coef = sb("coef", [T, NT])
        attend(nc, xT, wqkvT, bqkv, temperature, wprojT, bproj, mom, mT, x, x1)
        with nc.sbuf_tensor("xn2", [T, NT, C], F32) as xn2:
            layer_norm(nc, "l2_", x1, xn2, None, None)
            transposed_tiles(nc, "t2_", xn2, xT)
            route(nc, xT, gate_w, gate_b, xn2, buf, slot_i, coef)
        experts(nc, buf, w1, b1p, w2, b2, y)
        combine(nc, y, slot_i, coef, x1, out)



def kernel(**inputs):
    import numpy as _np
    import concourse.bacc as _bacc
    from concourse import mybir as _mybir
    from concourse.bass_utils import run_bass_kernel_spmd as _run

    laid = {
        "x": inputs["x"], "src": inputs["src"], "dst": inputs["dst"], "edge_weight": inputs["edge_weight"],
        "wqkvT": inputs["L0_mix_Wqkv"].T, "bqkv": inputs["L0_mix_bqkv"],
        "wprojT": inputs["L0_mix_Wproj"].T, "bproj": inputs["L0_mix_bproj"],
        "temperature": inputs["L0_mix_temperature"].reshape(-1),
        "gate_w": inputs["L0_ffn_gate_w"], "gate_b": inputs["L0_ffn_gate_b"], "w1": inputs["L0_ffn_w1"],
        "b1p": inputs["L0_ffn_b1"].reshape(8, 8, 128).transpose(2, 0, 1),
        "w2": inputs["L0_ffn_w2"], "b2": inputs["L0_ffn_b2"],
    }
    nc = _bacc.Bacc("TRN2", target_bir_lowering=False, num_devices=1)
    arrays, args = {}, {}
    for name, value in laid.items():
        a = _np.ascontiguousarray(value)
        arrays[f"in_{name}"] = a
        args[name] = nc.dram_tensor(f"in_{name}", a.shape, _mybir.dt.from_np(a.dtype), kind="ExternalInput").ap()
    args["out"] = nc.dram_tensor("out_0_dram", (6250, 256), F32, kind="ExternalOutput").ap()
    gps_layer(nc, **args)
    r = _run(nc, [arrays], core_ids=[0])
    return r.results[0]["out_0_dram"]
```

```python
import math
from contextlib import ExitStack, contextmanager
import concourse.bass as bass
from concourse import mybir

F32 = mybir.dt.float32
I32 = mybir.dt.int32
ALU = mybir.AluOpType
ACT = mybir.ActivationFunctionType
AX = mybir.AxisListType

P = 128
D = 256
SEG = 125
NPAR = 8
Z, QO, QL, FS, FO, CO, SO, D1 = range(NPAR)
LEVELS = 7

TWO_PI_A = 6.28125
TWO_PI_B = float(2 * math.pi - 6.28125) and 0.0019350051879882812
TWO_PI_C = 2 * math.pi - TWO_PI_A - TWO_PI_B
ROUND = 12582912.0
PI_IN = 3.1415925


@contextmanager
def a_semaphore(nc, name):
    held = nc.alloc_semaphore(name)
    yield held
    nc.clear_and_free_semaphores([held])


class Writes:

    def __init__(self, nc, ctx, steps):
        self.L = steps // SEG
        self.W = 2 * self.L
        self.NCH = -(-SEG * self.W // (P * (P - 1)))
        self.NB = self.NCH * P
        self.NPK = -(-(self.NB * (P - 1) + P) // P) * P
        self.segments = nc.dram_tensor("segments", (2, SEG, self.W), I32, kind="Internal").ap()
        self.packed = nc.dram_tensor("packed", (2, self.NPK), I32, kind="Internal").ap()
        self.nrun = ctx.enter_context(nc.sbuf_tensor("nrun", [1, 1], I32))
        self.ident = ctx.enter_context(nc.sbuf_tensor("ident", [P, P], F32))
        self.tot = ctx.enter_context(nc.sbuf_tensor("tot", [P, 1], F32))
        self.ones = ctx.enter_context(nc.sbuf_tensor("ones", [P, P], F32))
        self.base_i = ctx.enter_context(nc.sbuf_tensor("base_i", [1, SEG + 1], I32))
        self.s_packed = ctx.enter_context(a_semaphore(nc, "segment_packed"))
        self.s_order = ctx.enter_context(a_semaphore(nc, "segments_in_order"))

    def pack(self, sp, p):
        sp.wait_ge(self.s_packed, p * 16 + 16)
        sp.sem_inc(self.s_order, 1)
        at = sp.value_load(self.base_i[0:1, bass.ds(p, 1)], min_val=0, max_val=(SEG - 1) * self.W)
        sp.dma_start(self.packed[:, bass.ds(at + 1, self.W)],
                     self.segments[:, bass.ds(p, 1), :].rearrange("a o w -> a (o w)")).then_inc(self.s_packed, 16)


def write_segments(nc, ctx, wr, src, dst, ew):
    L, W, NPK, sc, pk = wr.L, wr.W, wr.NPK, wr.segments, wr.packed
    nrun, ident, tot, ones, base_i = wr.nrun, wr.ident, wr.tot, wr.ones, wr.base_i
    BITS = max(1, (W - 1).bit_length())
    assert BITS <= 12 and SEG * L == src.shape[0]

    def sem(n):
        return ctx.enter_context(a_semaphore(nc, n))

    with ExitStack() as c:
        def sb(n, s, t=F32):
            return c.enter_context(nc.sbuf_tensor(n, s, t))
        src_i = sb("src_i", [SEG, L], I32)
        dst_i = sb("dst_i", [SEG, L], I32)
        th = sb("th", [SEG, L])
        fi = sb("fi", [SEG, L]); fj = sb("fj", [SEG, L])
        va = sb("va", [SEG, L]); vb = sb("vb", [SEG, L]); pr = sb("pr", [SEG, L]); tmp = sb("tmp", [SEG, L])
        vw = sb("vw", [SEG, W]); kf = sb("kf", [SEG, W]); inc = sb("inc", [SEG, W]); slot = sb("slot", [SEG, W])
        ki = sb("ki", [SEG, W], I32); thw = sb("thw", [SEG, W], I32); bit = sb("bit", [SEG, W], I32)
        cleared = sb("cleared", [SEG, W], I32); zi = sb("zi", [P, max(W, NPK // P)], I32)
        tri = sb("tri", [SEG, SEG + 1])
        base_ps = c.enter_context(nc.psum_tensor("base_ps", [P, 512], F32))
        ld = sem("step_loads"); dv = sem("prep_dve"); tr = sem("tri_ready"); bs = sem("base_ps_ready")
        bi = sem("base_ready"); cz = sem("zeros_ready"); comp = sem("compressed"); so = sem("seg_stored"); pkd = sem("packed_zeroed")
        po = sem("pool_consts"); ths = sem("theta_copied"); counted = sem("counted")
        with nc.Block() as block:
            @block.sync
            def _(sp):
                sp.dma_start(src_i[:, :], src.rearrange("(p l) -> p l", l=L)).then_inc(ld, 16)
                sp.dma_start(dst_i[:, :], dst.rearrange("(p l) -> p l", l=L)).then_inc(ld, 16)
                sp.dma_start(th[:, :], ew.rearrange("(p l) -> p l", l=L)).then_inc(ld, 16)
                sp.wait_ge(cz, 1)
                for a in range(2):
                    sp.dma_start(pk[a].rearrange("(p l) -> p l", p=P), zi[:, 0:NPK // P]).then_inc(pkd, 16)
                sp.wait_ge(pkd, 32)
                sp.wait_ge(comp, 1)
                sp.dma_start(sc[0], ki[:, :]).then_inc(so, 16)
                sp.dma_start(sc[1], thw[:, :]).then_inc(so, 16)
                sp.wait_ge(so, 32)
                sp.sem_inc(wr.s_packed, 16)

            @block.gpsimd
            def _(g):
                g.memset(zi[:, :], 0).then_inc(cz, 1)
                g.memset(ones[:, :], 1.0).then_inc(po, 1)
                g.memset(ident[:, :], 0.0).then_inc(po, 1)
                g.memset(tri[:, :], 1.0).then_inc(po, 1)
                g.iota(slot[:, :], pattern=[[1, W]], base=1, channel_multiplier=0, allow_small_or_imprecise_dtypes=True).then_inc(po, 1)
                g.wait_ge(po, 4)
                g.affine_select(out=ident[:, :], in_=ident[:, :], compare_op=ALU.not_equal, fill=1.0,
                                base=0, pattern=[[-1, P]], channel_multiplier=1).then_inc(po, 1)
                g.affine_select(out=tri[:, :], in_=tri[:, :], compare_op=ALU.is_gt, fill=0.0,
                                base=0, pattern=[[1, SEG + 1]], channel_multiplier=-1).then_inc(tr, 1)

            @block.scalar
            def _(a):
                a.wait_ge(ld, 48)
                v = thw[:, :].bitcast(F32).rearrange("p (l o) -> p l o", o=2)
                a.activation(v[:, :, 0], th[:, :], ACT.Copy).then_inc(ths, 1)
                a.activation(v[:, :, 1], th[:, :], ACT.Copy).then_inc(ths, 1)

            @block.vector
            def _(v):
                n = [0]

                def link(ins):
                    n[0] += 1
                    ins.then_inc(dv, 1)
                    v.wait_ge(dv, n[0])
                v.wait_ge(ld, 48)
                vw2 = vw[:, :].rearrange("p (l o) -> p l o", o=2)
                kf2 = kf[:, :].rearrange("p (l o) -> p l o", o=2)
                v.tensor_copy(fi[:, :], src_i[:, :])
                link(v.tensor_copy(fj[:, :], dst_i[:, :]))
                v.tensor_scalar(va[:, :], fi[:, :], float(D), None, ALU.is_lt)
                link(v.tensor_scalar(vb[:, :], fj[:, :], float(D), None, ALU.is_lt))
                v.tensor_scalar(fi[:, :], fi[:, :], float(D - 1), None, ALU.min)
                link(v.tensor_scalar(fj[:, :], fj[:, :], float(D - 1), None, ALU.min))
                link(v.tensor_tensor(tmp[:, :], fi[:, :], fj[:, :], ALU.is_equal))
                link(v.tensor_tensor(tmp[:, :], tmp[:, :], vb[:, :], ALU.mult))
                link(v.tensor_scalar(tmp[:, :], tmp[:, :], -1.0, 1.0, ALU.mult, ALU.add))
                link(v.tensor_tensor(va[:, :], va[:, :], tmp[:, :], ALU.mult))
                v.tensor_copy(vw2[:, :, 0], va[:, :])
                v.tensor_copy(vw2[:, :, 1], vb[:, :])
                link(v.tensor_tensor(pr[:, :], va[:, :], vb[:, :], ALU.mult))
                v.scalar_tensor_tensor(kf2[:, :, 0], fj[:, :], float(D), fi[:, :], ALU.mult, ALU.add)
                v.tensor_scalar(pr[:, :], pr[:, :], 65536.0, 131072.0, ALU.mult, ALU.add)
                link(v.scalar_tensor_tensor(tmp[:, :], fi[:, :], float(D), fj[:, :], ALU.mult, ALU.add))
                link(v.tensor_tensor(kf2[:, :, 1], tmp[:, :], pr[:, :], ALU.add))
                v.wait_ge(cz, 1)
                link(v.tensor_tensor_scan(inc[:, :], vw[:, :], zi[0:SEG, 0:W].bitcast(F32), 0.0, ALU.add, ALU.add))
                v.engine_nop().then_inc(counted, 1)
                v.wait_ge(po, 4)
                link(v.tensor_tensor(slot[:, :], slot[:, :], inc[:, :], ALU.subtract))
                link(v.tensor_tensor(slot[:, :], slot[:, :], vw[:, :], ALU.mult))
                v.tensor_copy(ki[:, :], kf[:, :])
                link(v.tensor_copy(bit[:, :], slot[:, :]))
                link(v.tensor_scalar(bit[:, :], bit[:, :], 18, None, ALU.logical_shift_left))
                link(v.tensor_tensor(ki[:, :], ki[:, :], bit[:, :], ALU.bitwise_or))
                v.wait_ge(ths, 2)
                for b in range(BITS):
                    s = 1 << b
                    v.tensor_scalar(bit[:, :], ki[:, :], 1 << (18 + b), None, ALU.bitwise_and)
                    link(v.tensor_scalar(cleared[:, :], ki[:, :], ~(1 << (18 + b)), None, ALU.bitwise_and))
                    link(v.copy_predicated(ki[:, :], bit[:, :], zi[0:SEG, 0:W]))
                    v.copy_predicated(ki[:, 0:W - s], bit[:, s:W], cleared[:, s:W])
                    link(v.copy_predicated(thw[:, 0:W - s], bit[:, s:W], thw[:, s:W]))
                v.engine_nop().then_inc(comp, 1)
                v.wait_ge(bs, 1)
                v.tensor_copy(base_i[:, :], base_ps[0:1, 0:SEG + 1])
                link(v.tensor_copy(tot[:, :], base_ps[:, 256:257]))
                v.engine_nop().then_inc(bi, 1)
                link(v.tensor_scalar(nrun[:, :], base_ps[0:1, SEG:SEG + 1], 1.0 / (2 * (P - 1)), 1.0, ALU.mult, ALU.add))

            @block.tensor
            def _(pe):
                pe.wait_ge(counted, 1)
                pe.wait_ge(tr, 1)
                pe.wait_ge(po, 1)
                pe.matmul(base_ps[0:1, 0:SEG + 1], inc[:, W - 1:W], tri[:, :], start=True, stop=True)
                pe.matmul(base_ps[:, 256:257], ones[0:SEG, :], inc[:, W - 1:W], start=True, stop=True).then_inc(bs, 1)


def rotation_matrix(nc, ctx, wr, mT_out):
    B = P - 1
    NCH, NB, NPK, pk = wr.NCH, wr.NB, wr.NPK, wr.packed
    nrun, ident, tot, ones = wr.nrun, wr.ident, wr.tot, wr.ones

    def sem(n):
        return ctx.enter_context(a_semaphore(nc, n))

    keep_ctx = ExitStack()
    par = keep_ctx.enter_context(nc.sbuf_tensor("par", [P, NB + 2, NPAR], F32))
    with ExitStack() as c0:
      kt = c0.enter_context(nc.sbuf_tensor("kt", [P, NB], I32))
      tt = c0.enter_context(nc.sbuf_tensor("tt", [P, NB], F32))
      with ExitStack() as c:
          def sb(n, s, t=F32):
              return c.enter_context(nc.sbuf_tensor(n, s, t))
          E = P + 1
          kb = sb("kb", [P, NCH, E], I32)
          tb = sb("tb", [P, NCH, E])
          kbf = sb("kbf", [P, NCH, E]); posn = sb("posn", [P, NCH, E]); inr = sb("inr", [P, NCH, E]); pfl = sb("pfl", [P, NCH, 2])
          psk = [c.enter_context(nc.psum_tensor(f"psk{i}", [P, 512], F32)) for i in range(2)]
          pst = [c.enter_context(nc.psum_tensor(f"pst{i}", [P, 512], F32)) for i in range(2)]
          ld = sem("packed_loads"); kr = sem("keys_float"); tp = sem("transposed"); ev = sem("columns_kept")
          dv = sem("cols_dve"); io = sem("cols_iota")

          def overlapped(a):
              return bass.AP(tensor=pk.tensor, offset=a * NPK, ap=[[B, P], [P * B, NCH], [1, E]])

          with nc.Block() as block:
              @block.sync
              def _(sp):
                  sp.wait_ge(wr.s_packed, SEG * 16 + 16)
                  sp.dma_start(kb[:, :, :], overlapped(0)).then_inc(ld, 16)
                  sp.dma_start(tb[:, :, :].bitcast(I32), overlapped(1)).then_inc(ld, 16)

              @block.gpsimd
              def _(g):
                  g.iota(posn[:, :, :], pattern=[[P * B, NCH], [1, E]], base=-1, channel_multiplier=B, allow_small_or_imprecise_dtypes=True).then_inc(io, 1)

              @block.tensor
              def _(pe):
                  pe.wait_ge(kr, 1)
                  pe.wait_ge(ld, 32)
                  for q in range(0, NCH, 4):
                      m = min(4, NCH - q)
                      b = (q // 4) % 2
                      if q >= 8:
                          pe.wait_ge(ev, 2 * (q // 4) - 2)
                      for j in range(m):
                          pe.transpose(psk[b][:, j * P:(j + 1) * P], kbf[:, q + j, 0:P], ident[:, :])
                          last = pe.transpose(pst[b][:, j * P:(j + 1) * P], tb[:, q + j, 0:P], ident[:, :])
                      last.then_inc(tp, 1)

              @block.vector
              def _(v):
                  n = [0]

                  def link(ins):
                      n[0] += 1
                      ins.then_inc(dv, 1)
                      v.wait_ge(dv, n[0])
                  v.wait_ge(ld, 32)
                  link(v.tensor_scalar(kb[:, :, :], kb[:, :, :], (1 << 18) - 1, None, ALU.bitwise_and))
                  link(v.tensor_copy(kbf[:, :, :], kb[:, :, :]))
                  v.wait_ge(io, 1)
                  link(v.tensor_scalar(inr[:, :, :], posn[:, :, :], tot[:, 0:1], None, ALU.is_lt))
                  link(v.tensor_tensor(kbf[:, :, :], kbf[:, :, :], inr[:, :, :], ALU.mult))
                  link(v.tensor_copy(kb[:, :, :], kbf[:, :, :]))
                  link(v.tensor_scalar(kb[:, :, :], kb[:, :, :], 1 << 16, None, ALU.bitwise_and))
                  link(v.tensor_copy(pfl[:, :, 0], kb[:, :, 1]))
                  link(v.tensor_copy(pfl[:, :, 1], kb[:, :, P]))
                  link(v.tensor_scalar(inr[:, :, :], inr[:, :, :], -262144.0, 262144.0, ALU.mult, ALU.add))
                  link(v.tensor_scalar(inr[:, :, 0], pfl[:, :, 0], -4.0, 262144.0, ALU.mult, ALU.add))
                  link(v.scalar_tensor_tensor(inr[:, :, B], pfl[:, :, 1], 4.0, inr[:, :, B], ALU.mult, ALU.add))
                  v.tensor_tensor(kbf[:, :, :], kbf[:, :, :], inr[:, :, :], ALU.add).then_inc(kr, 1)
                  for q in range(0, NCH, 4):
                      m = min(4, NCH - q)
                      b = (q // 4) % 2
                      v.wait_ge(tp, q // 4 + 1)
                      v.tensor_copy(kt[:, q * P:(q + m) * P], psk[b][:, 0:m * P]).then_inc(ev, 1)
                      v.tensor_copy(tt[:, q * P:(q + m) * P], pst[b][:, 0:m * P]).then_inc(ev, 1)
                  v.wait_ge(ev, 2 * -(-NCH // 4))
      with ExitStack() as c:
          def sb(n, s, t=F32):
              return c.enter_context(nc.sbuf_tensor(n, s, t))
          w1 = sb("w1", [P, NB]); w2 = sb("w2", [P, NB]); vl = sb("vl", [P, NB]); sgn = sb("sgn", [P, NB])
          wi = sb("wi", [P, NB], I32)
          n1 = sb("n1", [P, 1]); halfpi = sb("halfpi", [P, 1])
          dv = sem("par_dve"); io = sem("par_consts"); ang = sem("angles"); tri_s = sem("sincos")
          with nc.Block() as block:
              @block.gpsimd
              def _(g):
                  g.iota(n1[:, :], pattern=[[0, 1]], base=1, channel_multiplier=1, allow_small_or_imprecise_dtypes=True).then_inc(io, 1)
                  g.memset(halfpi[:, :], math.pi / 2).then_inc(io, 1)
                  g.memset(par[:, NB:NB + 2, :], 0.0).then_inc(io, 1)
                  g.wait_ge(io, 3)
                  g.memset(par[:, NB:NB + 2, Z:Z + 1], -1.0).then_inc(io, 1)
                  g.wait_ge(io, 4)

              @block.scalar
              def _(a):
                  a.wait_ge(io, 2)
                  a.wait_ge(ang, 1)
                  a.activation(w2[:, :], tt[:, :], ACT.Sin).then_inc(tri_s, 1)
                  a.wait_ge(ang, 2)
                  a.wait_ge(tri_s, 1)
                  a.activation(tt[:, :], sgn[:, :], ACT.Sin, bias=halfpi[:, :], scale=-1.0).then_inc(tri_s, 1)

              @block.vector
              def _(v):
                  n = [0]

                  def link(ins):
                      n[0] += 1
                      ins.then_inc(dv, 1)
                      v.wait_ge(dv, n[0])
                  v.wait_ge(io, 2)
                  PA = par[:, 0:NB, :]
                  link(v.tensor_scalar(wi[:, :], kt[:, :], 18, None, ALU.logical_shift_right))
                  link(v.tensor_copy(vl[:, :], wi[:, :]))
                  link(v.tensor_scalar(vl[:, :], vl[:, :], -1.0, 1.0, ALU.mult, ALU.add))
                  link(v.tensor_scalar(w1[:, :], tt[:, :], 1.0 / (2 * math.pi), ROUND, ALU.mult, ALU.add))
                  link(v.tensor_scalar(w1[:, :], w1[:, :], ROUND, None, ALU.subtract))
                  for part in (TWO_PI_A, TWO_PI_B, TWO_PI_C):
                      link(v.scalar_tensor_tensor(tt[:, :], w1[:, :], -part, tt[:, :], ALU.mult, ALU.add))
                  link(v.tensor_scalar(tt[:, :], tt[:, :], PI_IN, -PI_IN, ALU.min, ALU.max))
                  v.engine_nop().then_inc(ang, 1)
                  v.wait_ge(ang, 1)
                  link(v.tensor_scalar(sgn[:, :], tt[:, :], -1.0, None, ALU.mult))
                  link(v.tensor_tensor(sgn[:, :], sgn[:, :], tt[:, :], ALU.max))
                  v.engine_nop().then_inc(ang, 1)
                  v.wait_ge(tri_s, 2)
                  v.tensor_tensor(PA[:, :, CO], tt[:, :], vl[:, :], ALU.mult)
                  link(v.tensor_tensor(w2[:, :], w2[:, :], vl[:, :], ALU.mult))
                  link(v.tensor_scalar(wi[:, :], kt[:, :], 17, 1, ALU.logical_shift_right, ALU.bitwise_and))
                  link(v.tensor_copy(sgn[:, :], wi[:, :]))
                  link(v.tensor_scalar(sgn[:, :], sgn[:, :], 2.0, -1.0, ALU.mult, ALU.add))
                  v.tensor_tensor(PA[:, :, SO], w2[:, :], sgn[:, :], ALU.mult)
                  link(v.tensor_scalar(wi[:, :], kt[:, :], D - 1, None, ALU.bitwise_and))
                  link(v.tensor_copy(w1[:, :], wi[:, :]))
                  v.tensor_scalar(PA[:, :, FS], w1[:, :], float(D), None, ALU.mult)
                  v.tensor_scalar(PA[:, :, QL], w1[:, :], float(D), float(D - 1), ALU.mult, ALU.add)
                  v.scalar_tensor_tensor(PA[:, :, D1], w1[:, :], 1.0, vl[:, :], ALU.add, ALU.mult)
                  link(v.tensor_scalar(tt[:, :], w1[:, :], float(D), n1[:, 0:1], ALU.mult, ALU.add))
                  link(v.scalar_tensor_tensor(tt[:, :], tt[:, :], 1.0, vl[:, :], ALU.add, ALU.mult))
                  v.tensor_scalar(PA[:, :, Z], tt[:, :], -1.0, None, ALU.add)
                  link(v.tensor_scalar(wi[:, :], kt[:, :], 8, D - 1, ALU.logical_shift_right, ALU.bitwise_and))
                  link(v.tensor_copy(w1[:, :], wi[:, :]))
                  v.tensor_scalar(PA[:, :, FO], w1[:, :], float(D), None, ALU.mult)
                  link(v.tensor_scalar(w2[:, :], w1[:, :], float(D), n1[:, 0:1], ALU.mult, ALU.add))
                  link(v.tensor_scalar(wi[:, :], kt[:, :], 16, 1, ALU.logical_shift_right, ALU.bitwise_and))
                  link(v.tensor_copy(w1[:, :], wi[:, :]))
                  link(v.tensor_tensor(PA[:, :, QO], w2[:, :], w1[:, :], ALU.subtract))


    with ExitStack() as c:
        def sb(n, s, t=F32):
            return c.enter_context(nc.sbuf_tensor(n, s, t))

        def ps(n):
            return c.enter_context(nc.psum_tensor(n, [P, 512], F32))
        X2 = range(2)
        parn = sb("parn", [P, 2, NPAR])
        nxt = sb("nxt", [P, 2, 5]); cur = sb("cur", [P, 2, 5])
        zd = sb("zd", [P, 2, P]); zx = sb("zx", [P, 2, P])
        q3 = sb("q3", [P, 3, P]); pred = sb("pred", [P, 3])
        e1 = sb("e1", [P, P]); e2 = sb("e2", [P, P])
        rowk = sb("rowk", [P, D]); row1 = sb("row1", [P, D])
        NN = [sb(f"N{x}", [P, P]) for x in X2]
        NI = [sb(f"NI{x}", [P, P]) for x in X2]
        NT = [sb(f"NT{x}", [P, P]) for x in X2]
        PQ = [[sb(f"PQ{x}{h}", [P, 2, P]) for h in range(2)] for x in X2]
        ST = [sb(f"ST{x}", [P, P]) for x in X2]
        RR = [sb(f"R{x}", [P, D]) for x in X2]
        r1 = sb("r1", [P, D]); r2 = sb("r2", [P, D])
        FT = [sb(f"FT{x}", [P, D]) for x in X2]
        WT = sb("WT", [P, 2, 2, P])
        M = sb("M", [P, 2, D]); V = sb("V", [P, D]); kp = sb("kp", [P, 2, 2])
        pq = [ps(f"pq{x}") for x in X2]
        pst = [ps(f"pss{x}") for x in X2]
        pz = ps("pz"); pv = ps("pv"); pd = ps("pd"); pw = ps("pw")
        s_nt = sem("nt_in_psum"); s_sp = sem("st_in_psum"); s_lv = sem("level_in_psum"); s_zr = sem("zrow_in_psum"); s_v = sem("v_in_psum")
        s_dl = sem("delta_in_psum"); s_cnt = sem("writers_in_psum"); s_wt = sem("wt_in_psum")
        s_q = sem("q_kept"); s_st = sem("st_kept"); s_zx = sem("zrow_kept"); s_wts = sem("wt_kept")
        s_p = [sem(f"pq_kept{x}") for x in X2]; s_vs = sem("v_kept"); s_m = sem("m_updated"); s_keep = sem("keep_ready")
        s_setup = sem("n_ready"); s_dc = sem("loop_dve"); s_par = sem("par_loaded"); s_cur = sem("cur_ready")
        s_zd = sem("zdiag_ready"); s_R = sem("r_ready"); s_FT = sem("ft_ready"); s_gc = sem("loop_pool")
        s_c = sem("loop_consts"); s_go = sem("pool_goes_on"); s_fin = sem("mt_in_psum"); s_mo = sem("mt_kept"); s_out = sem("mt_stored")
        mt = sb("mt", [P, 2, D])
        with nc.Block() as block:
            @block.gpsimd
            def _(g):
                g.iota(rowk[:, :], pattern=[[D, D]], base=0, channel_multiplier=0, allow_small_or_imprecise_dtypes=True).then_inc(s_c, 1)
                g.iota(row1[:, :], pattern=[[1, D]], base=1, channel_multiplier=0, allow_small_or_imprecise_dtypes=True).then_inc(s_c, 1)
                g.memset(M[:, :, :], 0.0).then_inc(s_c, 1)
                g.wait_ge(s_c, 3)
                for k in range(2):
                    g.tensor_copy(M[:, k, k * P:(k + 1) * P], ident[:, :]).then_inc(s_c, 1)
                g.wait_ge(s_c, 5)
                g.memset(kp[:, :, :], 1.0).then_inc(s_keep, 1)
                g.memset(WT[:, :, :, :], 0.0).then_inc(s_wts, 1)
                for x in X2:
                    g.memset(FT[x][:, :], 0.0).then_inc(s_FT, 1)
                g.engine_nop().then_inc(s_m, 1)
                g.tensor_copy(parn[:, :, :], par[:, 0:2, :]).then_inc(s_par, 1)
                g.wait_ge(s_par, 1)
                for x in X2:
                    g.tensor_scalar(zd[:, x, :], ident[:, :], parn[:, x, Z:Z + 1], None, ALU.mult).then_inc(s_zd, 1)
                cnt = g.value_load(nrun[0:1, 0:1], min_val=1, max_val=NB // 2)
                with g.Fori(0, cnt) as i:
                    g.wait_ge(s_setup, i * 2 + 2); g.sem_inc(s_go, 1)
                    g.tensor_copy(cur[:, :, :], nxt[:, :, :]).then_inc(s_cur, 1)
                    g.tensor_copy(parn[:, :, :], par[:, bass.ds(i * 2 + 2, 2), :]).then_inc(s_par, 1)
                    g.wait_ge(s_cur, i + 1)
                    g.wait_ge(s_par, i + 2)
                    g.wait_ge(s_zr, i + 1); g.sem_inc(s_go, 1)
                    for x in X2:
                        g.tensor_scalar(zd[:, x, :], ident[:, :], parn[:, x, Z:Z + 1], None, ALU.mult).then_inc(s_zd, 1)
                    g.wait_ge(s_wts, i + 1); g.sem_inc(s_go, 1)
                    for x in X2:
                        g.tensor_scalar(r1[:, :], rowk[:, :], cur[:, x, 0:1], cur[:, x, 2:3], ALU.is_equal, ALU.mult).then_inc(s_gc, 1)
                        g.tensor_scalar(r2[:, :], rowk[:, :], cur[:, x, 1:2], cur[:, x, 3:4], ALU.is_equal, ALU.mult).then_inc(s_gc, 1)
                        g.wait_ge(s_gc, i * 4 + 2 * x + 2); g.sem_inc(s_go, 1)
                        g.tensor_tensor(RR[x][:, :], r1[:, :], r2[:, :], ALU.add).then_inc(s_R, 1)
                        g.wait_ge(s_R, i * 2 + x + 1); g.sem_inc(s_go, 1)
                    g.wait_ge(s_dl, i * 2 + 2); g.sem_inc(s_go, 1)
                    for x in X2:
                        g.tensor_scalar(FT[x][:, :], row1[:, :], cur[:, x, 4:5], None, ALU.is_equal).then_inc(s_FT, 1)
                    g.wait_ge(s_FT, i * 2 + 4); g.sem_inc(s_go, 1)

            def chain_v(pe, x, i):
                i2 = i * 2
                pe.wait_ge(s_m, i2 + (x + 1))
                if x == 0:
                    pe.wait_ge(s_keep, i + 1)
                pe.wait_ge(s_wts, i + 1)
                pe.matmul(pv[:, 0:D], WT[:, x, 0, :], M[:, 0, :], start=True, stop=False)
                pe.matmul(pv[:, 0:D], WT[:, x, 1, :], M[:, 1, :], start=False, stop=True).then_inc(s_v, 1)

            def chain_d(pe, x, i):
                i2 = i * 2
                pe.wait_ge(s_vs, i2 + (x + 1))
                pe.wait_ge(s_FT, i2 + (x + 1))
                pe.matmul(pd[:, 0:D], FT[x][:, 0:P], V[:, :], start=True, stop=True)
                pe.matmul(pd[:, D:2 * D], FT[x][:, P:D], V[:, :], start=True, stop=True).then_inc(s_dl, 1)

            @block.tensor
            def _(pe):
                def zrow(i):
                    pe.wait_ge(s_zd, i * 2 + 2)
                    pe.matmul(pz[:, 0:D], ones[:, :], zd[:, :, :].rearrange("p a b -> p (a b)"), start=True, stop=True).then_inc(s_zr, 1)
                pe.wait_ge(s_c, 5)
                zrow(0)
                cnt = pe.value_load(nrun[0:1, 0:1], min_val=1, max_val=NB // 2)
                with pe.Fori(0, cnt) as i:
                    for x in X2:
                        pe.wait_ge(s_setup, i * 2 + (x + 1))
                        pe.transpose(pq[x][:, 0:P], NN[x][:, :], ident[:, :]).then_inc(s_nt, 1)
                        pe.transpose(pst[x][:, 0:P], NI[x][:, :], ident[:, :]).then_inc(s_sp, 1)
                    for k in range(LEVELS):
                        h, g = (k % 2), ((k + 1) % 2)
                        for x in X2:
                            if k == 0:
                                pe.wait_ge(s_q, i * 2 + (x + 1))
                                pw_k, qw_k = NN[x][:, :], NT[x][:, :]
                            else:
                                pe.wait_ge(s_p[x], i * (LEVELS - 1) + k)
                                pw_k, qw_k = PQ[x][k % 2][:, 0, :], PQ[x][k % 2][:, 1, :]
                            if k < LEVELS - 1:
                                last = pe.matmul(pq[x][:, 0:P], qw_k, pw_k, start=True, stop=True)
                                if k < LEVELS - 2:
                                    last = pe.matmul(pq[x][:, P:2 * P], pw_k, qw_k, start=True, stop=True)
                                last.then_inc(s_lv, 1)
                            if k:
                                pe.wait_ge(s_st, i * 14 + (2 * (k - 1) + x + 1))
                                pe.matmul(pst[x][:, 0:P], pw_k, ST[x][:, :], start=False, stop=True, skip_group_check=True).then_inc(s_sp, 1)
                        if k == 0:
                            pe.wait_ge(s_zx, i + 1)
                            zrow(i + 1)
                            chain_v(pe, 0, i)
                        if k == 1:
                            chain_d(pe, 0, i)
                        if k == 3:
                            chain_v(pe, 1, i)
                        if k == 4:
                            chain_d(pe, 1, i)
                    for x in X2:
                        pe.wait_ge(s_st, i * 14 + (12 + x + 1))
                        pe.wait_ge(s_R, i * 2 + (x + 1))
                        for r in range(2):
                            last = pe.matmul(pw[:, x * D + r * P:x * D + (r + 1) * P], RR[x][:, r * P:(r + 1) * P], ST[x][:, :], start=True, stop=True)
                    last.then_inc(s_wt, 1)
                    pe.wait_ge(s_keep, i + 1)
                    pe.wait_ge(s_FT, i * 2 + 4)
                    for x in X2:
                        for r in range(2):
                            last = pe.matmul(pv[:, D + 2 * x + r:D + 2 * x + r + 1], FT[x][:, r * P:(r + 1) * P], ones[:, 0:1], start=True, stop=True)
                    last.then_inc(s_cnt, 1)
                for x in X2:
                    chain_v(pe, x, cnt)
                    chain_d(pe, x, cnt)
                pe.wait_ge(s_m, cnt * 2 + 3)
                for a in range(2):
                    for b in range(2):
                        last = pe.transpose(pd[:, a * D + b * P:a * D + (b + 1) * P], M[:, b, a * P:(a + 1) * P], ident[:, :])
                last.then_inc(s_fin, 1)

            @block.scalar
            def _(a):
                def v_kept(a, x, i2):
                    a.wait_ge(s_v, i2 + (x + 1))
                    a.activation(V[:, :], pv[:, 0:D], ACT.Copy).then_inc(s_vs, 1)

                def zrow_kept():
                    a.activation(zx[:, :, :].rearrange("p a b -> p (a b)"), pz[:, 0:D], ACT.Copy).then_inc(s_zx, 1)
                a.wait_ge(s_zr, 1)
                zrow_kept()
                cnt = a.value_load(nrun[0:1, 0:1], min_val=1, max_val=NB // 2)
                with a.Fori(0, cnt) as i:
                    for x in X2:
                        a.wait_ge(s_nt, i * 2 + (x + 1))
                        a.activation(NT[x][:, :], pq[x][:, 0:P], ACT.Copy).then_inc(s_q, 1)
                    for k in range(LEVELS):
                        for x in X2:
                            if k < LEVELS - 1:
                                a.wait_ge(s_lv, i * 12 + (2 * k + x + 1))
                                w = 2 if k < LEVELS - 2 else 1
                                a.activation(PQ[x][(k + 1) % 2][:, 0:w, :].rearrange("p a b -> p (a b)"), pq[x][:, 0:w * P], ACT.Copy).then_inc(s_p[x], 1)
                            a.wait_ge(s_sp, i * 14 + (2 * k + x + 1))
                            a.activation(ST[x][:, :], pst[x][:, 0:P], ACT.Copy).then_inc(s_st, 1)
                        if k == 0:
                            v_kept(a, 0, i * 2)
                        if k == 3:
                            v_kept(a, 1, i * 2)
                        if k == 1:
                            a.wait_ge(s_zr, i + 2)
                            a.wait_ge(s_setup, i * 2 + 2)
                            zrow_kept()
                    a.wait_ge(s_wt, i + 1)
                    a.wait_ge(s_v, i * 2 + 2)
                    a.activation(WT[:, :, :, :].rearrange("p x a b -> p (x a b)"), pw[:, :], ACT.Copy).then_inc(s_wts, 1)
                for x in X2:
                    v_kept(a, x, cnt * 2)

            @block.vector
            def _(v):
                def found(x, base):
                    zrow = zx[:, x, :]
                    for k, q in enumerate((Z, QO, QL)):
                        last = v.scalar_tensor_tensor(q3[:, k, :], zrow, parn[:, x, q:q + 1], zrow, ALU.is_lt, ALU.mult)
                    last.then_inc(s_dc, 1)
                    v.wait_ge(s_dc, base + (5 * x + 1))
                    v.tensor_reduce(pred[:, :], q3[:, :, :], AX.X, ALU.max).then_inc(s_dc, 1)
                    v.wait_ge(s_dc, base + (5 * x + 2))
                    v.tensor_tensor(nxt[:, x, 0:2], pred[:, 0:2], parn[:, x, FS:FO + 1], ALU.max)
                    v.tensor_copy(nxt[:, x, 2:4], parn[:, x, CO:SO + 1])
                    v.tensor_scalar(nxt[:, x, 4:5], pred[:, 2:3], parn[:, x, Z:Z + 1], parn[:, x, D1:D1 + 1], ALU.is_equal, ALU.mult).then_inc(s_dc, 1)

                def matrix(x, base):
                    zrow = zx[:, x, :]
                    v.wait_ge(s_dc, base + (5 * x + 3))
                    v.tensor_scalar(e1[:, :], zrow, nxt[:, x, 0:1], nxt[:, x, 2:3], ALU.is_equal, ALU.mult)
                    v.tensor_scalar(e2[:, :], zrow, nxt[:, x, 1:2], nxt[:, x, 3:4], ALU.is_equal, ALU.mult).then_inc(s_dc, 1)
                    v.wait_ge(s_dc, base + (5 * x + 4))
                    v.tensor_tensor(NN[x][:, :], e1[:, :], e2[:, :], ALU.add).then_inc(s_dc, 1)
                    v.wait_ge(s_dc, base + (5 * x + 5))
                    v.tensor_tensor(NI[x][:, :], NN[x][:, :], ident[:, :], ALU.add).then_inc(s_setup, 1)

                def m_update(x, i2):
                    v.wait_ge(s_dl, i2 + (x + 1))
                    for r in range(2):
                        last = v.scalar_tensor_tensor(M[:, r, :], M[:, r, :], kp[:, x, r:r + 1], pd[:, r * D:(r + 1) * D], ALU.mult, ALU.add)
                    last.then_inc(s_m, 1)

                v.wait_ge(s_c, 5)
                v.wait_ge(s_par, 1)
                v.wait_ge(s_keep, 1)
                v.wait_ge(s_zx, 1)
                for x in X2:
                    found(x, 0)
                    matrix(x, 0)
                cnt = v.value_load(nrun[0:1, 0:1], min_val=1, max_val=NB // 2)
                with v.Fori(0, cnt) as i:
                    v.wait_ge(s_lv, i * 12 + 1)
                    v.wait_ge(s_zx, i + 2)
                    v.wait_ge(s_par, i + 2)
                    v.wait_ge(s_cur, i + 1)
                    found(0, i * 10 + 10)
                    m_update(0, i * 2)
                    matrix(0, i * 10 + 10)
                    found(1, i * 10 + 10)
                    m_update(1, i * 2)
                    v.wait_ge(s_lv, i * 12 + 2)
                    matrix(1, i * 10 + 10)
                    v.wait_ge(s_cnt, i + 1)
                    v.tensor_scalar(kp[:, :, :].rearrange("p a b -> p (a b)"), pv[:, D:D + 4], -1.0, 1.0, ALU.mult, ALU.add).then_inc(s_keep, 1)
                    v.wait_ge(s_keep, i + 2)
                for x in X2:
                    m_update(x, cnt * 2)
                v.wait_ge(s_fin, 1)
                v.tensor_copy(mt[:, :, :].rearrange("p a b -> p (a b)"), pd[:, :]).then_inc(s_mo, 1)

            @block.sync
            def _(sp):
                sp.wait_ge(s_mo, 1)
                sp.dma_start(mT_out.rearrange("(a p) c -> p a c", p=P), mt[:, :, :]).then_inc(s_out, 16)
                sp.wait_ge(s_out, 16)
    keep_ctx.close()

def dram_rows(ap1d, parts, n, at=0):
    return bass.AP(tensor=ap1d.tensor, offset=at, ap=[[0, parts], [1, n]])


class Chain:

    def __init__(self, eng, sem, base=0):
        self.eng, self.sem, self.base, self.n = eng, sem, base, 0

    def link(self, ins):
        self.n += 1
        ins.then_inc(self.sem, 1)
        self.eng.wait_ge(self.sem, self.base + self.n)


def over_tiles(eng, first, body, last):
    with eng.Fori(0, (last - first) // 2) as h:
        for b in range(2):
            body(h * 2 + (first + b), (first + b) % 2, h)


T = 125
NT = 50
H = 8
DH = 32
C = 256
QKV = 3 * C
RR_ = 17
PR = RR_ * DH
FEAT = PR + 1 + DH
KW = FEAT + DH // 2
VW = DH + 1
G5 = 5
SCALE = DH ** 0.25
EPS_N = 1e-12


PACKED_FIRST = SEG - 2 * NT


def layer_norm(nc, prefix, xs, xn, from_dram, wr):
    with ExitStack() as c:
        c.callback(nc.all_engine_barrier)
        def sb(n, s, t=F32):
            return c.enter_context(nc.sbuf_tensor(prefix + n, s, t))

        def sem(n):
            return c.enter_context(a_semaphore(nc, prefix + n))
        st = sb("stats", [T, G5, 6]); mv = sb("mean_var", [T, G5, 2]); sd = sb("sd", [T, G5]); eps = sb("eps", [T, 1])
        s_c = sem("consts"); s_ld = [sem(f"loaded{b}") for b in range(2)]; s_dv = sem("dve"); s_go = sem("dve_goes_on"); s_var = sem("var"); s_sd = sem("sd_ready")
        s_xn = sem("xn_ready")
        if xs is None:
            xs = sb("xs", [T, 2, G5, C])
        with nc.Block() as block:
            @block.gpsimd
            def _(g):
                g.memset(eps[:, :], 1e-5).then_inc(s_c, 1)

            def group(q, b):
                return xs[:, b] if from_dram is not None else xs[:, bass.ds(q * G5, G5), :]

            @block.sync
            def _(sp):
                def body(q, b, h_):
                    if from_dram is not None:
                        sp.wait_ge(s_xn, q + 1)
                        sp.dma_start(xs[:, b], from_dram[bass.ds(q * (G5 * T), G5 * T), :].rearrange("(t p) c -> p t c", p=T)).then_inc(s_ld[b], 16)
                        for k in range(2):
                            wr.pack(sp, q * 2 + k)
                if from_dram is not None:
                    over_tiles(sp, 0, body, NT // G5)
                    for p in range(2 * (NT // G5), PACKED_FIRST):
                        wr.pack(sp, p)

            @block.vector
            def _(v):
                v.engine_nop().then_inc(s_xn, 2)

                def body(q, b, h_):
                    ch = Chain(v, s_dv, q * 2)
                    x_ = group(q, b)
                    if from_dram is not None:
                        v.wait_ge(s_ld[b], h_ * 16 + 16)
                    for j in range(G5):
                        last = v.bn_stats(st[:, j, :], x_[:, j, :])
                    ch.link(last)
                    v.sem_inc(s_go, 1)
                    for j in range(G5):
                        last = v.bn_aggr(mv[:, j, :], st[:, j, :])
                    last.then_inc(s_var, 1)
                    v.wait_ge(s_sd, q + 1)
                    ch.link(v.reciprocal(sd[:, :], sd[:, :]))
                    for j in range(G5):
                        last = v.tensor_scalar(xn[:, bass.ds(q * G5 + j, 1), :].rearrange("p o c -> p (o c)"), x_[:, j, :] if from_dram is not None else xs[:, bass.ds(q * G5 + j, 1), :].rearrange("p o c -> p (o c)"),
                                               mv[:, j, 0:1], sd[:, j:j + 1], ALU.subtract, ALU.mult)
                    last.then_inc(s_xn, 1)
                over_tiles(v, 0, body, NT // G5)

            @block.scalar
            def _(a):
                a.wait_ge(s_c, 1)

                def body(q, b, h_):
                    a.wait_ge(s_var, q + 1)
                    a.wait_ge(s_xn, q + 2)
                    a.activation(sd[:, :], mv[:, :, 1], ACT.Sqrt, bias=eps[:, 0:1]).then_inc(s_sd, 1)
                over_tiles(a, 0, body, NT // G5)


def transposed_tiles(nc, prefix, xn, xT_dram):
    with ExitStack() as c:
        c.callback(nc.all_engine_barrier)
        ident = c.enter_context(nc.sbuf_tensor(prefix + "ident", [P, P], F32))
        xT = c.enter_context(nc.sbuf_tensor(prefix + "xT", [P, 2, 2 * T], F32))
        ps = [c.enter_context(nc.psum_tensor(f"{prefix}ps{b}", [P, 512], F32)) for b in range(2)]
        s_c, s_tp, s_kept, *s_st = (c.enter_context(a_semaphore(nc, prefix + n)) for n in ("consts", "transposed", "kept", "stored0", "stored1"))
        xs = c.enter_context(nc.sbuf_tensor(prefix + "xs", [T, 2, C], F32))
        s_xs = c.enter_context(a_semaphore(nc, prefix + "copied"))
        with nc.Block() as block:
            @block.gpsimd
            def _(g):
                g.memset(ident[:, :], 0.0).then_inc(s_c, 1)
                g.wait_ge(s_c, 1)
                g.affine_select(out=ident[:, :], in_=ident[:, :], compare_op=ALU.not_equal, fill=1.0, base=0,
                                pattern=[[-1, P]], channel_multiplier=1).then_inc(s_c, 1)

            @block.vector
            def _(v):
                v.wait_ge(s_c, 2)
                v.engine_nop().then_inc(s_tp, 2)

                def body(t, b, h_):
                    v.wait_ge(s_tp, t + 1)
                    v.tensor_copy(xs[:, b, :], xn[:, bass.ds(t, 1), :].rearrange("p o c -> p (o c)")).then_inc(s_xs, 1)
                over_tiles(v, 0, body, NT)

            @block.tensor
            def _(pe):
                pe.wait_ge(s_c, 2)

                def body(t, b, h_):
                    pe.wait_ge(s_xs, t + 1)
                    pe.wait_ge(s_kept, t + 1)
                    for k in range(2):
                        last = pe.transpose(ps[b][:, k * T:(k + 1) * T], xs[:, b, k * P:(k + 1) * P], ident[0:T, 0:T])
                    last.then_inc(s_tp, 1)
                over_tiles(pe, 0, body, NT)

            @block.scalar
            def _(a):
                a.wait_ge(s_c, 2)
                a.sem_inc(s_kept, 2)
                for q in s_st:
                    a.sem_inc(q, 16)

                def body(t, b, h_):
                    a.wait_ge(s_tp, t + 3)
                    a.wait_ge(s_st[b], h_ * 16 + 16)
                    a.activation(xT[:, b, :], ps[b][:, 0:2 * T], ACT.Copy).then_inc(s_kept, 1)
                over_tiles(a, 0, body, NT)

            @block.sync
            def _(sp):
                def body(t, b, h_):
                    sp.wait_ge(s_kept, t + 3)
                    sp.dma_start(xT_dram[bass.ds(t, 1), :, :].rearrange("o p c -> (o p) c"), xT[:, b, :]).then_inc(s_st[b], 16)
                over_tiles(sp, 0, body, NT)
                for q in s_st:
                    sp.wait_ge(q, 16 + 8 * NT)


def products(eng, dst, src_feat, heads):
    for h in heads:
        f = src_feat(h)
        out = dst(h).rearrange("p (r i) -> p r i", i=DH)
        once = bass.AP(tensor=f.tensor, offset=f.offset + PR + 1, ap=[list(f.ap[0]), [0, RR_], [1, DH]])
        moved = bass.AP(tensor=f.tensor, offset=f.offset + PR + 1, ap=[list(f.ap[0]), [1, RR_], [1, DH]])
        last = eng.tensor_tensor(out, once, moved, ALU.mult)
    return last


def moments(nc, xT_dram, wqkvT, bqkv, mom_dram, wr):
    with ExitStack() as c:
        c.callback(nc.all_engine_barrier)
        def sb(n, s, t=F32):
            return c.enter_context(nc.sbuf_tensor("mo_" + n, s, t))

        def sem(n):
            return c.enter_context(a_semaphore(nc, "mo_" + n))
        w = sb("w", [P, 2, 2 * C]); bias = sb("bias", [T, 2 * C]); xT = sb("xT", [P, 2, 2 * T])
        ks = sb("ks", [T, C]); sq = sb("sq", [T, C]); ss = sb("ss", [T, H])
        feat = [sb(f"feat{b}", [T, H, KW]) for b in range(2)]
        vh = [sb(f"vh{b}", [T, H, VW]) for b in range(2)]
        out = sb("out", [P, 5, 512])
        main = [c.enter_context(nc.psum_tensor(f"mo_main{q}", [P, 512], F32)) for q in range(4)]
        tail = c.enter_context(nc.psum_tensor("mo_tail", [P, 512], F32))
        kv = [c.enter_context(nc.psum_tensor(f"mo_kv{b}", [P, 512], F32)) for b in range(2)]
        s_w = sem("weights"); s_x = [sem(f"xT_loaded{b}") for b in range(2)]; s_kv = sem("kv_in_psum"); s_ks = sem("kv_kept"); s_sq = sem("norms_wanted")
        s_rt = sem("norms_ready"); s_kn = sem("k_normed"); s_fd = sem("features_dve"); s_fp = sem("features_pool"); s_mm = sem("tile_summed")
        s_dv = sem("dve"); s_c = sem("consts"); s_o = sem("kept"); s_out = sem("stored")
        TAIL = FEAT - 512
        with nc.Block() as block:
            @block.sync
            def _(sp):
                sp.dma_start(w[:, :, :], wqkvT[:, C:QKV].rearrange("(a p) n -> p a n", p=P)).then_inc(s_w, 16)
                sp.dma_start(bias[:, :], dram_rows(bqkv, T, 2 * C, C)).then_inc(s_w, 16)

                def body(t, b, h_):
                    sp.wait_ge(s_kv, t + 1)
                    sp.dma_start(xT[:, b, :], xT_dram[bass.ds(t, 1), :, :].rearrange("o p c -> (o p) c")).then_inc(s_x[b], 16)
                    for k in range(2):
                        wr.pack(sp, t * 2 + (PACKED_FIRST + k))
                over_tiles(sp, 0, body, NT)
                sp.wait_ge(s_o, 5)
                for h in range(H):
                    q, p0 = h // 2, 64 * (h % 2)
                    sp.dma_start(mom_dram[h, :, 0:512], out[p0:p0 + VW, q, :]).then_inc(s_out, 16)
                    sp.dma_start(mom_dram[h, :, 512:FEAT], out[p0:p0 + VW, 4, q * TAIL:(q + 1) * TAIL]).then_inc(s_out, 16)
                sp.wait_ge(s_out, 16 * 2 * H)

            @block.tensor
            def _(pe):
                pe.wait_ge(s_w, 32)
                pe.wait_ge(s_c, 2)
                pe.sem_inc(s_kv, 2)
                pe.sem_inc(s_mm, 2)

                def kv_of(t, b, turn):
                    pe.wait_ge(s_x[b], turn * 16 + 16)
                    pe.wait_ge(s_ks, t + 1)
                    for k in range(2):
                        last = pe.matmul(kv[b][0:T, :], xT[:, b, k * T:(k + 1) * T], w[:, k, :], start=(k == 0), stop=(k == 1))
                    last.then_inc(s_kv, 1)

                def sums(t, b):
                    pe.wait_ge(s_fd, t + 1)
                    pe.wait_ge(s_fp, t + 1)
                    for h in range(H):
                        q, p0 = h // 2, 64 * (h % 2)
                        pe.matmul(main[q][p0:p0 + VW, :], vh[b][:, h, :], feat[b][:, h, 0:512], start=False, stop=True, skip_group_check=True)
                        last = pe.matmul(tail[p0:p0 + VW, q * TAIL:(q + 1) * TAIL], vh[b][:, h, :], feat[b][:, h, 512:FEAT], start=False, stop=True, skip_group_check=True)
                    last.then_inc(s_mm, 1)
                kv_of(0, 0, 0)
                with pe.Fori(0, (NT - 2) // 2) as h2:
                    for b in range(2):
                        kv_of(h2 * 2 + (b + 1), 1 - b, h2 + b)
                        sums(h2 * 2 + b, b)
                kv_of(NT - 1, 1, NT // 2 - 1)
                sums(NT - 2, 0)
                sums(NT - 1, 1)

            @block.vector
            def _(v):
                for q in range(4):
                    v.memset(main[q][:, :], 0.0)
                v.memset(tail[:, :], 0.0).then_inc(s_c, 1)
                for b in range(2):
                    v.memset(vh[b][:, :, 0:1], 1.0)
                    last = v.memset(feat[b][:, :, PR:PR + 1], 1.0)
                last.then_inc(s_c, 1)
                v.wait_ge(s_c, 2)
                v.wait_ge(s_w, 32)
                v.engine_nop().then_inc(s_ks, 2)

                def body(t, b, h_):
                    ch = Chain(v, s_dv, t * 4)
                    v.wait_ge(s_kv, t + 3)
                    v.wait_ge(s_mm, t + 1)
                    v.tensor_tensor(vh[b][:, :, 1:VW], kv[b][0:T, C:2 * C].rearrange("p (h d) -> p h d", d=DH), bias[:, C:2 * C].rearrange("p (h d) -> p h d", d=DH), ALU.add)
                    v.tensor_tensor(ks[:, :], kv[b][0:T, 0:C], bias[:, 0:C], ALU.add).then_inc(s_ks, 1)
                    v.wait_ge(s_ks, t + 3)
                    ch.link(v.tensor_tensor(sq[:, :], ks[:, :], ks[:, :], ALU.mult))
                    v.tensor_reduce(ss[:, :], sq[:, :].rearrange("p (h d) -> p h d", d=DH), AX.X, ALU.add).then_inc(s_sq, 1)
                    v.wait_ge(s_rt, t + 1)
                    ch.link(v.tensor_scalar(ss[:, :], ss[:, :], EPS_N, None, ALU.max))
                    ch.link(v.reciprocal(ss[:, :], ss[:, :]))
                    ch.link(v.tensor_scalar(ss[:, :], ss[:, :], SCALE, None, ALU.mult))
                    ks3 = ks[:, :].rearrange("p (h d) -> p h d", d=DH)
                    v.tensor_tensor(feat[b][:, :, PR + 1:FEAT], ks3, ss[:, :].unsqueeze(2).to_broadcast([T, H, DH]), ALU.mult)
                    v.tensor_tensor(feat[b][:, :, FEAT:KW], ks3[:, :, 0:DH // 2], ss[:, :].unsqueeze(2).to_broadcast([T, H, DH // 2]), ALU.mult).then_inc(s_kn, 1)
                    v.wait_ge(s_kn, t + 1)
                    products(v, lambda h: feat[b][:, h, 0:PR], lambda h: feat[b][:, h, 0:1], range(0, 5)).then_inc(s_fd, 1)
                over_tiles(v, 0, body, NT)
                v.wait_ge(s_mm, NT + 2)
                for q in range(4):
                    v.tensor_copy(out[:, q, :], main[q][:, :]).then_inc(s_o, 1)
                v.tensor_copy(out[:, 4, :], tail[:, :]).then_inc(s_o, 1)

            @block.scalar
            def _(a):
                def body(t, b, h_):
                    a.wait_ge(s_sq, t + 1)
                    a.activation(ss[:, :], ss[:, :], ACT.Sqrt).then_inc(s_rt, 1)
                over_tiles(a, 0, body, NT)

            @block.gpsimd
            def _(g):
                def body(t, b, h_):
                    g.wait_ge(s_kn, t + 1)
                    g.sem_inc(s_c, 1)
                    products(g, lambda h: feat[b][:, h, 0:PR], lambda h: feat[b][:, h, 0:1], range(5, H)).then_inc(s_fp, 1)
                over_tiles(g, 0, body, NT)


def attend(nc, xT_dram, wqkvT, bqkv, temp, wprojT, bproj, mom_dram, mT_dram, x_dram, x1):
    with ExitStack() as c:
        c.callback(nc.all_engine_barrier)
        def sb(n, s, t=F32):
            return c.enter_context(nc.sbuf_tensor("at_" + n, s, t))

        def sem(n):
            return c.enter_context(a_semaphore(nc, "at_" + n))

        def ps(n):
            return c.enter_context(nc.psum_tensor("at_ps_" + n, [P, 512], F32))
        wq = sb("wq", [P, 2, 2 * C]); bq = sb("bq", [T, C]); tmp8 = sb("temp", [T, H]); wp = sb("wp", [P, 2, C]); bp = sb("bp", [T, C])
        ident = sb("ident", [P, P]); mom = sb("mom", [VW, H, FEAT]); momT = sb("momT", [P, 5, H, VW]); wt = sb("wt", [P, 5])
        xT = sb("xT", [P, 2, 2 * T]); xs = sb("xs", [T, 2, C])
        qs = sb("qs", [T, C]); sq = sb("sq", [T, C]); ss = sb("ss", [T, H])
        feat = [sb(f"feat{b}", [T, H, KW]) for b in range(2)]
        fT = [sb(f"fT{b}", [P, 4, T]) for b in range(2)]
        fE = [sb(f"fE{b}", [P, 4, T]) for b in range(2)]
        rec = sb("rec", [T, H]); o = sb("o", [T, C]); oT = sb("oT", [P, 2 * T])
        p_q = ps("q"); p_t = [ps(f"t{b}") for b in range(2)]; p_e = [ps(f"e{b}") for b in range(2)]; p_y = ps("y"); p_o = ps("o"); p_r = ps("r")
        names = ("w", "x_ld0", "x_ld1", "q_ps", "q_kept", "sq", "rt", "qn", "fd", "fp", "t_ps", "t_kept", "e_ps", "e_kept", "y_ps", "o_ready", "oT_ps", "oT_kept",
                 "r_ps", "r_kept", "consts", "momT_ps", "momT_kept", "dve_front", "dve_back", "temp_ready", "momw", "pool_goes_on", "x_bias")
        s = {n: sem(n) for n in names}

        def steps(eng, first, middle, last):
            first()
            over_tiles(eng, 1, middle, NT - 1)
            last()

        with nc.Block() as block:
            @block.sync
            def _(sp):
                sp.dma_start(wq[:, :, 0:C], wqkvT[:, 0:C].rearrange("(a p) n -> p a n", p=P)).then_inc(s["w"], 16)
                sp.dma_start(wq[:, :, C:2 * C], mT_dram.rearrange("(a p) n -> p a n", p=P)).then_inc(s["w"], 16)
                sp.dma_start(wp[:, :, :], wprojT.rearrange("(a p) n -> p a n", p=P)).then_inc(s["w"], 16)
                sp.dma_start(bq[:, :], dram_rows(bqkv, T, C)).then_inc(s["w"], 16)
                sp.dma_start(bp[:, :], dram_rows(bproj, T, C)).then_inc(s["w"], 16)
                sp.dma_start(tmp8[:, :], dram_rows(temp, T, H)).then_inc(s["w"], 16)
                sp.dma_start(mom[:, :, :], mom_dram.rearrange("h e f -> e h f")).then_inc(s["w"], 16)

                def body(t, b, h_):
                    sp.wait_ge(s["q_kept"], t + 1)
                    sp.dma_start(xT[:, b, :], xT_dram[bass.ds(t, 1), :, :].rearrange("o p c -> (o p) c")).then_inc(s[f"x_ld{b}"], 16)
                    sp.dma_start(xs[:, b, :], x_dram[bass.ds(t * T, T), :]).then_inc(s[f"x_ld{b}"], 16)
                over_tiles(sp, 0, body, NT)

            @block.gpsimd
            def _(g):
                g.memset(ident[:, :], 0.0).then_inc(s["consts"], 1)
                g.memset(wt[:, :], 1.0).then_inc(s["consts"], 1)
                g.wait_ge(s["consts"], 2)
                g.affine_select(out=ident[:, :], in_=ident[:, :], compare_op=ALU.not_equal, fill=1.0, base=0,
                                pattern=[[-1, P]], channel_multiplier=1).then_inc(s["consts"], 1)
                g.memset(wt[0:DH, 0:1], 0.5).then_inc(s["consts"], 1)
                g.memset(wt[:, 4:5], SCALE ** 2).then_inc(s["consts"], 1)
                g.wait_ge(s["consts"], 5)
                g.memset(wt[0:DH, 4:5], 0.5).then_inc(s["consts"], 1)
                g.wait_ge(s["consts"], 6)
                g.memset(wt[DH:DH + 1, 4:5], SCALE ** 4).then_inc(s["consts"], 1)
                g.wait_ge(s["consts"], 7)
                for b in range(2):
                    g.memset(feat[b][:, :, PR:PR + 1], 1.0).then_inc(s["consts"], 1)
                g.wait_ge(s["consts"], 9)
                g.wait_ge(s["w"], 16 * 7)
                g.sem_inc(s["pool_goes_on"], 1)

                def body(t, b, h_):
                    g.wait_ge(s[f"x_ld{b}"], h_ * 32 + 32)
                    g.sem_inc(s["pool_goes_on"], 1)
                    g.tensor_tensor(xs[:, b, :], xs[:, b, :], bp[:, :], ALU.add).then_inc(s["x_bias"], 1)
                    g.wait_ge(s["qn"], t + 1)
                    g.sem_inc(s["pool_goes_on"], 1)
                    products(g, lambda h: feat[b][:, h, 0:PR], lambda h: feat[b][:, h, 0:1], range(5, H)).then_inc(s["fp"], 1)
                over_tiles(g, 0, body, NT)

            @block.tensor
            def _(pe):
                pe.wait_ge(s["w"], 16 * 7)
                pe.wait_ge(s["consts"], 9)
                for h in range(H):
                    if h >= 2:
                        pe.wait_ge(s["momT_kept"], h - 1)
                    for k in range(5):
                        m = min(P, FEAT - k * P)
                        last = pe.transpose(p_t[h % 2][0:m, k * VW:(k + 1) * VW], mom[:, h, k * P:k * P + m], ident[0:VW, 0:VW])
                    last.then_inc(s["momT_ps"], 1)
                pe.wait_ge(s["momT_kept"], H)
                pe.wait_ge(s["momw"], 5)
                pe.sem_inc(s["t_ps"], 1)

                def q_of(t, b, turn):
                    pe.wait_ge(s[f"x_ld{b}"], turn * 32 + 32)
                    pe.wait_ge(s["q_kept"], t + 2)
                    for k in range(2):
                        last = pe.matmul(p_q[0:T, :], xT[:, b, k * T:(k + 1) * T], wq[:, k, :], start=(k == 0), stop=(k == 1))
                    last.then_inc(s["q_ps"], 1)

                def o_transposed(t):
                    pe.wait_ge(s["o_ready"], t + 1)
                    for k in range(2):
                        last = pe.transpose(p_o[:, k * T:(k + 1) * T], o[:, k * P:(k + 1) * P], ident[0:T, 0:T])
                    last.then_inc(s["oT_ps"], 1)

                def projected(t):
                    pe.wait_ge(s["oT_kept"], t + 1)
                    pe.wait_ge(s["r_kept"], t + 1)
                    for k in range(2):
                        last = pe.matmul(p_r[0:T, 0:C], oT[:, k * T:(k + 1) * T], wp[:, k, :], start=(k == 0), stop=(k == 1))
                    last.then_inc(s["r_ps"], 1)

                def heads(t, b, before):
                    pe.wait_ge(s["fd"], t + 1)
                    pe.wait_ge(s["fp"], t + 1)
                    for g4 in range(2):
                        pe.wait_ge(s["e_kept"], t * 2 + (g4 + 1))
                        for j in range(4):
                            last = pe.transpose(p_e[g4][0:FEAT - 512, j * T:(j + 1) * T], feat[b][:, g4 * 4 + j, 512:FEAT], ident[0:T, 0:T])
                        last.then_inc(s["e_ps"], 1)

                    def transposes(h):
                        pe.wait_ge(s["t_kept"], t * 8 + (h + 1))
                        for k in range(4):
                            last = pe.transpose(p_t[h % 2][:, k * T:(k + 1) * T], feat[b][:, h, k * P:(k + 1) * P], ident[0:T, 0:T])
                        last.then_inc(s["t_ps"], 1)

                    def apply(h):
                        pe.wait_ge(s["t_kept"], t * 8 + (h + 3))
                        if h % 4 == 0:
                            pe.wait_ge(s["e_kept"], t * 2 + (h // 4 + 3))
                        for k in range(4):
                            pe.matmul(p_y[0:T, h * VW:(h + 1) * VW], fT[h % 2][:, k, :], momT[:, k, h, :], start=(k == 0), stop=False)
                        last = pe.matmul(p_y[0:T, h * VW:(h + 1) * VW], fE[h // 4][0:FEAT - 512, h % 4, :], momT[0:FEAT - 512, 4, h, :], start=False, stop=True)
                        last.then_inc(s["y_ps"], 1)
                    transposes(0)
                    for h in range(H):
                        if h + 1 < H:
                            transposes(h + 1)
                        if before and h == 0:
                            o_transposed(t - 1)
                        if before and h == 3:
                            projected(t - 1)
                        apply(h)

                def first():
                    q_of(0, 0, 0)
                    q_of(1, 1, 0)
                    heads(0, 0, False)

                def middle(t, b, h_):
                    q_of(t + 1, 1 - b, h_ + 1)
                    heads(t, b, True)

                def last_():
                    heads(NT - 1, 1, True)
                    o_transposed(NT - 1)
                    projected(NT - 1)
                steps(pe, first, middle, last_)

            @block.scalar
            def _(a):
                a.sem_inc(s["t_kept"], 2)
                a.sem_inc(s["e_kept"], 2)

                def root(t):
                    a.wait_ge(s["sq"], t + 1)
                    a.activation(ss[:, :], ss[:, :], ACT.Sqrt).then_inc(s["rt"], 1)

                def oT_of(t):
                    a.wait_ge(s["oT_ps"], t + 1)
                    a.activation(oT[:, :], p_o[:, 0:2 * T], ACT.Copy).then_inc(s["oT_kept"], 1)

                def kept(t, before, after):
                    for g4 in range(2):
                        a.wait_ge(s["e_ps"], t * 2 + (g4 + 1))
                        a.activation(fE[g4][0:FEAT - 512, :, :].rearrange("p a b -> p (a b)"), p_e[g4][0:FEAT - 512, 0:4 * T], ACT.Copy).then_inc(s["e_kept"], 1)
                    for h in range(H):
                        a.wait_ge(s["t_ps"], t * 8 + (h + 2))
                        a.activation(fT[h % 2][:, :, :].rearrange("p a b -> p (a b)"), p_t[h % 2][:, 0:4 * T], ACT.Copy).then_inc(s["t_kept"], 1)
                        if before and h == 1:
                            oT_of(t - 1)
                        if after and h == 0:
                            root(t + 1)

                def first():
                    root(0)
                    kept(0, False, True)

                def middle(t, b, h_):
                    kept(t, True, True)

                def last_():
                    kept(NT - 1, True, False)
                    oT_of(NT - 1)
                steps(a, first, middle, last_)

            @block.vector
            def _(v):
                for h in range(H):
                    v.wait_ge(s["momT_ps"], h + 1)
                    v.tensor_copy(momT[:, 0:4, h, :], p_t[h % 2][:, 0:4 * VW].rearrange("p (k e) -> p k e", e=VW))
                    v.tensor_copy(momT[0:FEAT - 512, 4, h, :], p_t[h % 2][0:FEAT - 512, 4 * VW:5 * VW]).then_inc(s["momT_kept"], 1)
                v.wait_ge(s["momT_kept"], H)
                v.wait_ge(s["consts"], 9)
                for k in range(5):
                    m = min(P, FEAT - k * P)
                    v.tensor_scalar(momT[0:m, k, :, :], momT[0:m, k, :, :], wt[0:m, k:k + 1], 1.0 / (NT * T), ALU.mult, ALU.mult).then_inc(s["momw"], 1)
                v.wait_ge(s["w"], 16 * 7)
                v.engine_nop().then_inc(s["r_kept"], 1)
                v.engine_nop().then_inc(s["q_kept"], 2)
                v.tensor_scalar(tmp8[:, :], tmp8[:, :], SCALE * SCALE, None, ALU.mult).then_inc(s["temp_ready"], 1)
                v.wait_ge(s["temp_ready"], 1)

                def x1_of(t):
                    return x1[:, bass.ds(t, 1), :].rearrange("p o c -> p (o c)")

                def features(t, b):
                    ch = Chain(v, s["dve_front"], t * 4)
                    v.wait_ge(s["x_bias"], t + 1)
                    v.wait_ge(s["q_ps"], t + 1)
                    v.tensor_tensor(x1_of(t), p_q[0:T, C:2 * C], xs[:, b, :], ALU.add)
                    v.tensor_tensor(qs[:, :], p_q[0:T, 0:C], bq[:, :], ALU.add).then_inc(s["q_kept"], 1)
                    v.wait_ge(s["q_kept"], t + 3)
                    ch.link(v.tensor_tensor(sq[:, :], qs[:, :], qs[:, :], ALU.mult))
                    v.tensor_reduce(ss[:, :], sq[:, :].rearrange("p (h d) -> p h d", d=DH), AX.X, ALU.add).then_inc(s["sq"], 1)
                    v.wait_ge(s["rt"], t + 1)
                    ch.link(v.tensor_scalar(ss[:, :], ss[:, :], SCALE, EPS_N, ALU.mult, ALU.max))
                    ch.link(v.reciprocal(ss[:, :], ss[:, :]))
                    ch.link(v.tensor_tensor(ss[:, :], ss[:, :], tmp8[:, :], ALU.mult))
                    qs3 = qs[:, :].rearrange("p (h d) -> p h d", d=DH)
                    v.tensor_tensor(feat[b][:, :, PR + 1:FEAT], qs3, ss[:, :].unsqueeze(2).to_broadcast([T, H, DH]), ALU.mult)
                    v.tensor_tensor(feat[b][:, :, FEAT:KW], qs3[:, :, 0:DH // 2], ss[:, :].unsqueeze(2).to_broadcast([T, H, DH // 2]), ALU.mult).then_inc(s["qn"], 1)
                    v.wait_ge(s["qn"], t + 1)
                    products(v, lambda h: feat[b][:, h, 0:PR], lambda h: feat[b][:, h, 0:1], range(0, 5)).then_inc(s["fd"], 1)

                def attended(t):
                    v.wait_ge(s["y_ps"], t * 8 + 8)
                    y3 = p_y[0:T, 0:H * VW].rearrange("p (h e) -> p h e", e=VW)
                    v.reciprocal(rec[:, :], y3[:, :, 0]).then_inc(s["dve_back"], 1)
                    v.wait_ge(s["dve_back"], t + 1)
                    v.tensor_tensor(o[:, :].rearrange("p (h d) -> p h d", d=DH), y3[:, :, 1:VW], rec[:, :].unsqueeze(2).to_broadcast([T, H, DH]), ALU.mult).then_inc(s["o_ready"], 1)

                def summed(t):
                    v.wait_ge(s["r_ps"], t + 1)
                    v.tensor_tensor(x1_of(t), x1_of(t), p_r[0:T, 0:C], ALU.add).then_inc(s["r_kept"], 1)

                def first():
                    features(0, 0)
                    features(1, 1)
                    attended(0)

                def middle(t, b, h_):
                    features(t + 1, 1 - b)
                    summed(t - 1)
                    attended(t)

                def last_():
                    summed(NT - 2)
                    attended(NT - 1)
                    summed(NT - 1)
                steps(v, first, middle, last_)

E_N = 8
HID = 1024
CAP = -(-5 * NT * T // (4 * E_N))
ROOM = CAP
NONE = 100000
ZW = E_N * ROOM * C // (4 * P)
F_MAX = 3.4028234663852886e38


def route(nc, xT_dram, gate_w, gate_b, xn, buf_dram, slot_i, coef):
    with ExitStack() as c:
        c.callback(nc.all_engine_barrier)
        def sb(n, s, t=F32):
            return c.enter_context(nc.sbuf_tensor("ro_" + n, s, t))

        def sem(n):
            return c.enter_context(a_semaphore(nc, "ro_" + n))
        gw = sb("gw", [P, 2, E_N]); gb = sb("gb", [T, E_N]); xT = sb("xT", [P, 2, 2 * T]); zero = sb("zero", [P, ZW])
        lg = sb("lg", [T, NT, E_N]); w8 = sb("w8", [T, NT, E_N]); oh = sb("oh", [T, NT, E_N]); ex = sb("ex", [T, NT, E_N]); z50 = sb("z50", [T, NT])
        m = sb("m", [T, NT]); idx = sb("idx", [T, NT]); pos = sb("pos", [T, NT]); kept = sb("kept", [T, NT]); dst = sb("dst", [T, NT])
        tri = sb("tri", [T, T]); ones = sb("ones", [T, T]); dst_i = sb("dst_i", [T, NT], I32)
        rowi = [sb(f"rowi{b}", [T, 1], I32) for b in range(2)]
        rows = [sb(f"rows{b}", [T, C]) for b in range(2)]
        p_l = [c.enter_context(nc.psum_tensor(f"ro_l{b}", [P, 512], F32)) for b in range(2)]
        p_c = c.enter_context(nc.psum_tensor("ro_c", [P, 512], F32)); p_s = c.enter_context(nc.psum_tensor("ro_s", [P, 512], F32))
        s_w = sem("w"); s_z = sem("zero"); s_zf = sem("buf_zeroed"); s_x = [sem(f"x{b}") for b in range(2)]; s_l = sem("l_ps"); s_lk = sem("l_kept"); s_dv = sem("dve")
        s_e = sem("exp_wanted"); s_ex = sem("exp_ready"); s_oh = sem("oh_ready"); s_cp = sem("counts_ps"); s_di = sem("rows_known")
        s_c = sem("consts"); s_cpd = sem("copied"); s_sc = [sem(f"scattered{b}") for b in range(2)]; s_go = sem("pool_goes_on")
        with nc.Block() as block:
            @block.sync
            def _(sp):
                sp.dma_start(gw[:, :, :], gate_w.rearrange("(a p) n -> p a n", p=P)).then_inc(s_w, 16)
                sp.dma_start(gb[:, :], dram_rows(gate_b, T, E_N)).then_inc(s_w, 16)
                sp.wait_ge(s_z, 1)
                flat = bass.AP(tensor=buf_dram.tensor, offset=0, ap=[[4 * ZW, P], [1, 4 * ZW]])
                for k in range(4):
                    sp.dma_start(flat[:, k * ZW:(k + 1) * ZW], zero[:, :]).then_inc(s_zf, 16)

                def body(t, b, h_):
                    sp.wait_ge(s_l, t + 1)
                    sp.dma_start(xT[:, b, :], xT_dram[bass.ds(t, 1), :, :].rearrange("o p c -> (o p) c")).then_inc(s_x[b], 16)
                over_tiles(sp, 0, body, NT)

            @block.tensor
            def _(pe):
                pe.wait_ge(s_w, 32)
                pe.sem_inc(s_l, 2)

                def body(t, b, h_):
                    pe.wait_ge(s_x[b], h_ * 16 + 16)
                    pe.wait_ge(s_lk, t + 1)
                    for k in range(2):
                        last = pe.matmul(p_l[b][0:T, 0:E_N], xT[:, b, k * T:(k + 1) * T], gw[:, k, :], start=(k == 0), stop=(k == 1))
                    last.then_inc(s_l, 1)
                over_tiles(pe, 0, body, NT)
                pe.wait_ge(s_c, 5)
                pe.wait_ge(s_oh, 1)
                ohf = oh[:, :, :].rearrange("p t e -> p (t e)")
                pe.matmul(p_c[0:T, 0:NT * E_N], tri[:, :], ohf, start=True, stop=True)
                pe.matmul(p_s[0:T, 0:NT * E_N], ones[:, :], ohf, start=True, stop=True).then_inc(s_cp, 1)

            @block.scalar
            def _(a):
                a.wait_ge(s_e, 1)
                a.activation(lg[:, :, :], lg[:, :, :], ACT.Exp).then_inc(s_ex, 1)

            @block.vector
            def _(v):
                v.wait_ge(s_w, 32)
                v.engine_nop().then_inc(s_lk, 2)

                def body(t, b, h_):
                    v.wait_ge(s_l, t + 3)
                    v.tensor_tensor(lg[:, bass.ds(t, 1), :].rearrange("p o e -> p (o e)"), p_l[b][0:T, 0:E_N], gb[:, :], ALU.add).then_inc(s_lk, 1)
                over_tiles(v, 0, body, NT)
                v.wait_ge(s_lk, NT + 2)
                v.wait_ge(s_c, 5)
                ch = Chain(v, s_dv)

                def each(a):
                    return a[:, :].unsqueeze(2).to_broadcast([T, NT, E_N])
                ch.link(v.tensor_reduce(m[:, :], lg[:, :, :], AX.X, ALU.max))
                v.tensor_tensor(lg[:, :, :], lg[:, :, :], each(m), ALU.subtract).then_inc(s_e, 1)
                v.wait_ge(s_ex, 1)
                ch.link(v.tensor_reduce(m[:, :], lg[:, :, :], AX.X, ALU.add))
                ch.link(v.reciprocal(m[:, :], m[:, :]))
                ch.link(v.tensor_tensor(lg[:, :, :], lg[:, :, :], each(m), ALU.mult))
                ch.link(v.tensor_reduce(coef[:, :], lg[:, :, :], AX.X, ALU.max))
                ch.link(v.tensor_tensor(oh[:, :, :], lg[:, :, :], each(coef), ALU.is_equal))
                ch.link(v.tensor_tensor(lg[:, :, :], oh[:, :, :], w8[:, :, :], ALU.mult))
                ch.link(v.tensor_reduce(idx[:, :], lg[:, :, :], AX.X, ALU.max))
                v.tensor_tensor(oh[:, :, :], lg[:, :, :], each(idx), ALU.is_equal).then_inc(s_oh, 1)
                v.wait_ge(s_oh, 1)
                v.wait_ge(s_cp, 1)
                tot = p_s[0:T, 0:NT * E_N].rearrange("p (t e) -> p t e", e=E_N)
                for e in range(E_N):
                    last = v.tensor_tensor_scan(ex[:, :, e], tot[:, :, e], z50[:, :], 0.0, ALU.add, ALU.add)
                ch.link(last)
                ch.link(v.tensor_tensor(ex[:, :, :], ex[:, :, :], tot, ALU.subtract))
                ch.link(v.tensor_tensor(ex[:, :, :], ex[:, :, :], p_c[0:T, 0:NT * E_N].rearrange("p (t e) -> p t e", e=E_N), ALU.add))
                ch.link(v.tensor_tensor(ex[:, :, :], ex[:, :, :], oh[:, :, :], ALU.mult))
                ch.link(v.tensor_reduce(pos[:, :], ex[:, :, :], AX.X, ALU.add))
                v.tensor_scalar(idx[:, :], idx[:, :], -float(ROOM), float(E_N * ROOM), ALU.mult, ALU.add)
                ch.link(v.tensor_scalar(pos[:, :], pos[:, :], -1.0, None, ALU.add))
                ch.link(v.tensor_scalar(kept[:, :], pos[:, :], float(CAP), None, ALU.is_lt))
                ch.link(v.tensor_tensor(coef[:, :], coef[:, :], kept[:, :], ALU.mult))
                ch.link(v.tensor_tensor(dst[:, :], pos[:, :], idx[:, :], ALU.add))
                ch.link(v.tensor_scalar(kept[:, :], kept[:, :], -float(NONE), float(NONE), ALU.mult, ALU.add))
                ch.link(v.tensor_tensor(dst[:, :], dst[:, :], kept[:, :], ALU.add))
                v.tensor_copy(dst_i[:, :], dst[:, :]).then_inc(s_di, 1)
                ch.link(v.tensor_scalar(pos[:, :], pos[:, :], float(CAP - 1), None, ALU.min))
                ch.link(v.tensor_tensor(pos[:, :], pos[:, :], idx[:, :], ALU.add))
                ch.link(v.tensor_copy(slot_i[:, :], pos[:, :]))

            @block.gpsimd
            def _(g):
                g.memset(zero[:, :], 0.0).then_inc(s_z, 1)
                g.iota(w8[:, :, :], pattern=[[0, NT], [-1, E_N]], base=E_N, channel_multiplier=0, allow_small_or_imprecise_dtypes=True).then_inc(s_c, 1)
                g.memset(z50[:, :], 0.0).then_inc(s_c, 1)
                g.memset(ones[:, :], 1.0).then_inc(s_c, 1)
                g.memset(tri[:, :], 1.0).then_inc(s_c, 1)
                g.wait_ge(s_c, 4)
                g.affine_select(out=tri[:, :], in_=tri[:, :], compare_op=ALU.is_ge, fill=0.0, base=0,
                                pattern=[[1, T]], channel_multiplier=-1).then_inc(s_c, 1)
                g.wait_ge(s_di, 1)
                g.wait_ge(s_zf, 64)

                def scatter(t, b):
                    g.tensor_copy(rowi[b][:, :], dst_i[:, bass.ds(t, 1)]).then_inc(s_cpd, 1)
                    g.tensor_copy(rows[b][:, :], xn[:, bass.ds(t, 1), :].rearrange("p o c -> p (o c)")).then_inc(s_cpd, 1)
                    g.wait_ge(s_cpd, t * 2 + 2)
                    g.sem_inc(s_go, 1)
                    g.indirect_dma_start(out=buf_dram, out_offset=bass.IndirectOffsetOnAxis(ap=rowi[b][:, 0:1], axis=0),
                                         in_=rows[b][:, :], in_offset=None, bounds_check=E_N * ROOM - 1, oob_is_err=False).then_inc(s_sc[b], 16)
                for t in range(2):
                    scatter(t, t)

                def body(t, b, h_):
                    g.wait_ge(s_sc[b], h_ * 16 + 16)
                    g.sem_inc(s_go, 1)
                    scatter(t, b)
                over_tiles(g, 2, body, NT)
                for q in s_sc:
                    g.wait_ge(q, 8 * NT)


def experts(nc, buf_dram, w1, b1p, w2, b2, y_dram):
    with ExitStack() as c:
        c.callback(nc.all_engine_barrier)
        def sb(n, s, t=F32):
            return c.enter_context(nc.sbuf_tensor("ex_" + n, s, t))

        def sem(n):
            return c.enter_context(a_semaphore(nc, "ex_" + n))
        KC, FC, TT = C // P, HID // P, -(-ROOM // P)
        LAST = CAP - (TT - 1) * P
        ident = sb("ident", [P, P]); b1s = sb("b1", [P, E_N, FC]); b1c = sb("b1c", [P, FC]); b2s = sb("b2", [P, E_N, C])
        w1s = sb("w1", [P, 2, KC, HID]); w2s = sb("w2", [P, 2, FC, C]); xr = sb("xr", [P, 2, TT, C]); XT = sb("XT", [P, KC, TT * P])
        hT = sb("hT", [P, FC, TT * P]); yo = sb("yo", [P, 2, TT, C])
        p_x = [c.enter_context(nc.psum_tensor(f"ex_x{b}", [P, 512], F32)) for b in range(2)]
        p_h = [c.enter_context(nc.psum_tensor(f"ex_h{b}", [P, 512], F32)) for b in range(2)]
        p_y = [c.enter_context(nc.psum_tensor(f"ex_y{b}", [P, 512], F32)) for b in range(2)]
        s_b = sem("biases"); s_c = sem("ident_ready"); s_wl = [sem(f"weights{b}") for b in range(2)]; s_xl = [sem(f"rows{b}") for b in range(2)]; s_xp = sem("xT_ps"); s_xk = sem("xT_kept")
        s_hp = sem("h_ps"); s_hk = sem("h_kept"); s_yp = sem("y_ps"); s_yk = sem("y_kept"); s_ys = sem("y_stored"); s_bc = sem("b1_ready"); s_ysf = sem("rows_free")
        with nc.Block() as block:
            @block.sync
            def _(sp):
                sp.dma_start(b1s[:, :, :], b1p).then_inc(s_b, 16)
                sp.dma_start(b2s[:, :, :], bass.AP(tensor=b2.tensor, offset=0, ap=[[0, P], [C, E_N], [1, C]])).then_inc(s_b, 16)

                def body(e, b, h_):
                    sp.wait_ge(s_yp, e * TT + TT)
                    sp.dma_start(xr[:, b, 0:TT - 1, :], buf_dram[bass.ds(e * ROOM, (TT - 1) * P), :].rearrange("(t p) c -> p t c", p=P)).then_inc(s_xl[b], 16)
                    sp.dma_start(xr[0:LAST, b, TT - 1, :], buf_dram[bass.ds(e * ROOM + (TT - 1) * P, LAST), :]).then_inc(s_xl[b], 16)
                    sp.dma_start(w1s[:, b], w1[bass.ds(e, 1), :, :].rearrange("o (k p) f -> p (o k) f", p=P)).then_inc(s_wl[b], 16)
                    sp.dma_start(w2s[:, b], w2[bass.ds(e, 1), :, :].rearrange("o (k p) f -> p (o k) f", p=P)).then_inc(s_wl[b], 16)
                over_tiles(sp, 0, body, E_N)

            @block.gpsimd
            def _(g):
                g.memset(ident[:, :], 0.0).then_inc(s_c, 1)
                g.wait_ge(s_c, 1)
                g.affine_select(out=ident[:, :], in_=ident[:, :], compare_op=ALU.not_equal, fill=1.0, base=0,
                                pattern=[[-1, P]], channel_multiplier=1).then_inc(s_c, 1)
                g.sem_inc(s_ysf, 2)

                def body(e, b, h_):
                    g.wait_ge(s_yk, e * TT + (TT + 2))
                    g.sem_inc(s_c, 1)
                    g.dma_start(y_dram[bass.ds(e * ROOM, (TT - 1) * P), :].rearrange("(t p) c -> p t c", p=P), yo[:, b, 0:TT - 1, :]).then_inc(s_ys, 16)
                    g.dma_start(y_dram[bass.ds(e * ROOM + (TT - 1) * P, LAST), :], yo[0:LAST, b, TT - 1, :]).then_inc(s_ys, 16)
                    g.wait_ge(s_ys, e * 32 + 32)
                    g.sem_inc(s_ysf, 1)
                over_tiles(g, 0, body, E_N)
                g.wait_ge(s_ys, 32 * E_N)

            halves = [(0, 512), (512, CAP)]

            @block.tensor
            def _(pe):
                pe.wait_ge(s_c, 2)
                pe.sem_inc(s_yp, 2 * TT)

                def body(e, b, h_):
                    pe.wait_ge(s_xl[b], h_ * 32 + 32)
                    for k in range(KC):
                        for q in range(2):
                            n = 2 * k + q
                            pe.wait_ge(s_xk, e * 4 + (n + 1))
                            for j in range(4):
                                m = P if q * 4 + j < TT - 1 else LAST
                                last = pe.transpose(p_x[n % 2][:, j * P:j * P + m], xr[0:m, b, q * 4 + j, k * P:(k + 1) * P], ident[0:m, 0:m])
                            last.then_inc(s_xp, 1)
                    pe.wait_ge(s_wl[b], h_ * 32 + 32)
                    pe.wait_ge(s_xk, e * 4 + 6)
                    for f in range(FC):
                        for q, (lo, hi) in enumerate(halves):
                            n = 2 * f + q
                            pe.wait_ge(s_hk, e * 16 + (n + 1))
                            for k in range(KC):
                                last = pe.matmul(p_h[n % 2][:, 0:hi - lo], w1s[:, b, k, f * P:(f + 1) * P], XT[:, k, lo:hi], start=(k == 0), stop=(k == KC - 1))
                            last.then_inc(s_hp, 1)
                    pe.wait_ge(s_hk, e * 16 + 18)
                    for j in range(TT):
                        m = P if j < TT - 1 else LAST
                        pe.wait_ge(s_yk, e * TT + (j + 1))
                        for f in range(FC):
                            last = pe.matmul(p_y[j % 2][0:m, 0:C], hT[:, f, j * P:j * P + m], w2s[:, b, f, :], start=(f == 0), stop=(f == FC - 1))
                        last.then_inc(s_yp, 1)
                over_tiles(pe, 0, body, E_N)

            @block.scalar
            def _(a):
                a.wait_ge(s_b, 32)
                a.sem_inc(s_hk, 2)

                def body(e, b, h_):
                    a.wait_ge(s_hk, e * 16 + 2)
                    a.activation(b1c[:, :], b1s[:, bass.ds(e, 1), :].rearrange("p o f -> p (o f)"), ACT.Copy).then_inc(s_bc, 1)
                    a.wait_ge(s_bc, e + 1)
                    a.wait_ge(s_yp, e * TT + 2 * TT)
                    for f in range(FC):
                        for q, (lo, hi) in enumerate(halves):
                            a.wait_ge(s_hp, e * 16 + (2 * f + q + 1))
                            a.activation(hT[:, f, lo:hi], p_h[q][:, 0:hi - lo], ACT.Relu, bias=b1c[:, f:f + 1]).then_inc(s_hk, 1)
                over_tiles(a, 0, body, E_N)

            @block.vector
            def _(v):
                v.wait_ge(s_b, 32)
                v.engine_nop().then_inc(s_xk, 2)
                v.engine_nop().then_inc(s_yk, 2)

                def body(e, b, h_):
                    for k in range(KC):
                        for q in range(2):
                            n = 2 * k + q
                            v.wait_ge(s_xp, e * 4 + (n + 1))
                            v.tensor_copy(XT[:, k, halves[q][0]:halves[q][1]], p_x[n % 2][:, 0:halves[q][1] - halves[q][0]]).then_inc(s_xk, 1)
                    for j in range(TT):
                        m = P if j < TT - 1 else LAST
                        v.wait_ge(s_yp, e * TT + (j + 1 + 2 * TT))
                        if j == 0:
                            v.wait_ge(s_ysf, e + 1)
                        v.tensor_tensor(yo[0:m, b, j, :], p_y[j % 2][0:m, 0:C], b2s[0:m, bass.ds(e, 1), :].rearrange("p o c -> p (o c)"), ALU.add).then_inc(s_yk, 1)
                over_tiles(v, 0, body, E_N)


def combine(nc, y_dram, slot_i, coef, x1, out_dram):
    with ExitStack() as c:
        c.callback(nc.all_engine_barrier)
        def sb(n, s, t=F32):
            return c.enter_context(nc.sbuf_tensor("co_" + n, s, t))

        def sem(n):
            return c.enter_context(a_semaphore(nc, "co_" + n))
        rowi = [sb(f"rowi{b}", [T, 1], I32) for b in range(2)]
        y = [sb(f"y{b}", [T, C]) for b in range(2)]
        fine = sb("fine", [T, C], I32); up = sb("up", [T, C]); under = sb("under", [T, C]); down = sb("down", [T, C])
        o = [sb(f"o{b}", [T, C]) for b in range(2)]
        s_r = sem("rows_known"); s_g = [sem(f"gathered{b}") for b in range(2)]; s_dv = sem("dve"); s_o = sem("out_ready"); s_st = [sem(f"stored{b}") for b in range(2)]; s_go = sem("goes_on"); s_vgo = sem("dve_goes_on")
        with nc.Block() as block:
            @block.gpsimd
            def _(g):
                g.sem_inc(s_o, 2)

                def body(t, b, h_):
                    g.wait_ge(s_o, t + 1)
                    g.sem_inc(s_go, 1)
                    g.tensor_copy(rowi[b][:, :], slot_i[:, bass.ds(t, 1)]).then_inc(s_r, 1)
                    g.wait_ge(s_r, t + 1)
                    g.sem_inc(s_go, 1)
                    g.indirect_dma_start(out=y[b][:, :], out_offset=None, in_=y_dram,
                                         in_offset=bass.IndirectOffsetOnAxis(ap=rowi[b][:, 0:1], axis=0)).then_inc(s_g[b], 16)
                over_tiles(g, 0, body, NT)

            @block.vector
            def _(v):
                def body(t, b, h_):
                    ch = Chain(v, s_dv, t * 5)
                    v.wait_ge(s_g[b], h_ * 16 + 16)
                    ch.link(v.tensor_scalar(y[b][:, :], y[b][:, :], coef[:, bass.ds(t, 1)], None, ALU.mult))
                    v.tensor_scalar(up[:, :], y[b][:, :], F_MAX, 10000.0, ALU.is_gt, ALU.mult)
                    ch.link(v.tensor_scalar(under[:, :], y[b][:, :], F_MAX, None, ALU.is_le))
                    v.scalar_tensor_tensor(fine[:, :], y[b][:, :], -F_MAX, under[:, :], ALU.is_ge, ALU.mult)
                    ch.link(v.tensor_scalar(down[:, :], y[b][:, :], -F_MAX, -10000.0, ALU.is_lt, ALU.mult))
                    ch.link(v.tensor_tensor(up[:, :], up[:, :], down[:, :], ALU.add))
                    v.sem_inc(s_vgo, 1)
                    ch.link(v.copy_predicated(up[:, :], fine[:, :], y[b][:, :]))
                    v.wait_ge(s_st[b], h_ * 16 + 16)
                    v.tensor_tensor(o[b][:, :], up[:, :], x1[:, bass.ds(t, 1), :].rearrange("p o c -> p (o c)"), ALU.add).then_inc(s_o, 1)
                over_tiles(v, 0, body, NT)

            @block.sync
            def _(sp):
                for q in s_st:
                    sp.sem_inc(q, 16)

                def body(t, b, h_):
                    sp.wait_ge(s_o, t + 3)
                    sp.dma_start(out_dram[bass.ds(t * T, T), :], o[b][:, :]).then_inc(s_st[b], 16)
                over_tiles(sp, 0, body, NT)
                for q in s_st:
                    sp.wait_ge(q, 16 + 8 * NT)


def gps_layer(nc, x, src, dst, edge_weight, wqkvT, bqkv, wprojT, bproj, temperature, gate_w, gate_b, w1, b1p, w2, b2, out):
    def scratch(n, s):
        return nc.dram_tensor(n, s, F32, kind="Internal").ap()
    mT = scratch("rotationT", (C, C)); xT = scratch("xT_tiles", (NT, P, 2 * T)); mom = scratch("moments", (H, VW, FEAT))
    buf = scratch("expert_rows", (E_N * ROOM, C)); y = scratch("expert_out", (E_N * ROOM, C))
    with ExitStack() as ctx:
        ctx.callback(nc.all_engine_barrier)
        wr = Writes(nc, ctx, src.shape[0])
        with ExitStack() as c:
            c.callback(nc.all_engine_barrier)
            write_segments(nc, c, wr, src, dst, edge_weight)
        with nc.sbuf_tensor("xn", [T, NT, C], F32) as xn:
            layer_norm(nc, "l1_", None, xn, x, wr)
            transposed_tiles(nc, "t1_", xn, xT)
        moments(nc, xT, wqkvT, bqkv, mom, wr)
        rotation_matrix(nc, ctx, wr, mT)
    with ExitStack() as c:
        def sb(n, s, t=F32):
            return c.enter_context(nc.sbuf_tensor(n, s, t))
        x1 = sb("x1", [T, NT, C]); slot_i = sb("slot_i", [T, NT], I32); coef = sb("coef", [T, NT])
        attend(nc, xT, wqkvT, bqkv, temperature, wprojT, bproj, mom, mT, x, x1)
        with nc.sbuf_tensor("xn2", [T, NT, C], F32) as xn2:
            layer_norm(nc, "l2_", x1, xn2, None, None)
            transposed_tiles(nc, "t2_", xn2, xT)
            route(nc, xT, gate_w, gate_b, xn2, buf, slot_i, coef)
        experts(nc, buf, w1, b1p, w2, b2, y)
        combine(nc, y, slot_i, coef, x1, out)



def kernel(**inputs):
    import numpy as _np
    import concourse.bacc as _bacc
    from concourse import mybir as _mybir
    from concourse.bass_utils import run_bass_kernel_spmd as _run

    laid = {
        "x": inputs["x"], "src": inputs["src"], "dst": inputs["dst"], "edge_weight": inputs["edge_weight"],
        "wqkvT": inputs["L0_mix_Wqkv"].T, "bqkv": inputs["L0_mix_bqkv"],
        "wprojT": inputs["L0_mix_Wproj"].T, "bproj": inputs["L0_mix_bproj"],
        "temperature": inputs["L0_mix_temperature"].reshape(-1),
        "gate_w": inputs["L0_ffn_gate_w"], "gate_b": inputs["L0_ffn_gate_b"], "w1": inputs["L0_ffn_w1"],
        "b1p": inputs["L0_ffn_b1"].reshape(8, 8, 128).transpose(2, 0, 1),
        "w2": inputs["L0_ffn_w2"], "b2": inputs["L0_ffn_b2"],
    }
    nc = _bacc.Bacc("TRN2", target_bir_lowering=False, num_devices=1)
    arrays, args = {}, {}
    for name, value in laid.items():
        a = _np.ascontiguousarray(value)
        arrays[f"in_{name}"] = a
        args[name] = nc.dram_tensor(f"in_{name}", a.shape, _mybir.dt.from_np(a.dtype), kind="ExternalInput").ap()
    args["out"] = nc.dram_tensor("out_0_dram", (6250, 256), F32, kind="ExternalOutput").ap()
    gps_layer(nc, **args)
    r = _run(nc, [arrays], core_ids=[0])
    return r.results[0]["out_0_dram"]
```

```python
import math
from contextlib import ExitStack, contextmanager
import concourse.bass as bass
from concourse import mybir

F32 = mybir.dt.float32
I32 = mybir.dt.int32
ALU = mybir.AluOpType
ACT = mybir.ActivationFunctionType
AX = mybir.AxisListType

P = 128
D = 256
SEG = 125
NPAR = 8
Z, QO, QL, FS, FO, CO, SO, D1 = range(NPAR)
LEVELS = 7

TWO_PI_A = 6.28125
TWO_PI_B = 0.0019350051879882812
TWO_PI_C = 2 * math.pi - TWO_PI_A - TWO_PI_B
ROUND = 12582912.0
PI_IN = 3.1415925


@contextmanager
def a_semaphore(nc, name):
    held = nc.alloc_semaphore(name)
    yield held
    nc.clear_and_free_semaphores([held])


class Writes:

    def __init__(self, nc, ctx, steps):
        self.L = steps // SEG
        self.W = 2 * self.L
        self.NCH = -(-SEG * self.W // (P * (P - 1)))
        self.NB = self.NCH * P
        self.NPK = -(-(self.NB * (P - 1) + P) // P) * P
        self.segments = nc.dram_tensor("segments", (2, SEG, self.W), I32, kind="Internal").ap()
        self.packed = nc.dram_tensor("packed", (2, self.NPK), I32, kind="Internal").ap()
        self.GB = self.NB // next(n for n in (10, 8, 5, 4, 2) if self.NB % n == 0)
        self.ngroups = ctx.enter_context(nc.sbuf_tensor("ngroups", [1, 1], I32))
        self.nrun = ctx.enter_context(nc.sbuf_tensor("nrun", [1, 1], I32))
        self.ident = ctx.enter_context(nc.sbuf_tensor("ident", [P, P], F32))
        self.tot = ctx.enter_context(nc.sbuf_tensor("tot", [P, 1], F32))
        self.ones = ctx.enter_context(nc.sbuf_tensor("ones", [P, P], F32))
        self.base_i = ctx.enter_context(nc.sbuf_tensor("base_i", [1, SEG + 1], I32))
        self.s_packed = ctx.enter_context(a_semaphore(nc, "segment_packed"))
        self.s_order = ctx.enter_context(a_semaphore(nc, "segments_in_order"))

    def pack(self, sp, p):
        sp.wait_ge(self.s_packed, p * 16 + 16)
        sp.sem_inc(self.s_order, 1)
        at = sp.value_load(self.base_i[0:1, bass.ds(p, 1)], min_val=0, max_val=(SEG - 1) * self.W)
        sp.dma_start(self.packed[:, bass.ds(at + 1, self.W)],
                     self.segments[:, bass.ds(p, 1), :].rearrange("a o w -> a (o w)")).then_inc(self.s_packed, 16)


def write_segments(nc, ctx, wr, src, dst, ew):
    L, W, NPK, sc, pk = wr.L, wr.W, wr.NPK, wr.segments, wr.packed
    nrun, ident, tot, ones, base_i = wr.nrun, wr.ident, wr.tot, wr.ones, wr.base_i
    BITS = max(1, (W - 1).bit_length())
    assert BITS <= 12 and SEG * L == src.shape[0]

    def sem(n):
        return ctx.enter_context(a_semaphore(nc, n))

    with ExitStack() as c:
        def sb(n, s, t=F32):
            return c.enter_context(nc.sbuf_tensor(n, s, t))
        src_i = sb("src_i", [SEG, L], I32)
        dst_i = sb("dst_i", [SEG, L], I32)
        th = sb("th", [SEG, L])
        fi = sb("fi", [SEG, L]); fj = sb("fj", [SEG, L])
        va = sb("va", [SEG, L]); vb = sb("vb", [SEG, L]); pr = sb("pr", [SEG, L]); tmp = sb("tmp", [SEG, L])
        vw = sb("vw", [SEG, W]); kf = sb("kf", [SEG, W]); inc = sb("inc", [SEG, W]); slot = sb("slot", [SEG, W])
        ki = sb("ki", [SEG, W], I32); thw = sb("thw", [SEG, W], I32); bit = sb("bit", [SEG, W], I32)
        cleared = sb("cleared", [SEG, W], I32); zi = sb("zi", [P, max(W, NPK // P)], I32)
        tri = sb("tri", [SEG, SEG + 1]); groups_f = sb("groups_f", [1, 1])
        base_ps = c.enter_context(nc.psum_tensor("base_ps", [P, 512], F32))
        ld = sem("step_loads"); dv = sem("prep_dve"); tr = sem("tri_ready"); bs = sem("base_ps_ready")
        bi = sem("base_ready"); cz = sem("zeros_ready"); comp = sem("compressed"); so = sem("seg_stored"); pkd = sem("packed_zeroed")
        po = sem("pool_consts"); ths = sem("theta_copied"); counted = sem("counted")
        with nc.Block() as block:
            @block.sync
            def _(sp):
                sp.dma_start(src_i[:, :], src.rearrange("(p l) -> p l", l=L)).then_inc(ld, 16)
                sp.dma_start(dst_i[:, :], dst.rearrange("(p l) -> p l", l=L)).then_inc(ld, 16)
                sp.dma_start(th[:, :], ew.rearrange("(p l) -> p l", l=L)).then_inc(ld, 16)
                sp.wait_ge(cz, 1)
                for a in range(2):
                    sp.dma_start(pk[a].rearrange("(p l) -> p l", p=P), zi[:, 0:NPK // P]).then_inc(pkd, 16)
                sp.wait_ge(pkd, 32)
                sp.wait_ge(comp, 1)
                sp.dma_start(sc[0], ki[:, :]).then_inc(so, 16)
                sp.dma_start(sc[1], thw[:, :]).then_inc(so, 16)
                sp.wait_ge(so, 32)
                sp.sem_inc(wr.s_packed, 16)

            @block.gpsimd
            def _(g):
                g.memset(zi[:, :], 0).then_inc(cz, 1)
                g.memset(ones[:, :], 1.0).then_inc(po, 1)
                g.memset(ident[:, :], 0.0).then_inc(po, 1)
                g.memset(tri[:, :], 1.0).then_inc(po, 1)
                g.iota(slot[:, :], pattern=[[1, W]], base=1, channel_multiplier=0, allow_small_or_imprecise_dtypes=True).then_inc(po, 1)
                g.wait_ge(po, 4)
                g.affine_select(out=ident[:, :], in_=ident[:, :], compare_op=ALU.not_equal, fill=1.0,
                                base=0, pattern=[[-1, P]], channel_multiplier=1).then_inc(po, 1)
                g.affine_select(out=tri[:, :], in_=tri[:, :], compare_op=ALU.is_gt, fill=0.0,
                                base=0, pattern=[[1, SEG + 1]], channel_multiplier=-1).then_inc(tr, 1)

            @block.scalar
            def _(a):
                a.wait_ge(ld, 48)
                v = thw[:, :].bitcast(F32).rearrange("p (l o) -> p l o", o=2)
                a.activation(v[:, :, 0], th[:, :], ACT.Copy).then_inc(ths, 1)
                a.activation(v[:, :, 1], th[:, :], ACT.Copy).then_inc(ths, 1)

            @block.vector
            def _(v):
                n = [0]

                def link(ins):
                    n[0] += 1
                    ins.then_inc(dv, 1)
                    v.wait_ge(dv, n[0])
                v.wait_ge(ld, 48)
                vw2 = vw[:, :].rearrange("p (l o) -> p l o", o=2)
                kf2 = kf[:, :].rearrange("p (l o) -> p l o", o=2)
                v.tensor_copy(fi[:, :], src_i[:, :])
                link(v.tensor_copy(fj[:, :], dst_i[:, :]))
                v.tensor_scalar(va[:, :], fi[:, :], float(D), None, ALU.is_lt)
                link(v.tensor_scalar(vb[:, :], fj[:, :], float(D), None, ALU.is_lt))
                v.tensor_scalar(fi[:, :], fi[:, :], float(D - 1), None, ALU.min)
                link(v.tensor_scalar(fj[:, :], fj[:, :], float(D - 1), None, ALU.min))
                link(v.tensor_tensor(tmp[:, :], fi[:, :], fj[:, :], ALU.is_equal))
                link(v.tensor_tensor(tmp[:, :], tmp[:, :], vb[:, :], ALU.mult))
                link(v.tensor_scalar(tmp[:, :], tmp[:, :], -1.0, 1.0, ALU.mult, ALU.add))
                link(v.tensor_tensor(va[:, :], va[:, :], tmp[:, :], ALU.mult))
                v.tensor_copy(vw2[:, :, 0], va[:, :])
                v.tensor_copy(vw2[:, :, 1], vb[:, :])
                link(v.tensor_tensor(pr[:, :], va[:, :], vb[:, :], ALU.mult))
                v.scalar_tensor_tensor(kf2[:, :, 0], fj[:, :], float(D), fi[:, :], ALU.mult, ALU.add)
                v.tensor_scalar(pr[:, :], pr[:, :], 65536.0, 131072.0, ALU.mult, ALU.add)
                link(v.scalar_tensor_tensor(tmp[:, :], fi[:, :], float(D), fj[:, :], ALU.mult, ALU.add))
                link(v.tensor_tensor(kf2[:, :, 1], tmp[:, :], pr[:, :], ALU.add))
                v.wait_ge(cz, 1)
                link(v.tensor_tensor_scan(inc[:, :], vw[:, :], zi[0:SEG, 0:W].bitcast(F32), 0.0, ALU.add, ALU.add))
                v.engine_nop().then_inc(counted, 1)
                v.wait_ge(po, 4)
                link(v.tensor_tensor(slot[:, :], slot[:, :], inc[:, :], ALU.subtract))
                link(v.tensor_tensor(slot[:, :], slot[:, :], vw[:, :], ALU.mult))
                v.tensor_copy(ki[:, :], kf[:, :])
                link(v.tensor_copy(bit[:, :], slot[:, :]))
                link(v.tensor_scalar(bit[:, :], bit[:, :], 18, None, ALU.logical_shift_left))
                link(v.tensor_tensor(ki[:, :], ki[:, :], bit[:, :], ALU.bitwise_or))
                v.wait_ge(ths, 2)
                for b in range(BITS):
                    s = 1 << b
                    v.tensor_scalar(bit[:, :], ki[:, :], 1 << (18 + b), None, ALU.bitwise_and)
                    link(v.tensor_scalar(cleared[:, :], ki[:, :], ~(1 << (18 + b)), None, ALU.bitwise_and))
                    link(v.copy_predicated(ki[:, :], bit[:, :], zi[0:SEG, 0:W]))
                    v.copy_predicated(ki[:, 0:W - s], bit[:, s:W], cleared[:, s:W])
                    link(v.copy_predicated(thw[:, 0:W - s], bit[:, s:W], thw[:, s:W]))
                v.engine_nop().then_inc(comp, 1)
                v.wait_ge(bs, 1)
                v.tensor_copy(base_i[:, :], base_ps[0:1, 0:SEG + 1])
                link(v.tensor_copy(tot[:, :], base_ps[:, 256:257]))
                v.engine_nop().then_inc(bi, 1)
                link(v.tensor_scalar(nrun[:, :], base_ps[0:1, SEG:SEG + 1], 1.0 / (2 * (P - 1)), 1.0, ALU.mult, ALU.add))
                group = (P - 1) * wr.GB
                link(v.tensor_scalar(groups_f[:, :], base_ps[0:1, SEG:SEG + 1], 1.0 / group, 5.0 * (P - 1) / group + 1.0, ALU.mult, ALU.add))
                link(v.tensor_scalar(wr.ngroups[:, :], groups_f[:, :], float(wr.NB // wr.GB), None, ALU.min))

            @block.tensor
            def _(pe):
                pe.wait_ge(counted, 1)
                pe.wait_ge(tr, 1)
                pe.wait_ge(po, 1)
                pe.matmul(base_ps[0:1, 0:SEG + 1], inc[:, W - 1:W], tri[:, :], start=True, stop=True)
                pe.matmul(base_ps[:, 256:257], ones[0:SEG, :], inc[:, W - 1:W], start=True, stop=True).then_inc(bs, 1)


def rotation_matrix(nc, ctx, wr, mT_out, zeroed):
    B = P - 1
    NCH, NB, NPK, pk = wr.NCH, wr.NB, wr.NPK, wr.packed
    nrun, ident, tot, ones = wr.nrun, wr.ident, wr.tot, wr.ones

    def sem(n):
        return ctx.enter_context(a_semaphore(nc, n))

    keep_ctx = ExitStack()
    par = keep_ctx.enter_context(nc.sbuf_tensor("par", [P, NB + 2, NPAR], F32))
    with ExitStack() as c0:
      kt = c0.enter_context(nc.sbuf_tensor("kt", [P, NB], I32))
      tt = c0.enter_context(nc.sbuf_tensor("tt", [P, NB], F32))
      with ExitStack() as c:
          def sb(n, s, t=F32):
              return c.enter_context(nc.sbuf_tensor(n, s, t))
          E = P + 1
          kb = sb("kb", [P, NCH, E], I32)
          tb = sb("tb", [P, NCH, E])
          kbf = sb("kbf", [P, NCH, E]); posn = sb("posn", [P, NCH, E]); inr = sb("inr", [P, NCH, E]); pfl = sb("pfl", [P, NCH, 2])
          psk = [c.enter_context(nc.psum_tensor(f"psk{i}", [P, 512], F32)) for i in range(2)]
          pst = [c.enter_context(nc.psum_tensor(f"pst{i}", [P, 512], F32)) for i in range(2)]
          ld = sem("packed_loads"); kr = sem("keys_float"); tp = sem("transposed"); ev = sem("columns_kept")
          dv = sem("cols_dve"); io = sem("cols_iota")

          def overlapped(a):
              return bass.AP(tensor=pk.tensor, offset=a * NPK, ap=[[B, P], [P * B, NCH], [1, E]])

          with nc.Block() as block:
              @block.sync
              def _(sp):
                  sp.wait_ge(wr.s_packed, SEG * 16 + 16)
                  sp.dma_start(kb[:, :, :], overlapped(0)).then_inc(ld, 16)
                  sp.dma_start(tb[:, :, :].bitcast(I32), overlapped(1)).then_inc(ld, 16)

              @block.gpsimd
              def _(g):
                  g.iota(posn[:, :, :], pattern=[[P * B, NCH], [1, E]], base=-1, channel_multiplier=B, allow_small_or_imprecise_dtypes=True).then_inc(io, 1)

              @block.tensor
              def _(pe):
                  pe.wait_ge(kr, 1)
                  pe.wait_ge(ld, 32)
                  for q in range(0, NCH, 4):
                      m = min(4, NCH - q)
                      b = (q // 4) % 2
                      if q >= 8:
                          pe.wait_ge(ev, 2 * (q // 4) - 2)
                      for j in range(m):
                          pe.transpose(psk[b][:, j * P:(j + 1) * P], kbf[:, q + j, 0:P], ident[:, :])
                          last = pe.transpose(pst[b][:, j * P:(j + 1) * P], tb[:, q + j, 0:P], ident[:, :])
                      last.then_inc(tp, 1)

              @block.vector
              def _(v):
                  n = [0]

                  def link(ins):
                      n[0] += 1
                      ins.then_inc(dv, 1)
                      v.wait_ge(dv, n[0])
                  v.wait_ge(ld, 32)
                  link(v.tensor_scalar(kb[:, :, :], kb[:, :, :], (1 << 18) - 1, None, ALU.bitwise_and))
                  link(v.tensor_copy(kbf[:, :, :], kb[:, :, :]))
                  v.wait_ge(io, 1)
                  link(v.tensor_scalar(inr[:, :, :], posn[:, :, :], tot[:, 0:1], None, ALU.is_lt))
                  link(v.tensor_tensor(kbf[:, :, :], kbf[:, :, :], inr[:, :, :], ALU.mult))
                  link(v.tensor_copy(kb[:, :, :], kbf[:, :, :]))
                  link(v.tensor_scalar(kb[:, :, :], kb[:, :, :], 1 << 16, None, ALU.bitwise_and))
                  link(v.tensor_copy(pfl[:, :, 0], kb[:, :, 1]))
                  link(v.tensor_copy(pfl[:, :, 1], kb[:, :, P]))
                  link(v.tensor_scalar(inr[:, :, :], inr[:, :, :], -262144.0, 262144.0, ALU.mult, ALU.add))
                  link(v.tensor_scalar(inr[:, :, 0], pfl[:, :, 0], -4.0, 262144.0, ALU.mult, ALU.add))
                  link(v.scalar_tensor_tensor(inr[:, :, B], pfl[:, :, 1], 4.0, inr[:, :, B], ALU.mult, ALU.add))
                  v.tensor_tensor(kbf[:, :, :], kbf[:, :, :], inr[:, :, :], ALU.add).then_inc(kr, 1)
                  for q in range(0, NCH, 4):
                      m = min(4, NCH - q)
                      b = (q // 4) % 2
                      v.wait_ge(tp, q // 4 + 1)
                      v.tensor_copy(kt[:, q * P:(q + m) * P], psk[b][:, 0:m * P]).then_inc(ev, 1)
                      v.tensor_copy(tt[:, q * P:(q + m) * P], pst[b][:, 0:m * P]).then_inc(ev, 1)
                  v.wait_ge(ev, 2 * -(-NCH // 4))
      with ExitStack() as c:
          def sb(n, s, t=F32):
              return c.enter_context(nc.sbuf_tensor(n, s, t))
          GB = wr.GB
          w1 = sb("w1", [P, GB]); w2 = sb("w2", [P, GB]); vl = sb("vl", [P, GB]); sgn = sb("sgn", [P, GB])
          tg = sb("angle", [P, GB]); wi = sb("wi", [P, GB], I32)
          n1 = sb("n1", [P, 1]); halfpi = sb("halfpi", [P, 1])
          dv = sem("par_dve"); io = sem("par_consts"); ang = sem("angles"); tri_s = sem("sincos")
          with nc.Block() as block:
              @block.gpsimd
              def _(g):
                  g.iota(n1[:, :], pattern=[[0, 1]], base=1, channel_multiplier=1, allow_small_or_imprecise_dtypes=True).then_inc(io, 1)
                  g.memset(halfpi[:, :], math.pi / 2).then_inc(io, 1)
                  g.memset(par[:, NB:NB + 2, :], 0.0).then_inc(io, 1)
                  g.wait_ge(io, 3)
                  g.memset(par[:, NB:NB + 2, Z:Z + 1], -1.0).then_inc(io, 1)
                  g.wait_ge(io, 4)

              @block.scalar
              def _(a):
                  a.wait_ge(io, 2)
                  cnt = a.value_load(wr.ngroups[0:1, 0:1], min_val=1, max_val=NB // GB)
                  with a.Fori(0, cnt) as q:
                      a.wait_ge(ang, q * 2 + 1)
                      a.activation(w2[:, :], tg[:, :], ACT.Sin).then_inc(tri_s, 1)
                      a.wait_ge(ang, q * 2 + 2)
                      a.wait_ge(tri_s, q * 2 + 1)
                      a.activation(tg[:, :], sgn[:, :], ACT.Sin, bias=halfpi[:, :], scale=-1.0).then_inc(tri_s, 1)

              @block.vector
              def _(v):
                  def link(ins):
                      n[0] += 1
                      ins.then_inc(dv, 1)
                      v.wait_ge(dv, q * STEPS + n[0])
                  v.wait_ge(io, 2)
                  STEPS = 26
                  cnt = v.value_load(wr.ngroups[0:1, 0:1], min_val=1, max_val=NB // GB)
                  with v.Fori(0, cnt) as q:
                      n = [0]
                      keys = kt[:, bass.ds(q * GB, GB)]

                      def PA(number):
                          return par[:, bass.ds(q * GB, GB), number:number + 1].rearrange("p b o -> p (b o)")
                      link(v.tensor_copy(tg[:, :], tt[:, bass.ds(q * GB, GB)]))
                      link(v.tensor_scalar(wi[:, :], keys, 18, None, ALU.logical_shift_right))
                      link(v.tensor_copy(vl[:, :], wi[:, :]))
                      link(v.tensor_scalar(vl[:, :], vl[:, :], -1.0, 1.0, ALU.mult, ALU.add))
                      link(v.tensor_scalar(w1[:, :], tg[:, :], 1.0 / (2 * math.pi), ROUND, ALU.mult, ALU.add))
                      link(v.tensor_scalar(w1[:, :], w1[:, :], ROUND, None, ALU.subtract))
                      for part in (TWO_PI_A, TWO_PI_B, TWO_PI_C):
                          link(v.scalar_tensor_tensor(tg[:, :], w1[:, :], -part, tg[:, :], ALU.mult, ALU.add))
                      link(v.tensor_scalar(tg[:, :], tg[:, :], PI_IN, -PI_IN, ALU.min, ALU.max))
                      v.sem_inc(ang, 1)
                      v.wait_ge(ang, q * 2 + 1)
                      link(v.tensor_scalar(sgn[:, :], tg[:, :], -1.0, None, ALU.mult))
                      link(v.tensor_tensor(sgn[:, :], sgn[:, :], tg[:, :], ALU.max))
                      v.sem_inc(ang, 1)
                      v.wait_ge(tri_s, q * 2 + 2)
                      v.tensor_tensor(PA(CO), tg[:, :], vl[:, :], ALU.mult)
                      link(v.tensor_tensor(w2[:, :], w2[:, :], vl[:, :], ALU.mult))
                      link(v.tensor_scalar(wi[:, :], keys, 17, 1, ALU.logical_shift_right, ALU.bitwise_and))
                      link(v.tensor_copy(sgn[:, :], wi[:, :]))
                      link(v.tensor_scalar(sgn[:, :], sgn[:, :], 2.0, -1.0, ALU.mult, ALU.add))
                      v.tensor_tensor(PA(SO), w2[:, :], sgn[:, :], ALU.mult)
                      link(v.tensor_scalar(wi[:, :], keys, D - 1, None, ALU.bitwise_and))
                      link(v.tensor_copy(w1[:, :], wi[:, :]))
                      v.tensor_scalar(PA(FS), w1[:, :], float(D), None, ALU.mult)
                      v.tensor_scalar(PA(QL), w1[:, :], float(D), float(D - 1), ALU.mult, ALU.add)
                      v.scalar_tensor_tensor(PA(D1), w1[:, :], 1.0, vl[:, :], ALU.add, ALU.mult)
                      link(v.tensor_scalar(tg[:, :], w1[:, :], float(D), n1[:, 0:1], ALU.mult, ALU.add))
                      link(v.scalar_tensor_tensor(tg[:, :], tg[:, :], 1.0, vl[:, :], ALU.add, ALU.mult))
                      v.tensor_scalar(PA(Z), tg[:, :], -1.0, None, ALU.add)
                      link(v.tensor_scalar(wi[:, :], keys, 8, D - 1, ALU.logical_shift_right, ALU.bitwise_and))
                      link(v.tensor_copy(w1[:, :], wi[:, :]))
                      v.tensor_scalar(PA(FO), w1[:, :], float(D), None, ALU.mult)
                      link(v.tensor_scalar(w2[:, :], w1[:, :], float(D), n1[:, 0:1], ALU.mult, ALU.add))
                      link(v.tensor_scalar(wi[:, :], keys, 16, 1, ALU.logical_shift_right, ALU.bitwise_and))
                      link(v.tensor_copy(w1[:, :], wi[:, :]))
                      link(v.tensor_tensor(PA(QO), w2[:, :], w1[:, :], ALU.subtract))

                      assert n[0] == STEPS

    with ExitStack() as c:
        def sb(n, s, t=F32):
            return c.enter_context(nc.sbuf_tensor(n, s, t))

        def ps(n):
            return c.enter_context(nc.psum_tensor(n, [P, 512], F32))
        X2 = range(2)
        parn = sb("parn", [P, 2, NPAR])
        nxt = sb("nxt", [P, 2, 5]); cur = sb("cur", [P, 2, 5])
        zd = sb("zd", [P, 2, P]); zx = sb("zx", [P, 2, P])
        q3 = sb("q3", [P, 3, P]); pred = sb("pred", [P, 3])
        e1 = sb("e1", [P, P]); e2 = sb("e2", [P, P])
        rowk = sb("rowk", [P, D]); row1 = sb("row1", [P, D])
        NN = [sb(f"N{x}", [P, P]) for x in X2]
        NI = [sb(f"NI{x}", [P, P]) for x in X2]
        NT = [sb(f"NT{x}", [P, P]) for x in X2]
        PQ = [[sb(f"PQ{x}{h}", [P, 2, P]) for h in range(2)] for x in X2]
        ST = [sb(f"ST{x}", [P, P]) for x in X2]
        RR = [sb(f"R{x}", [P, D]) for x in X2]
        r1 = sb("r1", [P, D]); r2 = sb("r2", [P, D])
        FT = [sb(f"FT{x}", [P, D]) for x in X2]
        WT = sb("WT", [P, 2, 2, P])
        M = sb("M", [P, 2, D]); V = sb("V", [P, D + 1]); kp = sb("kp", [P, 2])
        pq = [ps(f"pq{x}") for x in X2]
        pst = [ps(f"pss{x}") for x in X2]
        pv = ps("pv"); pd = [ps(f"pd{r}") for r in range(2)]; pw = ps("pw")
        s_nt = sem("nt_in_psum"); s_sp = sem("st_in_psum"); s_lv = sem("level_in_psum"); s_zr = sem("zrow_in_psum"); s_v = sem("v_in_psum")
        s_dl = sem("delta_in_psum"); s_wt = sem("wt_in_psum")
        s_q = sem("q_kept"); s_st = sem("st_kept"); s_zx = sem("zrow_kept"); s_wts = sem("wt_kept")
        s_p = [sem(f"pq_kept{x}") for x in X2]; s_vs = sem("v_kept"); s_m = sem("m_updated"); s_keep = sem("keep_ready")
        s_setup = sem("n_ready"); s_dc = sem("loop_dve"); s_par = sem("par_loaded"); s_cur = sem("cur_ready")
        s_zd = sem("zdiag_ready"); s_R = sem("r_ready"); s_FT = sem("ft_ready"); s_gc = sem("loop_pool")
        s_c = sem("loop_consts"); s_go = sem("pool_goes_on"); s_fin = sem("mt_in_psum"); s_mo = sem("mt_kept"); s_out = sem("mt_stored")
        mt = sb("mt", [P, 2, D])
        zeroed_w = math.prod(zeroed.shape) // (4 * P)
        zeroed_rows = bass.AP(tensor=zeroed.tensor, offset=0, ap=[[4 * zeroed_w, P], [1, 4 * zeroed_w]])
        zero = sb("zero", [P, zeroed_w]); s_zero = sem("zeros"); s_zeroed = sem("dram_zeroed")
        with nc.Block() as block:
            @block.gpsimd
            def _(g):
                g.memset(zero[:, :], 0.0).then_inc(s_zero, 1)
                g.iota(rowk[:, :], pattern=[[D, D]], base=0, channel_multiplier=0, allow_small_or_imprecise_dtypes=True).then_inc(s_c, 1)
                g.iota(row1[:, :], pattern=[[1, D]], base=1, channel_multiplier=0, allow_small_or_imprecise_dtypes=True).then_inc(s_c, 1)
                g.memset(M[:, :, :], 0.0).then_inc(s_c, 1)
                g.wait_ge(s_c, 3)
                for k in range(2):
                    g.tensor_copy(M[:, k, k * P:(k + 1) * P], ident[:, :]).then_inc(s_c, 1)
                g.wait_ge(s_c, 5)
                g.memset(V[:, D:D + 1], 1.0).then_inc(s_c, 1)
                g.memset(WT[:, :, :, :], 0.0).then_inc(s_wts, 1)
                for x in X2:
                    g.memset(FT[x][:, :], 0.0).then_inc(s_FT, 1)
                g.engine_nop().then_inc(s_m, 1)
                g.tensor_copy(parn[:, :, :], par[:, 0:2, :]).then_inc(s_par, 1)
                g.wait_ge(s_par, 1)
                for x in X2:
                    g.tensor_scalar(zd[:, x, :], ident[:, :], parn[:, x, Z:Z + 1], None, ALU.mult).then_inc(s_zd, 1)
                cnt = g.value_load(nrun[0:1, 0:1], min_val=1, max_val=NB // 2)
                with g.Fori(0, cnt) as i:
                    g.wait_ge(s_setup, i * 2 + 2); g.sem_inc(s_go, 1)
                    g.tensor_copy(cur[:, :, :], nxt[:, :, :]).then_inc(s_cur, 1)
                    g.tensor_copy(parn[:, :, :], par[:, bass.ds(i * 2 + 2, 2), :]).then_inc(s_par, 1)
                    g.wait_ge(s_cur, i + 1)
                    g.wait_ge(s_par, i + 2)
                    g.wait_ge(s_zr, i + 1); g.sem_inc(s_go, 1)
                    for x in X2:
                        g.tensor_scalar(zd[:, x, :], ident[:, :], parn[:, x, Z:Z + 1], None, ALU.mult).then_inc(s_zd, 1)
                    g.wait_ge(s_wts, i + 1); g.sem_inc(s_go, 1)
                    for x in X2:
                        g.tensor_scalar(r1[:, :], rowk[:, :], cur[:, x, 0:1], cur[:, x, 2:3], ALU.is_equal, ALU.mult).then_inc(s_gc, 1)
                        g.tensor_scalar(r2[:, :], rowk[:, :], cur[:, x, 1:2], cur[:, x, 3:4], ALU.is_equal, ALU.mult).then_inc(s_gc, 1)
                        g.wait_ge(s_gc, i * 4 + 2 * x + 2); g.sem_inc(s_go, 1)
                        g.tensor_tensor(RR[x][:, :], r1[:, :], r2[:, :], ALU.add).then_inc(s_R, 1)
                        g.wait_ge(s_R, i * 2 + x + 1); g.sem_inc(s_go, 1)
                    for x in X2:
                        g.wait_ge(s_dl, i * 2 + (x + 1)); g.sem_inc(s_go, 1)
                        g.tensor_scalar(FT[x][:, :], row1[:, :], cur[:, x, 4:5], None, ALU.is_equal).then_inc(s_FT, 1)
                    g.wait_ge(s_FT, i * 2 + 4); g.sem_inc(s_go, 1)

            def chain_v(pe, x, i):
                i2 = i * 2
                pe.wait_ge(s_m, i2 + (x + 1))
                pe.wait_ge(s_wts, i + 1)
                pe.matmul(pv[:, 0:D], WT[:, x, 0, :], M[:, 0, :], start=True, stop=False)
                pe.matmul(pv[:, 0:D], WT[:, x, 1, :], M[:, 1, :], start=False, stop=True).then_inc(s_v, 1)

            def chain_d(pe, x, i):
                i2 = i * 2
                pe.wait_ge(s_vs, i2 + (x + 1))
                pe.wait_ge(s_FT, i2 + (x + 1))
                for r in range(2):
                    last = pe.matmul(pd[r][:, 0:D + 1], FT[x][:, r * P:(r + 1) * P], V[:, :], start=True, stop=True)
                last.then_inc(s_dl, 1)

            @block.tensor
            def _(pe):
                def zrow(i):
                    pe.wait_ge(s_zd, i * 2 + 2)
                    pe.matmul(pv[:, D:2 * D], ones[:, :], zd[:, :, :].rearrange("p a b -> p (a b)"), start=True, stop=True).then_inc(s_zr, 1)

                def n_transposed(x):
                    pe.transpose(pq[x][:, 0:P], NN[x][:, :], ident[:, :]).then_inc(s_nt, 1)

                def st_begun(x):
                    pe.transpose(pst[x][:, 0:P], NI[x][:, :], ident[:, :]).then_inc(s_sp, 1)
                pe.wait_ge(s_c, 6)
                zrow(0)
                cnt = pe.value_load(nrun[0:1, 0:1], min_val=1, max_val=NB // 2)
                for x in X2:
                    pe.wait_ge(s_setup, x + 1)
                    n_transposed(x)
                for x in X2:
                    st_begun(x)
                with pe.Fori(0, cnt) as i:
                    for k in range(LEVELS):
                        for x in X2:
                            if k == 0:
                                pe.wait_ge(s_q, i * 2 + (x + 1))
                                pw_k, qw_k = NN[x][:, :], NT[x][:, :]
                            else:
                                pe.wait_ge(s_p[x], i * (LEVELS - 1) + k)
                                pw_k, qw_k = PQ[x][k % 2][:, 0, :], PQ[x][k % 2][:, 1, :]
                            if k < LEVELS - 1:
                                last = pe.matmul(pq[x][:, 0:P], qw_k, pw_k, start=True, stop=True)
                                if k < LEVELS - 2:
                                    last = pe.matmul(pq[x][:, P:2 * P], pw_k, qw_k, start=True, stop=True)
                                last.then_inc(s_lv, 1)
                            if k:
                                pe.wait_ge(s_st, i * 14 + (2 * (k - 1) + x + 1))
                                pe.matmul(pst[x][:, 0:P], pw_k, ST[x][:, :], start=False, stop=True, skip_group_check=True).then_inc(s_sp, 1)
                        if k == 0:
                            pe.wait_ge(s_zx, i + 1)
                            zrow(i + 1)
                            chain_v(pe, 0, i)
                        if k == 1:
                            chain_d(pe, 0, i)
                        if k == 3:
                            pe.wait_ge(s_zx, i + 2)
                            chain_v(pe, 1, i)
                        if k == 4:
                            chain_d(pe, 1, i)
                    for x in X2:
                        pe.wait_ge(s_setup, i * 2 + (x + 3))
                        n_transposed(x)
                    for x in X2:
                        pe.wait_ge(s_st, i * 14 + (12 + x + 1))
                        pe.wait_ge(s_R, i * 2 + (x + 1))
                        for r in range(2):
                            last = pe.matmul(pw[:, x * D + r * P:x * D + (r + 1) * P], RR[x][:, r * P:(r + 1) * P], ST[x][:, :], start=True, stop=True)
                    last.then_inc(s_wt, 1)
                    for x in X2:
                        st_begun(x)
                for x in X2:
                    chain_v(pe, x, cnt)
                    chain_d(pe, x, cnt)
                pe.wait_ge(s_m, cnt * 2 + 3)
                for a in range(2):
                    for b in range(2):
                        last = pe.transpose(pd[a][:, b * P:(b + 1) * P], M[:, b, a * P:(a + 1) * P], ident[:, :])
                last.then_inc(s_fin, 1)

            @block.scalar
            def _(a):
                def v_kept(a, x, i2):
                    a.wait_ge(s_v, i2 + (x + 1))
                    a.activation(V[:, 0:D], pv[:, 0:D], ACT.Copy).then_inc(s_vs, 1)

                def zrow_kept():
                    a.activation(zx[:, :, :].rearrange("p a b -> p (a b)"), pv[:, D:2 * D], ACT.Copy).then_inc(s_zx, 1)

                def nt_kept(x):
                    a.activation(NT[x][:, :], pq[x][:, 0:P], ACT.Copy).then_inc(s_q, 1)
                a.wait_ge(s_zr, 1)
                zrow_kept()
                cnt = a.value_load(nrun[0:1, 0:1], min_val=1, max_val=NB // 2)
                for x in X2:
                    a.wait_ge(s_nt, x + 1)
                    nt_kept(x)
                with a.Fori(0, cnt) as i:
                    for k in range(LEVELS):
                        for x in X2:
                            if k < LEVELS - 1:
                                a.wait_ge(s_lv, i * 12 + (2 * k + x + 1))
                                w = 2 if k < LEVELS - 2 else 1
                                a.activation(PQ[x][(k + 1) % 2][:, 0:w, :].rearrange("p a b -> p (a b)"), pq[x][:, 0:w * P], ACT.Copy).then_inc(s_p[x], 1)
                            a.wait_ge(s_sp, i * 14 + (2 * k + x + 1))
                            a.activation(ST[x][:, :], pst[x][:, 0:P], ACT.Copy).then_inc(s_st, 1)
                        if k == 0:
                            v_kept(a, 0, i * 2)
                            a.wait_ge(s_zr, i + 2)
                            a.wait_ge(s_setup, i * 2 + 2)
                            zrow_kept()
                        if k == 3:
                            v_kept(a, 1, i * 2)
                    for x in X2:
                        a.wait_ge(s_nt, i * 2 + (x + 3))
                        nt_kept(x)
                    a.wait_ge(s_wt, i + 1)
                    a.wait_ge(s_v, i * 2 + 2)
                    a.activation(WT[:, :, :, :].rearrange("p x a b -> p (x a b)"), pw[:, :], ACT.Copy).then_inc(s_wts, 1)
                for x in X2:
                    v_kept(a, x, cnt * 2)

            @block.vector
            def _(v):
                def found(x, base):
                    zrow = zx[:, x, :]
                    for k, q in enumerate((Z, QO, QL)):
                        last = v.scalar_tensor_tensor(q3[:, k, :], zrow, parn[:, x, q:q + 1], zrow, ALU.is_lt, ALU.mult)
                    last.then_inc(s_dc, 1)
                    v.wait_ge(s_dc, base + (5 * x + 1))
                    v.tensor_reduce(pred[:, :], q3[:, :, :], AX.X, ALU.max).then_inc(s_dc, 1)
                    v.wait_ge(s_dc, base + (5 * x + 2))
                    v.tensor_tensor(nxt[:, x, 0:2], pred[:, 0:2], parn[:, x, FS:FO + 1], ALU.max)
                    v.tensor_copy(nxt[:, x, 2:4], parn[:, x, CO:SO + 1])
                    v.tensor_scalar(nxt[:, x, 4:5], pred[:, 2:3], parn[:, x, Z:Z + 1], parn[:, x, D1:D1 + 1], ALU.is_equal, ALU.mult).then_inc(s_dc, 1)

                def matrix(x, base):
                    zrow = zx[:, x, :]
                    v.wait_ge(s_dc, base + (5 * x + 3))
                    v.tensor_scalar(e1[:, :], zrow, nxt[:, x, 0:1], nxt[:, x, 2:3], ALU.is_equal, ALU.mult)
                    v.tensor_scalar(e2[:, :], zrow, nxt[:, x, 1:2], nxt[:, x, 3:4], ALU.is_equal, ALU.mult).then_inc(s_dc, 1)
                    v.wait_ge(s_dc, base + (5 * x + 4))
                    v.tensor_tensor(NN[x][:, :], e1[:, :], e2[:, :], ALU.add).then_inc(s_dc, 1)
                    v.wait_ge(s_dc, base + (5 * x + 5))
                    v.tensor_tensor(NI[x][:, :], NN[x][:, :], ident[:, :], ALU.add).then_inc(s_setup, 1)

                def m_update(x, i2):
                    v.wait_ge(s_dl, i2 + (x + 1))
                    for r in range(2):
                        last = v.tensor_scalar(kp[:, r:r + 1], pd[r][:, D:D + 1], -1.0, 1.0, ALU.mult, ALU.add)
                    last.then_inc(s_keep, 1)
                    v.wait_ge(s_keep, i2 + (x + 1))
                    for r in range(2):
                        last = v.scalar_tensor_tensor(M[:, r, :], M[:, r, :], kp[:, r:r + 1], pd[r][:, 0:D], ALU.mult, ALU.add)
                    last.then_inc(s_m, 1)

                v.wait_ge(s_c, 5)
                v.wait_ge(s_par, 1)
                v.wait_ge(s_zx, 1)
                for x in X2:
                    found(x, 0)
                    matrix(x, 0)
                cnt = v.value_load(nrun[0:1, 0:1], min_val=1, max_val=NB // 2)
                with v.Fori(0, cnt) as i:
                    v.wait_ge(s_lv, i * 12 + 1)
                    v.wait_ge(s_zx, i + 2)
                    v.wait_ge(s_par, i + 2)
                    v.wait_ge(s_cur, i + 1)
                    found(0, i * 10 + 10)
                    m_update(0, i * 2)
                    matrix(0, i * 10 + 10)
                    found(1, i * 10 + 10)
                    v.wait_ge(s_lv, i * 12 + 2)
                    matrix(1, i * 10 + 10)
                    m_update(1, i * 2)
                for x in X2:
                    m_update(x, cnt * 2)
                v.wait_ge(s_fin, 1)
                for a in range(2):
                    v.tensor_copy(mt[:, a, :], pd[a][:, 0:D]).then_inc(s_mo, 1)

            @block.sync
            def _(sp):
                sp.wait_ge(s_zero, 1)
                for k in range(4):
                    sp.dma_start(zeroed_rows[:, k * zeroed_w:(k + 1) * zeroed_w], zero[:, :]).then_inc(s_zeroed, 16)
                sp.wait_ge(s_zeroed, 64)
                sp.wait_ge(s_mo, 2)
                sp.dma_start(mT_out.rearrange("(a p) c -> p a c", p=P), mt[:, :, :]).then_inc(s_out, 16)
                sp.wait_ge(s_out, 16)
    keep_ctx.close()

def dram_rows(ap1d, parts, n, at=0):
    return bass.AP(tensor=ap1d.tensor, offset=at, ap=[[0, parts], [1, n]])


class Chain:

    def __init__(self, eng, sem, base=0):
        self.eng, self.sem, self.base, self.n = eng, sem, base, 0

    def link(self, ins):
        self.n += 1
        ins.then_inc(self.sem, 1)
        self.eng.wait_ge(self.sem, self.base + self.n)


def over_tiles(eng, first, body, last):
    with eng.Fori(0, (last - first) // 2) as h:
        for b in range(2):
            body(h * 2 + (first + b), (first + b) % 2, h)


T = 125
NT = 50
H = 8
DH = 32
E_N = 8
C = 256
QKV = 3 * C
MAIN = DH // 2 * DH
PR = MAIN + DH // 2
FEAT = PR + 1 + DH
TAIL = FEAT - MAIN
KW = MAIN + DH + DH // 2
VW = DH + 1
G5 = 5
SCALE = DH ** 0.25
EPS_N = 1e-12


PACKED_FIRST = SEG - 2 * NT


def norm_transposed(nc, x_dram, xT_dram, wr):
    with ExitStack() as c:
        c.callback(nc.all_engine_barrier)
        def sb(n, s, t=F32):
            return c.enter_context(nc.sbuf_tensor("ln_" + n, s, t))

        def sem(n):
            return c.enter_context(a_semaphore(nc, "ln_" + n))
        xs = sb("xs", [T, 2, G5, C]); st = sb("stats", [T, G5, 6]); mv = sb("mean_var", [T, G5, 2]); sd = sb("sd", [T, G5]); eps = sb("eps", [T, 1])
        ident = sb("ident", [P, P]); xn = sb("xn", [T, 2, G5, C]); xT = sb("xT", [P, 2, G5, 2 * T])
        ps = [c.enter_context(nc.psum_tensor(f"ln_ps{j}", [P, 512], F32)) for j in range(G5)]
        s_c = sem("consts"); s_ld = [sem(f"loaded{b}") for b in range(2)]; s_dv = sem("dve"); s_go = sem("dve_goes_on"); s_var = sem("var"); s_sd = sem("sd_ready")
        s_xn = sem("xn_ready"); s_tp = sem("transposed"); s_kept = sem("xT_kept"); s_st = sem("xT_stored"); s_free = sem("xT_free"); s_pool = sem("pool_goes_on")
        with nc.Block() as block:
            @block.sync
            def _(sp):
                def body(q, b, h_):
                    sp.wait_ge(s_xn, q + 1)
                    sp.dma_start(xs[:, b], x_dram[bass.ds(q * (G5 * T), G5 * T), :].rearrange("(t p) c -> p t c", p=T)).then_inc(s_ld[b], 16)
                    for k in range(2):
                        wr.pack(sp, q * 2 + k)
                over_tiles(sp, 0, body, NT // G5)
                for p in range(2 * (NT // G5), PACKED_FIRST):
                    wr.pack(sp, p)

            @block.vector
            def _(v):
                v.engine_nop().then_inc(s_xn, 2)

                def body(q, b, h_):
                    ch = Chain(v, s_dv, q * 2)
                    v.wait_ge(s_ld[b], h_ * 16 + 16)
                    for j in range(G5):
                        last = v.bn_stats(st[:, j, :], xs[:, b, j, :])
                    ch.link(last)
                    v.sem_inc(s_go, 1)
                    for j in range(G5):
                        last = v.bn_aggr(mv[:, j, :], st[:, j, :])
                    last.then_inc(s_var, 1)
                    v.wait_ge(s_sd, q + 1)
                    ch.link(v.reciprocal(sd[:, :], sd[:, :]))
                    v.wait_ge(s_tp, q * G5 + G5)
                    for j in range(G5):
                        last = v.tensor_scalar(xn[:, b, j, :], xs[:, b, j, :], mv[:, j, 0:1], sd[:, j:j + 1], ALU.subtract, ALU.mult)
                    last.then_inc(s_xn, 1)
                over_tiles(v, 0, body, NT // G5)

            @block.tensor
            def _(pe):
                pe.sem_inc(s_tp, 2 * G5)
                pe.wait_ge(s_c, 3)

                def body(q, b, h_):
                    pe.wait_ge(s_xn, q + 3)
                    for j in range(G5):
                        pe.wait_ge(s_kept, q * G5 + (j + 1))
                        for k in range(2):
                            last = pe.transpose(ps[j][:, k * T:(k + 1) * T], xn[:, b, j, k * P:(k + 1) * P], ident[0:T, 0:T])
                        last.then_inc(s_tp, 1)
                over_tiles(pe, 0, body, NT // G5)

            @block.scalar
            def _(a):
                a.sem_inc(s_kept, G5)
                a.wait_ge(s_c, 3)

                def body(q, b, h_):
                    a.wait_ge(s_var, q + 1)
                    a.wait_ge(s_xn, q + 2)
                    a.activation(sd[:, :], mv[:, :, 1], ACT.Sqrt, bias=eps[:, 0:1]).then_inc(s_sd, 1)
                    a.wait_ge(s_free, q + 1)
                    for j in range(G5):
                        a.wait_ge(s_tp, q * G5 + (j + 1 + 2 * G5))
                        a.activation(xT[:, b, j, :], ps[j][:, 0:2 * T], ACT.Copy).then_inc(s_kept, 1)
                over_tiles(a, 0, body, NT // G5)

            @block.gpsimd
            def _(g):
                g.memset(ident[:, :], 0.0).then_inc(s_c, 1)
                g.memset(eps[:, :], 1e-5).then_inc(s_c, 1)
                g.wait_ge(s_c, 2)
                g.affine_select(out=ident[:, :], in_=ident[:, :], compare_op=ALU.not_equal, fill=1.0, base=0,
                                pattern=[[-1, P]], channel_multiplier=1).then_inc(s_c, 1)
                g.sem_inc(s_free, 2)

                def body(q, b, h_):
                    g.wait_ge(s_kept, q * G5 + 2 * G5)
                    g.sem_inc(s_pool, 1)
                    g.dma_start(xT_dram[bass.ds(q * G5, G5), :, :].rearrange("t p c -> p t c"), xT[:, b]).then_inc(s_st, 16)
                    g.wait_ge(s_st, q * 16 + 16)
                    g.sem_inc(s_free, 1)
                over_tiles(g, 0, body, NT // G5)


def products(eng, feat, tails, h0, h1):
    for h in range(h0, h1):
        f = feat[:, h, 0:1]
        out = feat[:, h, 0:MAIN].rearrange("p (r i) -> p r i", i=DH)
        once = bass.AP(tensor=f.tensor, offset=f.offset + MAIN, ap=[list(f.ap[0]), [0, DH // 2], [1, DH]])
        moved = bass.AP(tensor=f.tensor, offset=f.offset + MAIN, ap=[list(f.ap[0]), [1, DH // 2], [1, DH]])
        eng.tensor_tensor(out, once, moved, ALU.mult)
    half, end = MAIN + DH // 2, MAIN + DH
    return eng.tensor_tensor(tails[:, h0:h1, 0:DH // 2], feat[:, h0:h1, MAIN:half], feat[:, h0:h1, half:end], ALU.mult)


def moments(nc, xT_dram, wqkvT, bqkv, mom_dram, wr):
    with ExitStack() as c:
        c.callback(nc.all_engine_barrier)
        def sb(n, s, t=F32):
            return c.enter_context(nc.sbuf_tensor("mo_" + n, s, t))

        def sem(n):
            return c.enter_context(a_semaphore(nc, "mo_" + n))
        w = sb("w", [P, 2, 2 * C]); bias = sb("bias", [T, 2 * C]); xT = sb("xT", [P, 2, 2 * T])
        ks = sb("ks", [T, C]); sq = sb("sq", [T, C]); ss = sb("ss", [T, H])
        feat = [sb(f"feat{b}", [T, H, KW]) for b in range(2)]
        tails = [sb(f"tails{b}", [T, H, TAIL]) for b in range(2)]
        vh = [sb(f"vh{b}", [T, H, VW]) for b in range(2)]
        out = sb("out", [P, 5, 512])
        main = [c.enter_context(nc.psum_tensor(f"mo_main{q}", [P, 512], F32)) for q in range(4)]
        tail = c.enter_context(nc.psum_tensor("mo_tail", [P, 512], F32))
        kv = [c.enter_context(nc.psum_tensor(f"mo_kv{b}", [P, 512], F32)) for b in range(2)]
        s_w = sem("weights"); s_x = [sem(f"xT_loaded{b}") for b in range(2)]; s_kv = sem("kv_in_psum"); s_ks = sem("kv_kept"); s_sq = sem("norms_wanted")
        s_rt = sem("norms_ready"); s_kn = sem("k_normed"); s_fd = sem("features_dve"); s_fp = sem("features_pool"); s_mm = sem("tile_summed")
        s_dv = sem("dve"); s_c = sem("consts"); s_o = sem("kept"); s_out = sem("stored")
        with nc.Block() as block:
            @block.sync
            def _(sp):
                sp.dma_start(w[:, :, :], wqkvT[:, C:QKV].rearrange("(a p) n -> p a n", p=P)).then_inc(s_w, 16)
                sp.dma_start(bias[:, :], dram_rows(bqkv, T, 2 * C, C)).then_inc(s_w, 16)

                def body(t, b, h_):
                    sp.wait_ge(s_kv, t + 1)
                    sp.dma_start(xT[:, b, :], xT_dram[bass.ds(t, 1), :, :].rearrange("o p c -> (o p) c")).then_inc(s_x[b], 16)
                    for k in range(2):
                        wr.pack(sp, t * 2 + (PACKED_FIRST + k))
                over_tiles(sp, 0, body, NT)
                sp.wait_ge(s_o, 5)
                for h in range(H):
                    q, p0 = h // 2, 64 * (h % 2)
                    sp.dma_start(mom_dram[h, :, 0:512], out[p0:p0 + VW, q, :]).then_inc(s_out, 16)
                    sp.dma_start(mom_dram[h, :, 512:FEAT], out[p0:p0 + VW, 4, q * TAIL:(q + 1) * TAIL]).then_inc(s_out, 16)
                sp.wait_ge(s_out, 16 * 2 * H)

            @block.tensor
            def _(pe):
                pe.wait_ge(s_w, 32)
                pe.wait_ge(s_c, 2)
                pe.sem_inc(s_kv, 2)
                pe.sem_inc(s_mm, 2)

                def kv_of(t, b, turn):
                    pe.wait_ge(s_x[b], turn * 16 + 16)
                    pe.wait_ge(s_ks, t + 1)
                    for k in range(2):
                        last = pe.matmul(kv[b][0:T, :], xT[:, b, k * T:(k + 1) * T], w[:, k, :], start=(k == 0), stop=(k == 1))
                    last.then_inc(s_kv, 1)

                def sums(t, b):
                    pe.wait_ge(s_fd, t + 1)
                    pe.wait_ge(s_fp, t + 1)
                    for h in range(H):
                        q, p0 = h // 2, 64 * (h % 2)
                        pe.matmul(main[q][p0:p0 + VW, :], vh[b][:, h, :], feat[b][:, h, 0:512], start=False, stop=True, skip_group_check=True)
                        last = pe.matmul(tail[p0:p0 + VW, q * TAIL:(q + 1) * TAIL], vh[b][:, h, :], tails[b][:, h, :], start=False, stop=True, skip_group_check=True)
                    last.then_inc(s_mm, 1)
                kv_of(0, 0, 0)
                with pe.Fori(0, (NT - 2) // 2) as h2:
                    for b in range(2):
                        kv_of(h2 * 2 + (b + 1), 1 - b, h2 + b)
                        sums(h2 * 2 + b, b)
                kv_of(NT - 1, 1, NT // 2 - 1)
                sums(NT - 2, 0)
                sums(NT - 1, 1)

            @block.vector
            def _(v):
                for q in range(4):
                    v.memset(main[q][:, :], 0.0)
                v.memset(tail[:, :], 0.0).then_inc(s_c, 1)
                for b in range(2):
                    v.memset(vh[b][:, :, 0:1], 1.0)
                    last = v.memset(tails[b][:, :, PR - MAIN:PR - MAIN + 1], 1.0)
                last.then_inc(s_c, 1)
                v.wait_ge(s_c, 2)
                v.wait_ge(s_w, 32)
                v.engine_nop().then_inc(s_ks, 2)

                def body(t, b, h_):
                    ch = Chain(v, s_dv, t * 4)
                    v.wait_ge(s_kv, t + 3)
                    v.wait_ge(s_mm, t + 1)
                    v.tensor_tensor(vh[b][:, :, 1:VW], kv[b][0:T, C:2 * C].rearrange("p (h d) -> p h d", d=DH), bias[:, C:2 * C].rearrange("p (h d) -> p h d", d=DH), ALU.add)
                    v.tensor_tensor(ks[:, :], kv[b][0:T, 0:C], bias[:, 0:C], ALU.add).then_inc(s_ks, 1)
                    v.wait_ge(s_ks, t + 3)
                    ch.link(v.tensor_tensor(sq[:, :], ks[:, :], ks[:, :], ALU.mult))
                    v.tensor_reduce(ss[:, :], sq[:, :].rearrange("p (h d) -> p h d", d=DH), AX.X, ALU.add).then_inc(s_sq, 1)
                    v.wait_ge(s_rt, t + 1)
                    ch.link(v.tensor_scalar(ss[:, :], ss[:, :], EPS_N, None, ALU.max))
                    ch.link(v.reciprocal(ss[:, :], ss[:, :]))
                    ch.link(v.tensor_scalar(ss[:, :], ss[:, :], SCALE, None, ALU.mult))
                    ks3 = ks[:, :].rearrange("p (h d) -> p h d", d=DH)
                    v.tensor_tensor(feat[b][:, :, MAIN:MAIN + DH], ks3, ss[:, :].unsqueeze(2).to_broadcast([T, H, DH]), ALU.mult)
                    v.tensor_tensor(tails[b][:, :, TAIL - DH:TAIL], ks3, ss[:, :].unsqueeze(2).to_broadcast([T, H, DH]), ALU.mult)
                    v.tensor_tensor(feat[b][:, :, MAIN + DH:KW], ks3[:, :, 0:DH // 2], ss[:, :].unsqueeze(2).to_broadcast([T, H, DH // 2]), ALU.mult).then_inc(s_kn, 1)
                    v.wait_ge(s_kn, t + 1)
                    products(v, feat[b], tails[b], 0, 5).then_inc(s_fd, 1)
                over_tiles(v, 0, body, NT)
                v.wait_ge(s_mm, NT + 2)
                for q in range(4):
                    v.tensor_copy(out[:, q, :], main[q][:, :]).then_inc(s_o, 1)
                v.tensor_copy(out[:, 4, :], tail[:, :]).then_inc(s_o, 1)

            @block.scalar
            def _(a):
                def body(t, b, h_):
                    a.wait_ge(s_sq, t + 1)
                    a.activation(ss[:, :], ss[:, :], ACT.Sqrt).then_inc(s_rt, 1)
                over_tiles(a, 0, body, NT)

            @block.gpsimd
            def _(g):
                def body(t, b, h_):
                    g.wait_ge(s_kn, t + 1)
                    g.sem_inc(s_c, 1)
                    products(g, feat[b], tails[b], 5, H).then_inc(s_fp, 1)
                over_tiles(g, 0, body, NT)


def attend(nc, xT_dram, wqkvT, bqkv, temp, wprojT, bproj, mom_dram, mT_dram, x_dram, gate_w, gate_b, x1, xn2, logits):
    with ExitStack() as c:
        c.callback(nc.all_engine_barrier)
        def sb(n, s, t=F32):
            return c.enter_context(nc.sbuf_tensor("at_" + n, s, t))

        def sem(n):
            return c.enter_context(a_semaphore(nc, "at_" + n))

        def ps(n):
            return c.enter_context(nc.psum_tensor("at_ps_" + n, [P, 512], F32))
        wq = sb("wq", [P, 2, 2 * C]); bq = sb("bq", [T, C]); tmp8 = sb("temp", [T, H]); wp = sb("wp", [P, 2, C]); bp = sb("bp", [T, C])
        ident = sb("ident", [P, P]); momT = sb("momT", [P, 4, H, VW]); momE = sb("momE", [2 * TAIL, H // 2, 2, VW]); wt = sb("wt", [P, 4]); we = sb("we", [P, 2])
        xT = sb("xT", [P, 2, 2 * T]); xs = sb("xs", [T, 2, C])
        qs = sb("qs", [T, C]); sq = sb("sq", [T, C]); ss = sb("ss", [T, H])
        feat = [sb(f"feat{b}", [T, H, KW]) for b in range(2)]
        tails = [sb(f"tails{b}", [T, H, TAIL]) for b in range(2)]
        mom, momtail = feat[0], tails[0]
        gw = sb("gate_w", [P, 2, E_N]); gb = sb("gate_b", [T, E_N]); eps = sb("eps", [T, 1])
        stats = sb("stats", [T, 6]); mv = sb("mean_var", [T, 2]); sd = sb("sd", [T, 1]); xns = sb("xns", [T, C]); xnT = sb("xnT", [P, 2 * T])
        L0 = H * VW
        fT = [sb(f"fT{b}", [P, 4, T]) for b in range(2)]
        fE = [sb(f"fE{b}", [2 * TAIL, 4, T]) for b in range(2)]
        rec = sb("rec", [T, H]); o = sb("o", [T, C]); oT = sb("oT", [P, 2 * T])
        p_q = ps("q"); p_t = [ps(f"t{b}") for b in range(2)]; p_e = [ps(f"e{b}") for b in range(2)]; p_y = ps("y"); p_o = ps("o"); p_r = ps("r")
        names = ("w", "x_ld0", "x_ld1", "q_ps", "q_kept", "sq", "rt", "qn", "fd", "fp", "t_ps", "t_kept", "e_ps", "e_kept", "y_ps", "o_ready", "oT_ps", "oT_kept",
                 "r_ps", "r_kept", "consts", "momT_ps", "momT_kept", "dve_front", "dve_back", "temp_ready", "momw", "pool_goes_on", "x_bias",
                 "ones_ready", "tail_weights", "dve_ln", "dve_goes_on", "var", "sd", "xn_ready", "xn_stored", "xnT_ps", "xnT_kept", "l_ps", "l_kept")
        s = {n: sem(n) for n in names}

        def steps(eng, first, middle, last):
            first()
            over_tiles(eng, 1, middle, NT - 1)
            last()

        with nc.Block() as block:
            @block.sync
            def _(sp):
                sp.dma_start(wq[:, :, 0:C], wqkvT[:, 0:C].rearrange("(a p) n -> p a n", p=P)).then_inc(s["w"], 16)
                sp.dma_start(wq[:, :, C:2 * C], mT_dram.rearrange("(a p) n -> p a n", p=P)).then_inc(s["w"], 16)
                sp.dma_start(wp[:, :, :], wprojT.rearrange("(a p) n -> p a n", p=P)).then_inc(s["w"], 16)
                sp.dma_start(bq[:, :], dram_rows(bqkv, T, C)).then_inc(s["w"], 16)
                sp.dma_start(bp[:, :], dram_rows(bproj, T, C)).then_inc(s["w"], 16)
                sp.dma_start(tmp8[:, :], dram_rows(temp, T, H)).then_inc(s["w"], 16)
                sp.dma_start(mom[0:VW, :, 0:MAIN], mom_dram[:, :, 0:MAIN].rearrange("h e f -> e h f")).then_inc(s["w"], 16)
                sp.dma_start(momtail[0:VW, :, :], mom_dram[:, :, MAIN:FEAT].rearrange("h e f -> e h f")).then_inc(s["w"], 16)
                sp.dma_start(gw[:, :, :], gate_w.rearrange("(a p) n -> p a n", p=P)).then_inc(s["w"], 16)
                sp.dma_start(gb[:, :], dram_rows(gate_b, T, E_N)).then_inc(s["w"], 16)

                def body(t, b, h_):
                    sp.wait_ge(s["q_kept"], t + 1)
                    sp.dma_start(xT[:, b, :], xT_dram[bass.ds(t, 1), :, :].rearrange("o p c -> (o p) c")).then_inc(s[f"x_ld{b}"], 16)
                    sp.dma_start(xs[:, b, :], x_dram[bass.ds(t * T, T), :]).then_inc(s[f"x_ld{b}"], 16)
                over_tiles(sp, 0, body, NT)

            @block.gpsimd
            def _(g):
                g.memset(ident[:, :], 0.0).then_inc(s["consts"], 1)
                g.memset(wt[:, :], 1.0).then_inc(s["consts"], 1)
                g.wait_ge(s["consts"], 2)
                g.affine_select(out=ident[:, :], in_=ident[:, :], compare_op=ALU.not_equal, fill=1.0, base=0,
                                pattern=[[-1, P]], channel_multiplier=1).then_inc(s["consts"], 1)
                g.memset(wt[0:DH, 0:1], 0.5).then_inc(s["consts"], 1)
                for x in range(2):
                    n = x * 4
                    w = we[:, x:x + 1]
                    g.memset(w, SCALE ** 2).then_inc(s["tail_weights"], 1)
                    g.wait_ge(s["tail_weights"], n + 1)
                    g.affine_select(out=w, in_=w, compare_op=ALU.is_ge, fill=SCALE ** 4, base=-(x * TAIL + DH // 2 + 1),
                                    pattern=[[0, 1]], channel_multiplier=1).then_inc(s["tail_weights"], 1)
                    g.wait_ge(s["tail_weights"], n + 2)
                    g.affine_select(out=w, in_=w, compare_op=ALU.is_ge, fill=1.0, base=-(x * TAIL + DH // 2),
                                    pattern=[[0, 1]], channel_multiplier=1).then_inc(s["tail_weights"], 1)
                    g.wait_ge(s["tail_weights"], n + 3)
                    g.affine_select(out=w, in_=w, compare_op=ALU.is_ge, fill=0.0, base=-TAIL if x else TAIL - 1,
                                    pattern=[[0, 1]], channel_multiplier=1 if x else -1).then_inc(s["tail_weights"], 1)
                g.memset(eps[:, :], 1e-5).then_inc(s["consts"], 1)
                g.wait_ge(s["momT_ps"], H)
                for b in range(2):
                    g.memset(tails[b][:, :, PR - MAIN:PR - MAIN + 1], 1.0).then_inc(s["ones_ready"], 1)
                g.wait_ge(s["w"], 16 * 10)
                g.sem_inc(s["pool_goes_on"], 1)

                def body(t, b, h_):
                    g.wait_ge(s[f"x_ld{b}"], h_ * 32 + 32)
                    g.sem_inc(s["pool_goes_on"], 1)
                    g.tensor_tensor(xs[:, b, :], xs[:, b, :], bp[:, :], ALU.add).then_inc(s["x_bias"], 1)
                    g.wait_ge(s["qn"], t + 1)
                    g.sem_inc(s["pool_goes_on"], 1)
                    products(g, feat[b], tails[b], 5, H).then_inc(s["fp"], 1)
                over_tiles(g, 0, body, NT)

            @block.tensor
            def _(pe):
                pe.wait_ge(s["w"], 16 * 10)
                pe.wait_ge(s["consts"], 5)
                for h in range(H):
                    if h >= 2:
                        pe.wait_ge(s["momT_kept"], h - 1)
                    for k in range(4):
                        last = pe.transpose(p_t[h % 2][:, k * VW:(k + 1) * VW], mom[0:VW, h, k * P:(k + 1) * P], ident[0:VW, 0:VW])
                    if h % 2:
                        last = pe.transpose(p_t[1][0:2 * TAIL, 4 * VW:5 * VW], momtail[0:VW, h - 1:h + 1, :].rearrange("p a f -> p (a f)"), ident[0:VW, 0:VW])
                    last.then_inc(s["momT_ps"], 1)
                pe.wait_ge(s["momT_kept"], H)
                pe.wait_ge(s["momw"], 4)
                pe.wait_ge(s["ones_ready"], 2)
                pe.sem_inc(s["t_ps"], 1)

                def q_of(t, b, turn):
                    pe.wait_ge(s[f"x_ld{b}"], turn * 32 + 32)
                    pe.wait_ge(s["q_kept"], t + 2)
                    for k in range(2):
                        last = pe.matmul(p_q[0:T, :], xT[:, b, k * T:(k + 1) * T], wq[:, k, :], start=(k == 0), stop=(k == 1))
                    last.then_inc(s["q_ps"], 1)

                def o_transposed(t):
                    pe.wait_ge(s["o_ready"], t + 1)
                    for k in range(2):
                        last = pe.transpose(p_o[:, k * T:(k + 1) * T], o[:, k * P:(k + 1) * P], ident[0:T, 0:T])
                    last.then_inc(s["oT_ps"], 1)

                def projected(t):
                    pe.wait_ge(s["oT_kept"], t + 1)
                    pe.wait_ge(s["r_kept"], t + 1)
                    for k in range(2):
                        last = pe.matmul(p_r[0:T, 0:C], oT[:, k * T:(k + 1) * T], wp[:, k, :], start=(k == 0), stop=(k == 1))
                    last.then_inc(s["r_ps"], 1)

                def xn_transposed(t):
                    pe.wait_ge(s["xn_ready"], t + 1)
                    for k in range(2):
                        last = pe.transpose(p_o[:, C + k * T:C + (k + 1) * T], xns[:, k * P:(k + 1) * P], ident[0:T, 0:T])
                    last.then_inc(s["xnT_ps"], 1)

                def gated(t):
                    pe.wait_ge(s["xnT_kept"], t + 1)
                    for k in range(2):
                        last = pe.matmul(p_y[0:T, L0:L0 + E_N], xnT[:, k * T:(k + 1) * T], gw[:, k, :], start=(k == 0), stop=(k == 1))
                    last.then_inc(s["l_ps"], 1)

                def heads(t, b, before, q_ahead):
                    pe.wait_ge(s["fd"], t + 1)
                    pe.wait_ge(s["fp"], t + 1)
                    pe.wait_ge(s["e_kept"], t + 1)
                    for j in range(4):
                        last = pe.transpose(p_e[b][0:2 * TAIL, j * T:(j + 1) * T], tails[b][:, 2 * j:2 * j + 2, :].rearrange("p a f -> p (a f)"), ident[0:T, 0:T])
                    last.then_inc(s["e_ps"], 1)

                    def transposes(h):
                        pe.wait_ge(s["t_kept"], t * 8 + (h + 1))
                        for k in range(4):
                            last = pe.transpose(p_t[h % 2][:, k * T:(k + 1) * T], feat[b][:, h, k * P:(k + 1) * P], ident[0:T, 0:T])
                        last.then_inc(s["t_ps"], 1)

                    def apply(h):
                        pe.wait_ge(s["t_kept"], t * 8 + (h + 3))
                        if h % 2 == 0:
                            pe.wait_ge(s["e_kept"], t + 3)
                            pe.matmul(p_y[0:T, h * VW:(h + 2) * VW], fE[b][:, h // 2, :], momE[:, h // 2, :, :].rearrange("p a e -> p (a e)"),
                                      start=True, stop=False, skip_group_check=True)
                        for k in range(4):
                            last = pe.matmul(p_y[0:T, h * VW:(h + 1) * VW], fT[h % 2][:, k, :], momT[:, k, h, :], start=False, stop=(k == 3), skip_group_check=True)
                        last.then_inc(s["y_ps"], 1)
                    transposes(0)
                    for h in range(H):
                        if h + 1 < H:
                            transposes(h + 1)
                        if before and h == 0:
                            o_transposed(t - 1)
                        if before and h == 2:
                            projected(t - 1)
                        if h == 1 and q_ahead:
                            q_ahead()
                        if before and h == 6:
                            xn_transposed(t - 1)
                        apply(h)
                    if before:
                        gated(t - 1)

                def first():
                    q_of(0, 0, 0)
                    q_of(1, 1, 0)
                    heads(0, 0, False, lambda: q_of(2, 0, 1))
                    heads(1, 1, True, lambda: q_of(3, 1, 1))

                def middle(t, b, h_):
                    heads(t, b, True, lambda: q_of(t + 2, b, h_ + 2))

                def last_():
                    heads(NT - 2, 0, True, None)
                    heads(NT - 1, 1, True, None)
                    o_transposed(NT - 1)
                    projected(NT - 1)
                    xn_transposed(NT - 1)
                    gated(NT - 1)
                first()
                over_tiles(pe, 2, middle, NT - 2)
                last_()

            @block.scalar
            def _(a):
                a.sem_inc(s["t_kept"], 2)
                a.sem_inc(s["e_kept"], 2)
                a.wait_ge(s["consts"], 5)

                def root(t):
                    a.wait_ge(s["sq"], t + 1)
                    a.activation(ss[:, :], ss[:, :], ACT.Sqrt).then_inc(s["rt"], 1)

                def oT_of(t):
                    a.wait_ge(s["oT_ps"], t + 1)
                    a.activation(oT[:, :], p_o[:, 0:2 * T], ACT.Copy).then_inc(s["oT_kept"], 1)

                def sd_of(t):
                    a.wait_ge(s["var"], t + 1)
                    a.activation(sd[:, :], mv[:, 1:2], ACT.Sqrt, bias=eps[:, 0:1]).then_inc(s["sd"], 1)

                def xnT_of(t):
                    a.wait_ge(s["xnT_ps"], t + 1)
                    a.activation(xnT[:, :], p_o[:, C:C + 2 * T], ACT.Copy).then_inc(s["xnT_kept"], 1)
                    a.activation(xn2[:, bass.ds(t, 1), :].rearrange("p o c -> p (o c)"), xns[:, :], ACT.Copy).then_inc(s["xn_stored"], 1)

                def kept(t, b, before, after):
                    a.wait_ge(s["e_ps"], t + 1)
                    a.activation(fE[b][:, :, :].rearrange("p a b -> p (a b)"), p_e[b][0:2 * TAIL, 0:4 * T], ACT.Copy).then_inc(s["e_kept"], 1)
                    for h in range(H):
                        a.wait_ge(s["t_ps"], t * 8 + (h + 2))
                        a.activation(fT[h % 2][:, :, :].rearrange("p a b -> p (a b)"), p_t[h % 2][:, 0:4 * T], ACT.Copy).then_inc(s["t_kept"], 1)
                        if before and h == 1:
                            oT_of(t - 1)
                        if after and h == 0:
                            root(t + 1)
                        if before and h == 5:
                            sd_of(t - 1)
                        if before and h == 7:
                            xnT_of(t - 1)

                def first():
                    root(0)
                    kept(0, 0, False, True)

                def middle(t, b, h_):
                    kept(t, b, True, True)

                def last_():
                    kept(NT - 1, 1, True, False)
                    oT_of(NT - 1)
                    sd_of(NT - 1)
                    xnT_of(NT - 1)
                steps(a, first, middle, last_)

            @block.vector
            def _(v):
                v.wait_ge(s["consts"], 5)
                v.wait_ge(s["tail_weights"], 8)
                for h in range(H):
                    v.wait_ge(s["momT_ps"], h + 1)
                    if h % 2:
                        for x in range(2):
                            v.tensor_scalar(momE[:, h // 2, x, :], p_t[1][0:2 * TAIL, 4 * VW:5 * VW], we[0:2 * TAIL, x:x + 1], 1.0 / (NT * T), ALU.mult, ALU.mult)
                    v.tensor_copy(momT[:, :, h, :], p_t[h % 2][:, 0:4 * VW].rearrange("p (k e) -> p k e", e=VW)).then_inc(s["momT_kept"], 1)
                v.wait_ge(s["momT_kept"], H)
                for k in range(4):
                    v.tensor_scalar(momT[:, k, :, :], momT[:, k, :, :], wt[:, k:k + 1], 1.0 / (NT * T), ALU.mult, ALU.mult).then_inc(s["momw"], 1)
                v.wait_ge(s["w"], 16 * 10)
                v.engine_nop().then_inc(s["r_kept"], 1)
                v.engine_nop().then_inc(s["q_kept"], 2)
                v.engine_nop().then_inc(s["xn_stored"], 1)
                v.tensor_scalar(tmp8[:, :], tmp8[:, :], SCALE * SCALE, None, ALU.mult).then_inc(s["temp_ready"], 1)
                v.wait_ge(s["temp_ready"], 1)

                def x1_of(t):
                    return x1[:, bass.ds(t, 1), :].rearrange("p o c -> p (o c)")

                def features(t, b):
                    ch = Chain(v, s["dve_front"], t * 4)
                    v.wait_ge(s["x_bias"], t + 1)
                    v.wait_ge(s["q_ps"], t + 1)
                    v.tensor_tensor(x1_of(t), p_q[0:T, C:2 * C], xs[:, b, :], ALU.add)
                    v.tensor_tensor(qs[:, :], p_q[0:T, 0:C], bq[:, :], ALU.add).then_inc(s["q_kept"], 1)
                    v.wait_ge(s["q_kept"], t + 3)
                    ch.link(v.tensor_tensor(sq[:, :], qs[:, :], qs[:, :], ALU.mult))
                    v.tensor_reduce(ss[:, :], sq[:, :].rearrange("p (h d) -> p h d", d=DH), AX.X, ALU.add).then_inc(s["sq"], 1)
                    v.wait_ge(s["rt"], t + 1)
                    ch.link(v.tensor_scalar(ss[:, :], ss[:, :], SCALE, EPS_N, ALU.mult, ALU.max))
                    ch.link(v.reciprocal(ss[:, :], ss[:, :]))
                    ch.link(v.tensor_tensor(ss[:, :], ss[:, :], tmp8[:, :], ALU.mult))
                    qs3 = qs[:, :].rearrange("p (h d) -> p h d", d=DH)
                    v.tensor_tensor(feat[b][:, :, MAIN:MAIN + DH], qs3, ss[:, :].unsqueeze(2).to_broadcast([T, H, DH]), ALU.mult)
                    v.tensor_tensor(tails[b][:, :, TAIL - DH:TAIL], qs3, ss[:, :].unsqueeze(2).to_broadcast([T, H, DH]), ALU.mult)
                    v.tensor_tensor(feat[b][:, :, MAIN + DH:KW], qs3[:, :, 0:DH // 2], ss[:, :].unsqueeze(2).to_broadcast([T, H, DH // 2]), ALU.mult).then_inc(s["qn"], 1)
                    v.wait_ge(s["qn"], t + 1)
                    products(v, feat[b], tails[b], 0, 5).then_inc(s["fd"], 1)

                def gate_kept(t):
                    v.tensor_tensor(logits[:, bass.ds(t, 1), :].rearrange("p o e -> p (o e)"), p_y[0:T, L0:L0 + E_N], gb[:, :], ALU.add).then_inc(s["l_kept"], 1)

                def attended(t, before):
                    v.wait_ge(s["y_ps"], t * 8 + 8)
                    if before:
                        v.wait_ge(s["l_ps"], t)
                    y3 = p_y[0:T, 0:H * VW].rearrange("p (h e) -> p h e", e=VW)
                    v.reciprocal(rec[:, :], y3[:, :, 0]).then_inc(s["dve_back"], 1)
                    if before:
                        gate_kept(t - 1)
                    v.wait_ge(s["dve_back"], t + 1)
                    v.tensor_tensor(o[:, :].rearrange("p (h d) -> p h d", d=DH), y3[:, :, 1:VW], rec[:, :].unsqueeze(2).to_broadcast([T, H, DH]), ALU.mult).then_inc(s["o_ready"], 1)

                def summed(t):
                    v.wait_ge(s["r_ps"], t + 1)
                    v.tensor_tensor(x1_of(t), x1_of(t), p_r[0:T, 0:C], ALU.add).then_inc(s["r_kept"], 1)

                def normed(t):
                    ch = Chain(v, s["dve_ln"], t * 2)
                    v.wait_ge(s["r_kept"], t + 2)
                    v.sem_inc(s["dve_goes_on"], 1)
                    ch.link(v.bn_stats(stats[:, :], x1_of(t)))
                    v.sem_inc(s["dve_goes_on"], 1)
                    v.bn_aggr(mv[:, :], stats[:, :]).then_inc(s["var"], 1)
                    v.wait_ge(s["sd"], t + 1)
                    ch.link(v.reciprocal(sd[:, :], sd[:, :]))
                    v.wait_ge(s["xn_stored"], t + 1)
                    v.tensor_scalar(xns[:, :], x1_of(t), mv[:, 0:1], sd[:, 0:1], ALU.subtract, ALU.mult).then_inc(s["xn_ready"], 1)

                def first():
                    features(0, 0)
                    features(1, 1)
                    attended(0, False)

                def middle(t, b, h_):
                    features(t + 1, 1 - b)
                    summed(t - 1)
                    normed(t - 1)
                    attended(t, True)

                def last_():
                    summed(NT - 2)
                    normed(NT - 2)
                    attended(NT - 1, True)
                    summed(NT - 1)
                    normed(NT - 1)
                    v.wait_ge(s["l_ps"], NT)
                    gate_kept(NT - 1)
                steps(v, first, middle, last_)

HID = 1024
CAP = -(-5 * NT * T // (4 * E_N))
ROOM = CAP
NONE = 100000
F_MAX = 3.4028234663852886e38


def route(nc, lg, xn, buf_dram, slot_i, coef):
    with ExitStack() as c:
        c.callback(nc.all_engine_barrier)
        def sb(n, s, t=F32):
            return c.enter_context(nc.sbuf_tensor("ro_" + n, s, t))

        def sem(n):
            return c.enter_context(a_semaphore(nc, "ro_" + n))
        w8 = sb("w8", [T, NT, E_N]); oh = sb("oh", [T, NT, E_N]); ex = sb("ex", [T, NT, E_N]); z50 = sb("z50", [T, NT])
        m = sb("m", [T, NT]); idx = sb("idx", [T, NT]); pos = sb("pos", [T, NT]); kept = sb("kept", [T, NT]); dst = sb("dst", [T, NT])
        tri = sb("tri", [T, T]); ones = sb("ones", [T, T]); dst_i = sb("dst_i", [T, NT], I32)
        rowi = [sb(f"rowi{b}", [T, G5], I32) for b in range(2)]
        rows = [sb(f"rows{b}", [T, G5, C]) for b in range(2)]
        p_c = c.enter_context(nc.psum_tensor("ro_c", [P, 512], F32)); p_s = c.enter_context(nc.psum_tensor("ro_s", [P, 512], F32))
        s_dv = sem("dve")
        s_e = sem("exp_wanted"); s_ex = sem("exp_ready"); s_oh = sem("oh_ready"); s_cp = sem("counts_ps"); s_di = sem("rows_known")
        s_c = sem("consts"); s_cpd = sem("staged"); s_sc = [sem(f"scattered{b}") for b in range(2)]; s_go = sem("pool_goes_on")
        with nc.Block() as block:
            @block.tensor
            def _(pe):
                pe.wait_ge(s_c, 5)
                pe.wait_ge(s_oh, 1)
                ohf = oh[:, :, :].rearrange("p t e -> p (t e)")
                pe.matmul(p_c[0:T, 0:NT * E_N], tri[:, :], ohf, start=True, stop=True)
                pe.matmul(p_s[0:T, 0:NT * E_N], ones[:, :], ohf, start=True, stop=True).then_inc(s_cp, 1)

            @block.scalar
            def _(a):
                a.wait_ge(s_e, 1)
                a.activation(lg[:, :, :], lg[:, :, :], ACT.Exp).then_inc(s_ex, 1)

            @block.vector
            def _(v):
                v.wait_ge(s_c, 5)
                ch = Chain(v, s_dv)

                def each(a):
                    return a[:, :].unsqueeze(2).to_broadcast([T, NT, E_N])
                ch.link(v.tensor_reduce(m[:, :], lg[:, :, :], AX.X, ALU.max))
                v.tensor_tensor(lg[:, :, :], lg[:, :, :], each(m), ALU.subtract).then_inc(s_e, 1)
                v.wait_ge(s_ex, 1)
                ch.link(v.tensor_reduce(m[:, :], lg[:, :, :], AX.X, ALU.add))
                ch.link(v.reciprocal(m[:, :], m[:, :]))
                ch.link(v.tensor_tensor(lg[:, :, :], lg[:, :, :], each(m), ALU.mult))
                ch.link(v.tensor_reduce(coef[:, :], lg[:, :, :], AX.X, ALU.max))
                ch.link(v.tensor_tensor(oh[:, :, :], lg[:, :, :], each(coef), ALU.is_equal))
                ch.link(v.tensor_tensor(lg[:, :, :], oh[:, :, :], w8[:, :, :], ALU.mult))
                ch.link(v.tensor_reduce(idx[:, :], lg[:, :, :], AX.X, ALU.max))
                v.tensor_tensor(oh[:, :, :], lg[:, :, :], each(idx), ALU.is_equal).then_inc(s_oh, 1)
                v.wait_ge(s_oh, 1)
                v.wait_ge(s_cp, 1)
                tot = p_s[0:T, 0:NT * E_N].rearrange("p (t e) -> p t e", e=E_N)
                for e in range(E_N):
                    last = v.tensor_tensor_scan(ex[:, :, e], tot[:, :, e], z50[:, :], 0.0, ALU.add, ALU.add)
                ch.link(last)
                ch.link(v.tensor_tensor(ex[:, :, :], ex[:, :, :], tot, ALU.subtract))
                ch.link(v.tensor_tensor(ex[:, :, :], ex[:, :, :], p_c[0:T, 0:NT * E_N].rearrange("p (t e) -> p t e", e=E_N), ALU.add))
                ch.link(v.tensor_tensor(ex[:, :, :], ex[:, :, :], oh[:, :, :], ALU.mult))
                ch.link(v.tensor_reduce(pos[:, :], ex[:, :, :], AX.X, ALU.add))
                v.tensor_scalar(idx[:, :], idx[:, :], -float(ROOM), float(E_N * ROOM), ALU.mult, ALU.add)
                ch.link(v.tensor_scalar(pos[:, :], pos[:, :], -1.0, None, ALU.add))
                ch.link(v.tensor_scalar(kept[:, :], pos[:, :], float(CAP), None, ALU.is_lt))
                ch.link(v.tensor_tensor(coef[:, :], coef[:, :], kept[:, :], ALU.mult))
                ch.link(v.tensor_tensor(dst[:, :], pos[:, :], idx[:, :], ALU.add))
                ch.link(v.tensor_scalar(kept[:, :], kept[:, :], -float(NONE), float(NONE), ALU.mult, ALU.add))
                ch.link(v.tensor_tensor(dst[:, :], dst[:, :], kept[:, :], ALU.add))
                v.tensor_copy(dst_i[:, :], dst[:, :]).then_inc(s_di, 1)
                ch.link(v.tensor_scalar(pos[:, :], pos[:, :], float(CAP - 1), None, ALU.min))
                ch.link(v.tensor_tensor(pos[:, :], pos[:, :], idx[:, :], ALU.add))
                ch.link(v.tensor_copy(slot_i[:, :], pos[:, :]))

                def stage(q, b):
                    v.tensor_copy(rowi[b][:, :], dst_i[:, bass.ds(q * G5, G5)])
                    v.tensor_copy(rows[b][:, :, :], xn[:, bass.ds(q * G5, G5), :]).then_inc(s_cpd, 1)
                v.wait_ge(s_di, 1)
                for q in range(2):
                    stage(q, q)

                def body(q, b, h_):
                    v.wait_ge(s_sc[b], h_ * (16 * G5) + 16 * G5)
                    stage(q, b)
                over_tiles(v, 2, body, NT // G5)

            @block.gpsimd
            def _(g):
                g.iota(w8[:, :, :], pattern=[[0, NT], [-1, E_N]], base=E_N, channel_multiplier=0, allow_small_or_imprecise_dtypes=True).then_inc(s_c, 1)
                g.memset(z50[:, :], 0.0).then_inc(s_c, 1)
                g.memset(ones[:, :], 1.0).then_inc(s_c, 1)
                g.memset(tri[:, :], 1.0).then_inc(s_c, 1)
                g.wait_ge(s_c, 4)
                g.affine_select(out=tri[:, :], in_=tri[:, :], compare_op=ALU.is_ge, fill=0.0, base=0,
                                pattern=[[1, T]], channel_multiplier=-1).then_inc(s_c, 1)

                def body(q, b, h_):
                    g.wait_ge(s_cpd, q + 1)
                    g.sem_inc(s_go, 1)
                    for j in range(G5):
                        g.indirect_dma_start(out=buf_dram, out_offset=bass.IndirectOffsetOnAxis(ap=rowi[b][:, j:j + 1], axis=0),
                                             in_=rows[b][:, j, :], in_offset=None, bounds_check=E_N * ROOM - 1, oob_is_err=False).then_inc(s_sc[b], 16)
                over_tiles(g, 0, body, NT // G5)
                for q in s_sc:
                    g.wait_ge(q, 8 * NT)


def experts(nc, buf_dram, w1, b1p, w2, b2, y_dram):
    with ExitStack() as c:
        c.callback(nc.all_engine_barrier)
        def sb(n, s, t=F32):
            return c.enter_context(nc.sbuf_tensor("ex_" + n, s, t))

        def sem(n):
            return c.enter_context(a_semaphore(nc, "ex_" + n))
        KC, FC, TT = C // P, HID // P, -(-ROOM // P)
        LAST = CAP - (TT - 1) * P
        ident = sb("ident", [P, P]); b1s = sb("b1", [P, E_N, FC]); b1c = sb("b1c", [P, FC]); b2s = sb("b2", [P, E_N, C])
        w1s = sb("w1", [P, 2, KC, HID]); w2s = sb("w2", [P, 2, FC, C]); xr = sb("xr", [P, 2, TT, C]); XT = sb("XT", [P, KC, TT * P])
        hT = sb("hT", [P, FC, TT * P]); yo = sb("yo", [P, 2, TT, C])
        p_x = [c.enter_context(nc.psum_tensor(f"ex_x{b}", [P, 512], F32)) for b in range(2)]
        p_h = [c.enter_context(nc.psum_tensor(f"ex_h{b}", [P, 512], F32)) for b in range(2)]
        p_y = [c.enter_context(nc.psum_tensor(f"ex_y{b}", [P, 512], F32)) for b in range(2)]
        s_b = sem("biases"); s_c = sem("ident_ready"); s_wl = [sem(f"weights{b}") for b in range(2)]; s_xl = [sem(f"rows{b}") for b in range(2)]; s_xp = sem("xT_ps"); s_xk = sem("xT_kept")
        s_hp = sem("h_ps"); s_hk = sem("h_kept"); s_yp = sem("y_ps"); s_yk = sem("y_kept"); s_ys = sem("y_stored"); s_bc = sem("b1_ready"); s_ysf = sem("rows_free")
        with nc.Block() as block:
            @block.sync
            def _(sp):
                sp.dma_start(b1s[:, :, :], b1p).then_inc(s_b, 16)
                sp.dma_start(b2s[:, :, :], bass.AP(tensor=b2.tensor, offset=0, ap=[[0, P], [C, E_N], [1, C]])).then_inc(s_b, 16)

                def body(e, b, h_):
                    sp.wait_ge(s_yp, e * TT + TT)
                    sp.dma_start(xr[:, b, 0:TT - 1, :], buf_dram[bass.ds(e * ROOM, (TT - 1) * P), :].rearrange("(t p) c -> p t c", p=P)).then_inc(s_xl[b], 16)
                    sp.dma_start(xr[0:LAST, b, TT - 1, :], buf_dram[bass.ds(e * ROOM + (TT - 1) * P, LAST), :]).then_inc(s_xl[b], 16)
                    sp.dma_start(w1s[:, b], w1[bass.ds(e, 1), :, :].rearrange("o (k p) f -> p (o k) f", p=P)).then_inc(s_wl[b], 16)
                    sp.dma_start(w2s[:, b], w2[bass.ds(e, 1), :, :].rearrange("o (k p) f -> p (o k) f", p=P)).then_inc(s_wl[b], 16)
                over_tiles(sp, 0, body, E_N)

            @block.gpsimd
            def _(g):
                g.memset(ident[:, :], 0.0).then_inc(s_c, 1)
                g.wait_ge(s_c, 1)
                g.affine_select(out=ident[:, :], in_=ident[:, :], compare_op=ALU.not_equal, fill=1.0, base=0,
                                pattern=[[-1, P]], channel_multiplier=1).then_inc(s_c, 1)
                g.sem_inc(s_ysf, 2)

                def body(e, b, h_):
                    g.wait_ge(s_yk, e * TT + (TT + 2))
                    g.sem_inc(s_c, 1)
                    g.dma_start(y_dram[bass.ds(e * ROOM, (TT - 1) * P), :].rearrange("(t p) c -> p t c", p=P), yo[:, b, 0:TT - 1, :]).then_inc(s_ys, 16)
                    g.dma_start(y_dram[bass.ds(e * ROOM + (TT - 1) * P, LAST), :], yo[0:LAST, b, TT - 1, :]).then_inc(s_ys, 16)
                    g.wait_ge(s_ys, e * 32 + 32)
                    g.sem_inc(s_ysf, 1)
                over_tiles(g, 0, body, E_N)
                g.wait_ge(s_ys, 32 * E_N)

            halves = [(0, 512), (512, CAP)]

            @block.tensor
            def _(pe):
                pe.wait_ge(s_c, 2)
                pe.sem_inc(s_yp, 2 * TT)

                def body(e, b, h_):
                    pe.wait_ge(s_xl[b], h_ * 32 + 32)
                    for k in range(KC):
                        for q in range(2):
                            n = 2 * k + q
                            pe.wait_ge(s_xk, e * 4 + (n + 1))
                            for j in range(4):
                                m = P if q * 4 + j < TT - 1 else LAST
                                last = pe.transpose(p_x[n % 2][:, j * P:j * P + m], xr[0:m, b, q * 4 + j, k * P:(k + 1) * P], ident[0:m, 0:m])
                            last.then_inc(s_xp, 1)
                    pe.wait_ge(s_wl[b], h_ * 32 + 32)
                    pe.wait_ge(s_xk, e * 4 + 6)
                    for f in range(FC):
                        for q, (lo, hi) in enumerate(halves):
                            n = 2 * f + q
                            pe.wait_ge(s_hk, e * 16 + (n + 1))
                            for k in range(KC):
                                last = pe.matmul(p_h[n % 2][:, 0:hi - lo], w1s[:, b, k, f * P:(f + 1) * P], XT[:, k, lo:hi], start=(k == 0), stop=(k == KC - 1))
                            last.then_inc(s_hp, 1)
                    pe.wait_ge(s_hk, e * 16 + 18)
                    for j in range(TT):
                        m = P if j < TT - 1 else LAST
                        pe.wait_ge(s_yk, e * TT + (j + 1))
                        for f in range(FC):
                            last = pe.matmul(p_y[j % 2][0:m, 0:C], hT[:, f, j * P:j * P + m], w2s[:, b, f, :], start=(f == 0), stop=(f == FC - 1))
                        last.then_inc(s_yp, 1)
                over_tiles(pe, 0, body, E_N)

            @block.scalar
            def _(a):
                a.wait_ge(s_b, 32)
                a.sem_inc(s_hk, 2)

                def body(e, b, h_):
                    a.wait_ge(s_hk, e * 16 + 2)
                    a.activation(b1c[:, :], b1s[:, bass.ds(e, 1), :].rearrange("p o f -> p (o f)"), ACT.Copy).then_inc(s_bc, 1)
                    a.wait_ge(s_bc, e + 1)
                    a.wait_ge(s_yp, e * TT + 2 * TT)
                    for f in range(FC):
                        for q, (lo, hi) in enumerate(halves):
                            a.wait_ge(s_hp, e * 16 + (2 * f + q + 1))
                            a.activation(hT[:, f, lo:hi], p_h[q][:, 0:hi - lo], ACT.Relu, bias=b1c[:, f:f + 1]).then_inc(s_hk, 1)
                over_tiles(a, 0, body, E_N)

            @block.vector
            def _(v):
                v.wait_ge(s_b, 32)
                v.engine_nop().then_inc(s_xk, 2)
                v.engine_nop().then_inc(s_yk, 2)

                def body(e, b, h_):
                    for k in range(KC):
                        for q in range(2):
                            n = 2 * k + q
                            v.wait_ge(s_xp, e * 4 + (n + 1))
                            v.tensor_copy(XT[:, k, halves[q][0]:halves[q][1]], p_x[n % 2][:, 0:halves[q][1] - halves[q][0]]).then_inc(s_xk, 1)
                    for j in range(TT):
                        m = P if j < TT - 1 else LAST
                        v.wait_ge(s_yp, e * TT + (j + 1 + 2 * TT))
                        if j == 0:
                            v.wait_ge(s_ysf, e + 1)
                        v.tensor_tensor(yo[0:m, b, j, :], p_y[j % 2][0:m, 0:C], b2s[0:m, bass.ds(e, 1), :].rearrange("p o c -> p (o c)"), ALU.add).then_inc(s_yk, 1)
                over_tiles(v, 0, body, E_N)


def combine(nc, y_dram, slot_i, coef, x1, out_dram):
    with ExitStack() as c:
        c.callback(nc.all_engine_barrier)
        def sb(n, s, t=F32):
            return c.enter_context(nc.sbuf_tensor("co_" + n, s, t))

        def sem(n):
            return c.enter_context(a_semaphore(nc, "co_" + n))
        rowi = [sb(f"rowi{b}", [T, G5], I32) for b in range(2)]
        y = [sb(f"y{b}", [T, G5, C]) for b in range(2)]
        fine = sb("fine", [T, G5, C], I32); below = sb("below", [T, G5, C]); sign = sb("sign", [T, G5, C]); ymul = sb("ymul", [T, G5, C])
        o = [sb(f"o{b}", [T, G5, C]) for b in range(2)]
        s_r = sem("rows_known"); s_g = [sem(f"gathered{b}") for b in range(2)]; s_dv = sem("dve"); s_o = sem("out_ready"); s_st = [sem(f"stored{b}") for b in range(2)]; s_go = sem("goes_on"); s_vgo = sem("dve_goes_on")
        s_free = sem("y_read")
        with nc.Block() as block:
            @block.gpsimd
            def _(g):
                g.sem_inc(s_free, 2)

                def body(q, b, h_):
                    g.wait_ge(s_free, q + 1)
                    g.sem_inc(s_go, 1)
                    g.tensor_copy(rowi[b][:, :], slot_i[:, bass.ds(q * G5, G5)]).then_inc(s_r, 1)
                    g.wait_ge(s_r, q + 1)
                    g.sem_inc(s_go, 1)
                    for j in range(G5):
                        g.indirect_dma_start(out=y[b][:, j, :], out_offset=None, in_=y_dram,
                                             in_offset=bass.IndirectOffsetOnAxis(ap=rowi[b][:, j:j + 1], axis=0)).then_inc(s_g[b], 16)
                over_tiles(g, 0, body, NT // G5)

            @block.vector
            def _(v):
                v.sem_inc(s_vgo, 1)

                def body(q, b, h_):
                    ch = Chain(v, s_dv, q * 3)
                    v.wait_ge(s_g[b], h_ * (16 * G5) + 16 * G5)
                    v.tensor_tensor(ymul[:, :, :], y[b][:, :, :], coef[:, bass.ds(q * G5, G5)].unsqueeze(2).to_broadcast([T, G5, C]), ALU.mult).then_inc(s_free, 1)
                    v.wait_ge(s_free, q + 3)
                    v.tensor_scalar(below[:, :, :], ymul[:, :, :], F_MAX, None, ALU.is_le)
                    ch.link(v.tensor_scalar(sign[:, :, :], ymul[:, :, :], F_MAX, None, ALU.is_gt))
                    v.scalar_tensor_tensor(fine[:, :, :], ymul[:, :, :], -F_MAX, below[:, :, :], ALU.is_ge, ALU.mult)
                    ch.link(v.scalar_tensor_tensor(sign[:, :, :], ymul[:, :, :], -F_MAX, sign[:, :, :], ALU.is_lt, ALU.subtract))
                    ch.link(v.tensor_scalar(sign[:, :, :], sign[:, :, :], -10000.0, None, ALU.mult))
                    v.sem_inc(s_vgo, 1)
                    v.copy_predicated(sign[:, :, :], fine[:, :, :], ymul[:, :, :]).then_inc(s_vgo, 1)
                    v.wait_ge(s_vgo, q * 2 + 3)
                    v.wait_ge(s_st[b], h_ * 16 + 16)
                    v.tensor_tensor(o[b][:, :, :], sign[:, :, :], x1[:, bass.ds(q * G5, G5), :], ALU.add).then_inc(s_o, 1)
                    v.wait_ge(s_o, q + 1)
                over_tiles(v, 0, body, NT // G5)

            @block.sync
            def _(sp):
                for q in s_st:
                    sp.sem_inc(q, 16)

                def body(q, b, h_):
                    sp.wait_ge(s_o, q + 1)
                    sp.dma_start(out_dram[bass.ds(q * (G5 * T), G5 * T), :].rearrange("(t p) c -> p t c", p=T), o[b][:, :, :]).then_inc(s_st[b], 16)
                over_tiles(sp, 0, body, NT // G5)
                for q in s_st:
                    sp.wait_ge(q, 16 + 16 * (NT // G5 // 2))


def gps_layer(nc, x, src, dst, edge_weight, wqkvT, bqkv, wprojT, bproj, temperature, gate_w, gate_b, w1, b1p, w2, b2, out):
    def scratch(n, s):
        return nc.dram_tensor(n, s, F32, kind="Internal").ap()
    mT = scratch("rotationT", (C, C)); xT = scratch("xT_tiles", (NT, P, 2 * T)); mom = scratch("moments", (H, VW, FEAT))
    buf = scratch("expert_rows", (E_N * ROOM, C)); y = scratch("expert_out", (E_N * ROOM, C))
    with ExitStack() as ctx:
        ctx.callback(nc.all_engine_barrier)
        wr = Writes(nc, ctx, src.shape[0])
        with ExitStack() as c:
            c.callback(nc.all_engine_barrier)
            write_segments(nc, c, wr, src, dst, edge_weight)
        norm_transposed(nc, x, xT, wr)
        moments(nc, xT, wqkvT, bqkv, mom, wr)
        rotation_matrix(nc, ctx, wr, mT, buf)
    with ExitStack() as c:
        def sb(n, s, t=F32):
            return c.enter_context(nc.sbuf_tensor(n, s, t))
        x1 = sb("x1", [T, NT, C]); slot_i = sb("slot_i", [T, NT], I32); coef = sb("coef", [T, NT])
        with nc.sbuf_tensor("xn2", [T, NT, C], F32) as xn2, nc.sbuf_tensor("logits", [T, NT, E_N], F32) as logits:
            attend(nc, xT, wqkvT, bqkv, temperature, wprojT, bproj, mom, mT, x, gate_w, gate_b, x1, xn2, logits)
            route(nc, logits, xn2, buf, slot_i, coef)
        experts(nc, buf, w1, b1p, w2, b2, y)
        combine(nc, y, slot_i, coef, x1, out)



def kernel(**inputs):
    import numpy as _np
    import concourse.bacc as _bacc
    from concourse import mybir as _mybir
    from concourse.bass_utils import run_bass_kernel_spmd as _run

    laid = {
        "x": inputs["x"], "src": inputs["src"], "dst": inputs["dst"], "edge_weight": inputs["edge_weight"],
        "wqkvT": inputs["L0_mix_Wqkv"].T, "bqkv": inputs["L0_mix_bqkv"],
        "wprojT": inputs["L0_mix_Wproj"].T, "bproj": inputs["L0_mix_bproj"],
        "temperature": inputs["L0_mix_temperature"].reshape(-1),
        "gate_w": inputs["L0_ffn_gate_w"], "gate_b": inputs["L0_ffn_gate_b"], "w1": inputs["L0_ffn_w1"],
        "b1p": inputs["L0_ffn_b1"].reshape(8, 8, 128).transpose(2, 0, 1),
        "w2": inputs["L0_ffn_w2"], "b2": inputs["L0_ffn_b2"],
    }
    nc = _bacc.Bacc("TRN2", target_bir_lowering=False, num_devices=1)
    arrays, args = {}, {}
    for name, value in laid.items():
        a = _np.ascontiguousarray(value)
        arrays[f"in_{name}"] = a
        args[name] = nc.dram_tensor(f"in_{name}", a.shape, _mybir.dt.from_np(a.dtype), kind="ExternalInput").ap()
    args["out"] = nc.dram_tensor("out_0_dram", (6250, 256), F32, kind="ExternalOutput").ap()
    gps_layer(nc, **args)
    r = _run(nc, [arrays], core_ids=[0])
    return r.results[0]["out_0_dram"]
```
